# Optimizing a Trainium2 kernel written in Bass

```python
import numpy as np
import jax
import jax.numpy as jnp

def _softmax(x, axis=-1):
    return jax.nn.softmax(x, axis=axis)

def _gelu(x):
    return jax.nn.gelu(x, approximate=True)

def _silu(x):
    return jax.nn.silu(x)

def _sigmoid(x):
    return jax.nn.sigmoid(x)

def _layernorm(x, axis=-1, eps=1e-05):
    m = jnp.mean(x, axis=axis, keepdims=True)
    v = jnp.var(x, axis=axis, keepdims=True)
    return (x - m) / jnp.sqrt(v + eps)

def _scatter_add(tgt, idx, src, axis=0):
    return tgt.at[idx].add(src)

def _segment_sum(src, seg, n):
    return jax.ops.segment_sum(src, seg, n)
kernel_name = 'mk_xattn_ffn_d1_seqx_r4_293de5'

def setup_inputs(seed: int=0):
    np.random.seed(seed)
    _w = jnp.asarray

    def _rec_inputs():
        import jax
        import jax.numpy as jnp
        _rk = jax.random.key(seed)
        x = 7.22e-05 + 1 * jax.random.normal(jax.random.fold_in(_rk, 1), (2, 512, 512), jnp.float32)
        _lenS = 512 - jax.random.randint(jax.random.fold_in(_rk, 7), (2,), 0, max(1, 512 // 4) + 1, jnp.int32)
        _lenS2 = 1024 - jax.random.randint(jax.random.fold_in(_rk, 8), (2,), 0, max(1, 1024 // 4) + 1, jnp.int32)
        _ctx_2048P = jax.random.normal(jax.random.fold_in(_rk, 11), (2, 16, 512), jnp.float32)
        _ctx_2048c = jax.random.dirichlet(jax.random.fold_in(_rk, 511), 0.3 * jnp.ones((16,), jnp.float32), (2, 1024))
        _ctx_2048t = jnp.einsum('bsk,bkd->bsd', _ctx_2048c, _ctx_2048P)
        _ctx_2048t = _ctx_2048t * jax.lax.rsqrt(jnp.mean(jnp.square(_ctx_2048t)) + 1e-12) * 0.953939
        ctx_2048 = -0.000514642 + 1.00011 * (_ctx_2048t + 0.3 * jax.random.normal(jax.random.fold_in(_rk, 611), (2, 1024, 512), jnp.float32))
        return (x, ctx_2048)
    x, ctx_2048 = _rec_inputs()

    def _L0_xattn_setup():
        import jax, jax.numpy as jnp
        import numpy as np
        D_MODEL = 512
        NUM_HEADS = 16
        HEAD_DIM = D_MODEL // NUM_HEADS

        def _fq_sym(x, axis):
            s = jnp.max(jnp.abs(x), axis=axis, keepdims=True) / 127.0
            s = jnp.maximum(s, 1e-08)
            q = jnp.clip(jnp.round(x / s), -127.0, 127.0) * s
            return x + jax.lax.stop_gradient(q - x)

        def _fq_unsigned(x, axis):
            s = jnp.max(x, axis=axis, keepdims=True) / 255.0
            s = jnp.maximum(s, 1e-08)
            q = jnp.clip(jnp.round(x / s), 0.0, 255.0) * s
            return x + jax.lax.stop_gradient(q - x)
        key = jax.random.key(seed)
        ks = jax.random.split(key, 8)
        B, N, M, C = (2, 512, 128, D_MODEL)
        return {'x': jax.random.normal(ks[0], (B, N, C), jnp.float32), 'cond': jax.random.normal(ks[1], (B, M, C), jnp.float32), 'Wq': jax.random.normal(ks[2], (C, C), jnp.float32) * 0.02, 'bq': jnp.zeros((C,), jnp.float32), 'Wkv': jax.random.normal(ks[3], (C, 2 * C), jnp.float32) * 0.02, 'bkv': jnp.zeros((2 * C,), jnp.float32), 'Wp': jax.random.normal(ks[4], (C, C), jnp.float32) * 0.02, 'bp': jnp.zeros((C,), jnp.float32)}
    _L0_xattn_all = _L0_xattn_setup()
    _L0_xattn_in = {k: v for k, v in _L0_xattn_all.items() if k in ('Wq', 'bq', 'Wkv', 'bkv', 'Wp', 'bp')}
    del _L0_xattn_all

    def _L0_ffn_setup():
        import jax, jax.numpy as jnp
        import numpy as np
        GOLDEN_CENTER = 1.0 / np.e
        GOLDEN_LOWER = 0.5 - np.log(4.0 / 3.0)
        GOLDEN_UPPER = 0.5

        def _golden_weights(x, Wr, temperature):
            inh = jax.nn.sigmoid(x @ Wr / temperature)
            in_zone = (inh >= GOLDEN_LOWER) & (inh <= GOLDEN_UPPER)
            distance = jnp.abs(inh - GOLDEN_CENTER)
            weights = jnp.exp(-distance / 0.1) * in_zone.astype(x.dtype)
            wsum = jnp.sum(weights, axis=-1, keepdims=True)
            no_expert = wsum < 1e-08
            fb = jnp.exp(-distance / 0.3)
            _, top2 = jax.lax.top_k(fb, 2)
            fb_mask = jnp.sum(jax.nn.one_hot(top2, weights.shape[-1], dtype=x.dtype), axis=-2)
            fb_w = fb * fb_mask
            fb_w = fb_w / jnp.maximum(jnp.sum(fb_w, axis=-1, keepdims=True), 1e-08)
            weights = jnp.where(no_expert, fb_w, weights)
            weights = weights / jnp.maximum(jnp.sum(weights, axis=-1, keepdims=True), 1e-08)
            return weights
        key = jax.random.key(seed)
        ks = jax.random.split(key, 5)
        B, T, D, E, F = (2, 512, 512, 8, 512)
        s_in = 1.0 / np.sqrt(D)
        s_f = 1.0 / np.sqrt(F)
        return {'x': jax.random.normal(ks[0], (B, T, D), dtype=jnp.float32), 'Wg': jax.random.normal(ks[1], (E, D, F), dtype=jnp.float32) * s_in, 'Wu': jax.random.normal(ks[2], (E, D, F), dtype=jnp.float32) * s_in, 'Wd': jax.random.normal(ks[3], (E, F, D), dtype=jnp.float32) * s_f, 'Wr': jax.random.normal(ks[4], (D, E), dtype=jnp.float32) * s_in, 'temperature': jnp.ones((1,), dtype=jnp.float32)}
    _L0_ffn_all = _L0_ffn_setup()
    _L0_ffn_in = {k: v for k, v in _L0_ffn_all.items() if k in ('Wg', 'Wu', 'Wd', 'Wr', 'temperature')}
    del _L0_ffn_all
    return {'x': x, 'ctx_2048': ctx_2048, 'L0_xattn_Wq': _L0_xattn_in['Wq'], 'L0_xattn_bq': _L0_xattn_in['bq'], 'L0_xattn_Wkv': _L0_xattn_in['Wkv'], 'L0_xattn_bkv': _L0_xattn_in['bkv'], 'L0_xattn_Wp': _L0_xattn_in['Wp'], 'L0_xattn_bp': _L0_xattn_in['bp'], 'L0_ffn_Wg': _L0_ffn_in['Wg'], 'L0_ffn_Wu': _L0_ffn_in['Wu'], 'L0_ffn_Wd': _L0_ffn_in['Wd'], 'L0_ffn_Wr': _L0_ffn_in['Wr'], 'L0_ffn_temperature': _L0_ffn_in['temperature']}

def reference(x, ctx_2048, L0_xattn_Wq, L0_xattn_bq, L0_xattn_Wkv, L0_xattn_bkv, L0_xattn_Wp, L0_xattn_bp, L0_ffn_Wg, L0_ffn_Wu, L0_ffn_Wd, L0_ffn_Wr, L0_ffn_temperature):
    import jax
    import jax.numpy as jnp

    def _L0_xattn_ref(x, cond, Wq, bq, Wkv, bkv, Wp, bp):
        import jax, jax.numpy as jnp
        import numpy as np
        D_MODEL = 512
        NUM_HEADS = 16
        HEAD_DIM = D_MODEL // NUM_HEADS

        def _fq_sym(x, axis):
            s = jnp.max(jnp.abs(x), axis=axis, keepdims=True) / 127.0
            s = jnp.maximum(s, 1e-08)
            q = jnp.clip(jnp.round(x / s), -127.0, 127.0) * s
            return x + jax.lax.stop_gradient(q - x)

        def _fq_unsigned(x, axis):
            s = jnp.max(x, axis=axis, keepdims=True) / 255.0
            s = jnp.maximum(s, 1e-08)
            q = jnp.clip(jnp.round(x / s), 0.0, 255.0) * s
            return x + jax.lax.stop_gradient(q - x)
        B, N, C = x.shape
        H, hd = (NUM_HEADS, HEAD_DIM)
        q = (x @ Wq + bq).reshape(1, B * N, H, hd)
        kv = (cond @ Wkv + bkv).reshape(1, -1, 2, H, hd)
        k, v = (kv[:, :, 0], kv[:, :, 1])
        scale = 1.0 / np.sqrt(hd).astype(np.float32)
        q = jnp.transpose(q * scale, (0, 2, 1, 3))
        k = jnp.transpose(k, (0, 2, 1, 3))
        v = jnp.transpose(v, (0, 2, 1, 3))
        q = _fq_sym(q, axis=-1)
        k = _fq_sym(k, axis=-1)
        v = _fq_sym(v, axis=2)
        attn = jnp.einsum('bhqd,bhkd->bhqk', q, k)
        attn = jax.nn.softmax(attn.astype(jnp.float32), axis=-1)
        attn = _fq_unsigned(attn, axis=-1)
        out = jnp.einsum('bhqk,bhkd->bhqd', attn, v)
        out = jnp.transpose(out, (0, 2, 1, 3)).reshape(B, N, C)
        return out @ Wp + bp

    def _L0_ffn_ref(x, Wg, Wu, Wd, Wr, temperature):
        import jax, jax.numpy as jnp
        import numpy as np
        GOLDEN_CENTER = 1.0 / np.e
        GOLDEN_LOWER = 0.5 - np.log(4.0 / 3.0)
        GOLDEN_UPPER = 0.5

        def _golden_weights(x, Wr, temperature):
            inh = jax.nn.sigmoid(x @ Wr / temperature)
            in_zone = (inh >= GOLDEN_LOWER) & (inh <= GOLDEN_UPPER)
            distance = jnp.abs(inh - GOLDEN_CENTER)
            weights = jnp.exp(-distance / 0.1) * in_zone.astype(x.dtype)
            wsum = jnp.sum(weights, axis=-1, keepdims=True)
            no_expert = wsum < 1e-08
            fb = jnp.exp(-distance / 0.3)
            _, top2 = jax.lax.top_k(fb, 2)
            fb_mask = jnp.sum(jax.nn.one_hot(top2, weights.shape[-1], dtype=x.dtype), axis=-2)
            fb_w = fb * fb_mask
            fb_w = fb_w / jnp.maximum(jnp.sum(fb_w, axis=-1, keepdims=True), 1e-08)
            weights = jnp.where(no_expert, fb_w, weights)
            weights = weights / jnp.maximum(jnp.sum(weights, axis=-1, keepdims=True), 1e-08)
            return weights
        weights = _golden_weights(x, Wr, temperature)
        gate = jnp.einsum('btd,edf->betf', x, Wg)
        up = jnp.einsum('btd,edf->betf', x, Wu)
        h = jax.nn.silu(gate) * up
        e_out = jnp.einsum('betf,efd->betd', h, Wd)
        out = jnp.einsum('bte,betd->btd', weights, e_out)
        return out
    x = x + _L0_xattn_ref(_layernorm(x, axis=-1), ctx_2048, L0_xattn_Wq, L0_xattn_bq, L0_xattn_Wkv, L0_xattn_bkv, L0_xattn_Wp, L0_xattn_bp)
    x = x + _L0_ffn_ref(_layernorm(x, axis=-1), L0_ffn_Wg, L0_ffn_Wu, L0_ffn_Wd, L0_ffn_Wr, L0_ffn_temperature)
    return x

_drawn_inputs = setup_inputs


def setup_inputs(seed=0):
    import zlib

    import numpy as np

    out = dict(_drawn_inputs(seed))
    spreads = {'L0_xattn_bq': (0.0, 0.46), 'L0_xattn_bkv': (0.0, 0.1), 'L0_xattn_bp': (0.0, 0.1)}
    factors = {}
    for name, (base, spread) in spreads.items():
        noise = np.random.default_rng([zlib.crc32(name.encode()), seed]).standard_normal(out[name].shape)
        drawn = base * np.exp(spread * noise) if base else spread * noise
        out[name] = jnp.asarray(drawn.astype(out[name].dtype))
    for name, factor in factors.items():
        out[name] = (out[name] * factor).astype(out[name].dtype)
    return out
```

```python
import concourse.bass as bass
from concourse import mybir
from contextlib import ExitStack
import numpy as np

F32, F16, BF16 = mybir.dt.float32, mybir.dt.float16, mybir.dt.bfloat16
I16, I32 = mybir.dt.int16, mybir.dt.int32
ALU = mybir.AluOpType
ACT = mybir.ActivationFunctionType
AX = mybir.AxisListType

P = 128
T, S, D = 1024, 2048, 512
H, HD = 16, 32
E, F = 8, 512
DK = D // P
QT, KT = T // P, S // P
SG = S // 512
WS = 64.0
PS = 2.0 ** 14
ROUND = 1.5 * 2.0 ** 23
LN255 = float(np.log(255.0))
PASSES = ((0, 0), (0, 1), (1, 0))
LN_EPS = 1e-5
RSQRT_GUESS = 0x5F3759DF
GOLDEN_CENTER = float(1.0 / np.e)
GOLDEN_LOWER = float(0.5 - np.log(4.0 / 3.0))
GOLDEN_UPPER = 0.5


class Steps:

    def __init__(self, engine, sem, base=0):
        self.engine, self.sem, self.base, self.n = engine, sem, base, 0

    def mark(self, instruction):
        self.n += 1
        instruction.then_inc(self.sem, 1)

    def link(self, instruction):
        self.mark(instruction)
        self.engine.wait_ge(self.sem, self.base + self.n)


def xattn_moe(nc, A_x, A_ctx, A_wq, A_bq, A_wkv, A_bkv, A_wp, A_bp, A_wg, A_wu, A_wd, A_wr, A_temp, out):
    x_t = A_x.rearrange("b (t p) d -> p (b t) d", p=P)
    ctx_g = A_ctx.rearrange("b (g s p) d -> (b g) p s d", p=P, s=DK)
    out_t = out.rearrange("b (t p) d -> p (b t) d", p=P)
    w_rows = [w.rearrange("e (c p) n -> e p c n", p=P) for w in (A_wg, A_wu, A_wd)]

    ctx = ExitStack()
    with ctx:
        def sb(name, shape, dt=F32):
            return ctx.enter_context(nc.sbuf_tensor(name, shape, dt))

        def sem(name):
            return ctx.enter_context(nc.semaphore(name))

        keys_region = sb("keys_region", [P, H * S // 2])
        query_region = sb("query_region", [P, DK * S])
        token_region = sb("token_region", [P, DK * T])
        work = sb("work", [P, 14400])
        resid = sb("resid", [P, QT, D])
        v_int = sb("v_int", [P, KT, D], BF16)

        def view(region, at, words, dt, pattern=None, **dims):
            v = region[:, at:at + words]
            if dt != F32:
                v = v.bitcast(dt)
            return v.rearrange(pattern, **dims) if pattern else v

        key_parts = view(keys_region, 0, H * S // 2, BF16, "p (h k) -> p h k", h=H)
        v_T = view(query_region, 0, DK * S, F32, "p (m k) -> p m k", m=DK)
        q_int = view(query_region, 0, H * T // 2, BF16, "p (h q) -> p h q", h=H)
        wkv_raw = view(token_region, 0, DK * 2 * D, F32, "p (c n) -> p c n", c=DK)
        v_T_int = view(token_region, 0, DK * S // 2, BF16, "p (m k) -> p m k", m=DK)
        tok_T = view(token_region, 0, DK * T, F16, "p (l c t) -> p l c t", l=2, c=DK)

        ctx_raw = view(work, 0, 2048, F32, "p (s d) -> p s d", s=DK)
        ctx_hl = view(work, 2048, 2048, F16, "p (l s d) -> p l s d", l=2, s=DK)
        ctx_T = view(work, 4096, 2048, F16, "p (l c k) -> p l c k", l=2, c=DK)
        wkv_hl = view(work, 6144, 4096, F16, "p (l c n) -> p l c n", l=2, c=DK)
        k_raw = [view(work, 10240 + 512 * s, 512, F32) for s in range(2)]
        k_work = view(work, 11264, 512, F32)
        k_rest = view(work, 11776, 512, F32)
        k_cut = [view(work, 12288 + 768 * s, 768, BF16, "p (h r d) -> p h r d", h=H, r=3) for s in range(2)]
        bk_all = view(work, 13824, 512, F32)
        wq_raw = view(work, 0, 2048, F32, "p (c n) -> p c n", c=DK)
        wp_raw = view(work, 2048, 2048, F32, "p (c n) -> p c n", c=DK)
        wq_hl = view(work, 4096, 2048, F16, "p (l c n) -> p l c n", l=2, c=DK)
        x_norm = view(work, 6144, 512, F32)
        x_hl = [view(work, 6656 + 512 * s, 512, F16, "p (l d) -> p l d", l=2) for s in range(2)]
        q_raw = view(work, 7680, 512, F32)
        q_cut = [view(work, 8192 + 768 * s, 768, BF16, "p (h r d) -> p h r d", h=H, r=3) for s in range(2)]
        x_T = [view(work, 9728 + 512 * s, 512, F16, "p (l c t) -> p l c t", l=2, c=DK) for s in range(2)]
        bq_all = view(work, 11264, 512, F32)
        p_int = [view(work, 1024 * s, 1024, I16) for s in range(2)]
        p_bf = [view(work, 2048 + 1024 * s, 1024, BF16) for s in range(2)]
        p_T = [view(work, 4096 + 1024 * s, 1024, BF16, "p (t q) -> p t q", t=KT) for s in range(4)]
        att = view(work, 8192, 512, F32)
        att_hl = view(work, 8704, 512, F16, "p (l d) -> p l d", l=2)
        att_T = view(work, 9216, 512, F16, "p (l c t) -> p l c t", l=2, c=DK)
        x_bias = view(work, 9728, 512, F32)
        x1 = view(work, 10240, 512, F32)
        x1_norm = view(work, 10752, 512, F32)
        x1_hl = view(work, 11264, 512, F16, "p (l d) -> p l d", l=2)
        wp_hl = view(work, 12288, 2048, F16, "p (l c n) -> p l c n", l=2, c=DK)
        w_raw = [view(keys_region, 2048 * m, 2048, F32, "p (c n) -> p c n", c=DK) for m in range(3)]
        w_hl = [[view(keys_region, 6144 + 2048 * (3 * e + m), 2048, F16, "p (l c n) -> p l c n", l=2, c=DK)
                 if 3 * e + m < 5 else
                 view(query_region, 0, 2048, F16, "p (l c n) -> p l c n", l=2, c=DK)
                 for m in range(3)] for e in range(2)]
        hid_T = [view(query_region, 2048 + 2048 * c, 2048, F16, "p (l f t) -> p l f t", l=2, f=DK) for c in range(2)]
        tanh_g = [view(work, 512 * s, 512, F32) for s in range(2)]
        gate_1 = [view(work, 1024 + 512 * s, 512, F32) for s in range(2)]
        hidden = [view(work, 2048 + 512 * s, 512, F32) for s in range(2)]

        ident_f = sb("ident_f", [P, P])
        ident_h = sb("ident_h", [P, P], F16)
        ident_b = sb("ident_b", [P, P], BF16)
        bp_all = sb("bp_all", [P, D])
        bv_col = sb("bv_col", [P, DK])
        wr_raw = sb("wr_raw", [P, DK, E])
        wr_hl = sb("wr_hl", [P, 2, DK, E], F16)
        temp = sb("temp", [P, 1])
        r_temp = sb("r_temp", [P, 1])
        k_amax, k_step, k_rstep = (sb(n, [P, H]) for n in ("k_amax", "k_step", "k_rstep"))
        v_amax, v_step, v_rstep, v_fold = (sb(n, [P, DK]) for n in ("v_amax", "v_step", "v_rstep", "v_fold"))
        ln_stats = sb("ln_stats", [P, QT, 6])
        ln_mv = sb("ln_mv", [P, QT, 2])
        ln_a, ln_b = (sb(n, [P, QT]) for n in ("ln_a", "ln_b"))
        ln_rstd = sb("ln_rstd", [P, QT])
        ln_mean = sb("ln_mean", [P, QT])
        q_amax, q_rstep = (sb(n, [P, H]) for n in ("q_amax", "q_rstep"))
        q_step = sb("q_step", [P, QT, H])
        q_step_now = sb("q_step_now", [P, H])
        s_max = sb("s_max", [P, 4])
        s_nmax = sb("s_nmax", [P, 1])
        exp_bias = sb("exp_bias", [P, 2])
        p_sum = sb("p_sum", [P, H, 2])
        p_rsum = sb("p_rsum", [P, H])
        logits = sb("logits", [P, QT, E])
        g_inh, g_dist, g_w, g_zone, g_fb, g_tmp, g_rank = (
            sb(n, [P, QT, E]) for n in ("g_inh", "g_dist", "g_w", "g_zone", "g_fb", "g_tmp", "g_rank"))
        g_gt, g_eq = (view(work, 4096 + 512 * n, 512, F32, "p (t a b) -> p t a b", t=QT, a=E) for n in range(2))
        lower_tri = sb("lower_tri", [P, E, E])
        g_sum, g_none, g_has = (sb(n, [P, QT]) for n in ("g_sum", "g_none", "g_has"))
        w_now = sb("w_now", [P, QT, 2])

        psum = ctx.enter_context(nc.psum_tensor("psum", [P, 8, 512], F32))

        def bank(b):
            return psum[:, b, :]

        def bank16(b, dt):
            return psum[:, b, :].bitcast(dt)

        ctx_in, small_in, x_in, wq_in, wp_in = (sem(n) for n in ("ctx_in", "small_in", "x_in", "wq_in", "wp_in"))
        wkv_in = [sem(f"wkv_in{n}") for n in range(2)]
        dve_step, act_step, pool_step = sem("dve_step"), sem("act_step"), sem("pool_step")
        ident_ready = sem("ident_ready")
        wkv_hi, wkv_ready, ctx_hi, ctx_cut = (sem(n) for n in ("wkv_hi", "wkv_ready", "ctx_hi", "ctx_cut"))
        ctxT_full = sem("ctxT_full")
        ctxT_out = [sem(f"ctxT_out{b}") for b in range(2)]
        k_full = sem("k_full")
        k_out = [sem(f"k_out{b}") for b in range(2)]
        k_used = [sem(f"k_used{b}") for b in range(2)]
        k_cut_ready = sem("k_cut_ready")
        kT_full = [sem(f"kT_full{b}") for b in range(2)]
        kT_out = [sem(f"kT_out{b}") for b in range(2)]
        v_full = sem("v_full")
        v_out = [sem(f"v_out{b}") for b in range(2)]
        v_rounded, vT_full, v_ready = sem("v_rounded"), sem("vT_full"), sem("v_ready")
        wq_hi, wq_ready, wp_scaled, wp_hi, wp_ready = (
            sem(n) for n in ("wq_hi", "wq_ready", "wp_scaled", "wp_hi", "wp_ready"))
        x_norm_ready, x_hi, x_cut, xT_full, tokT_ready = (
            sem(n) for n in ("x_norm_ready", "x_hi", "x_cut", "xT_full", "tokT_ready"))
        q_full, q_out, q_rounded, q_cut_ready = (sem(n) for n in ("q_full", "q_out", "q_rounded", "q_cut_ready"))
        qT_full, qT_out = sem("qT_full"), sem("qT_out")
        scores_full, bias_ready, exp_done = sem("scores_full"), sem("bias_ready"), sem("exp_done")
        probs_ready, pv_done = sem("probs_ready"), sem("pv_done")
        probsT_in = [sem(f"probsT_in{b}") for b in range(4)]
        att_ready, att_cut, misc_full, misc_out = (sem(n) for n in ("att_ready", "att_cut", "misc_full", "misc_out"))
        att_hi, x1_normed, x1_hi, x1_cut = sem("att_hi"), sem("x1_normed"), sem("x1_hi"), sem("x1_cut")
        neg_exp, dist_ready, dist_exp = sem("neg_exp"), sem("dist_ready"), sem("dist_exp")
        tri_ready = sem("tri_ready")
        w_in = [sem(f"w_in{m}") for m in range(3)]
        w_hi = [sem(f"w_hi{m}") for m in range(3)]
        w_ready = [sem(f"w_ready{m}") for m in range(3)]
        gate_full, up_full, tanh_ready = sem("gate_full"), sem("up_full"), sem("tanh_ready")
        hidden_ready = [sem(f"hidden_ready{b}") for b in range(2)]
        hid_hi, hid_cut, down_full = sem("hid_hi"), sem("hid_cut"), sem("down_full")
        down_out = [[sem(f"down_out{c}{b}") for b in range(2)] for c in range(2)]
        stored, sp_passed = sem("stored"), sem("sp_passed")

        block = ctx.enter_context(nc.Block())

        @block.sync
        def _(sp):
            def passed():
                sp.sem_inc(sp_passed, 1)

            sp.dma_start(ctx_raw, ctx_g[0]).then_inc(ctx_in, 16)
            wkv_v = A_wkv.rearrange("(c p) n -> p c n", p=P)
            for n in range(2):
                sp.dma_start(wkv_raw[:, :, n * D:(n + 1) * D], wkv_v[:, :, n * D:(n + 1) * D]).then_inc(wkv_in[n], 16)
            with nc.allow_non_contiguous_dma("small constants"):
                sp.dma_start(bk_all, A_bkv[0:D].partition_broadcast(P)).then_inc(small_in, 16)
                sp.dma_start(bv_col[:, :], A_bkv[D:2 * D].rearrange("(m p) -> p m", p=P)).then_inc(small_in, 16)
                sp.dma_start(bp_all[:, :], A_bp.partition_broadcast(P)).then_inc(small_in, 16)
                sp.dma_start(temp[:, :], A_temp.partition_broadcast(P)).then_inc(small_in, 16)
                sp.dma_start(wr_raw[:, :, :], A_wr.rearrange("(c p) e -> p c e", p=P)).then_inc(small_in, 16)
            sp.dma_start(resid[:, :, :], x_t).then_inc(x_in, 16)
            with sp.Fori(1, SG) as g:
                sp.wait_ge(ctx_cut, g)
                passed()
                sp.dma_start(ctx_raw, ctx_g[bass.ds(g, 1)].rearrange("a p s d -> (a p) s d")).then_inc(ctx_in, 16)
            sp.wait_ge(kT_full[1], 2 * 2 * SG)
            sp.wait_ge(k_cut_ready, SG * DK)
            sp.dma_start(wq_raw, A_wq.rearrange("(c p) n -> p c n", p=P)).then_inc(wq_in, 16)
            sp.dma_start(bq_all, A_bq.partition_broadcast(P)).then_inc(wq_in, 16)
            sp.dma_start(wp_raw, A_wp.rearrange("(c p) n -> p c n", p=P)).then_inc(wp_in, 16)

            def transpose_tile(i, first):
                for h in range(H):
                    u = H * i + h
                    sp.wait_ge(probs_ready, u + 1)
                    passed()
                    if not first or h >= 4:
                        sp.wait_ge(pv_done, u - 3)
                        passed()
                    sp.dma_start_transpose(p_T[h % 4], p_bf[h % 2]).then_inc(probsT_in[h % 4], 16)

            transpose_tile(0, True)
            with sp.Fori(1, QT) as i:
                transpose_tile(i, False)

            sp.wait_ge(scores_full, 4 * H * QT)
            for m in range(3):
                sp.dma_start(w_raw[m], w_rows[m][0]).then_inc(w_in[m], 16)
            with sp.Fori(1, E) as e:
                for m in range(3):
                    sp.wait_ge(w_ready[m], e)
                    passed()
                    sp.dma_start(w_raw[m], w_rows[m][bass.ds(e, 1)].rearrange("a p c n -> (a p) c n")
                                 ).then_inc(w_in[m], 16)
            for t in range(QT):
                c, b = t // 4, t % 2
                sp.wait_ge(down_out[c][b], 2 * (E - 1) + (t % 4) // 2 + 1)
                sp.dma_start(out_t[:, t, :], resid[:, t, :]).then_inc(stored, 16)
            sp.wait_ge(stored, 16 * QT)

        @block.gpsimd
        def _(pool):
            own = Steps(pool, pool_step)
            own.link(nc.gpsimd.memset(ident_f[:, :], 0.0))
            own.link(nc.gpsimd.affine_select(out=ident_f[:, :], in_=ident_f[:, :], compare_op=ALU.not_equal, fill=1.0,
                                             base=0, pattern=[[-1, P]], channel_multiplier=1))
            nc.gpsimd.tensor_copy(ident_h[:, :], ident_f[:, :]).then_inc(ident_ready, 1)
            nc.gpsimd.tensor_copy(ident_b[:, :], ident_f[:, :]).then_inc(ident_ready, 1)
            own.link(nc.gpsimd.memset(lower_tri[:, :, :], 1.0))
            nc.gpsimd.affine_select(out=lower_tri[:, :, :], in_=lower_tri[:, :, :], compare_op=ALU.is_gt, fill=0.0,
                                    base=0, pattern=[[1, E], [-1, E]], channel_multiplier=0).then_inc(tri_ready, 1)

            with pool.Fori(0, QT) as j:
                pool.wait_ge(att_hi, j + 1)
                nc.gpsimd.tensor_tensor(att_hl[:, 1, :], att, att_hl[:, 0, :], ALU.subtract).then_inc(att_cut, 1)
                pool.wait_ge(x1_hi, j + 1)
                nc.gpsimd.tensor_tensor(x1_hl[:, 1, :], x1_norm, x1_hl[:, 0, :], ALU.subtract).then_inc(x1_cut, 1)

        @block.scalar
        def _(act):
            for n in range(2):
                act.wait_ge(wkv_in[n], 16)
                part = slice(n * D, (n + 1) * D)
                nc.scalar.activation(wkv_hl[:, 0, :, part], wkv_raw[:, :, part], ACT.Copy, scale=WS).then_inc(wkv_hi, 1)
            act.wait_ge(small_in, 80)
            with act.Fori(0, SG) as g:
                act.wait_ge(ctx_in, 16 * g + 16)
                nc.scalar.activation(ctx_hl[:, 0], ctx_raw, ACT.Copy).then_inc(ctx_hi, 1)
                for c in (1, 3):
                    act.wait_ge(ctxT_full, 4 * g + c + 1)
                    nc.scalar.activation(ctx_T[:, :, c, :], bank16(1, F16).rearrange("p (l k) -> p l k", l=2),
                                         ACT.Copy).then_inc(ctxT_out[1], 1)
                for s in range(DK):
                    act.wait_ge(k_full, 4 * g + s + 1)
                    act.wait_ge(k_used[s % 2], 2 * g + s // 2)
                    nc.scalar.activation(k_raw[s % 2], bank(2 + s % 2), ACT.Copy, scale=1.0 / WS).then_inc(k_out[s % 2], 1)
                for s in range(DK):
                    act.wait_ge(v_full, 4 * g + s + 1)
                    nc.scalar.activation(v_T[:, s, bass.ds(g * 512, 512)], bank(4 + s % 2), ACT.Identity,
                                         bias=bv_col[:, s:s + 1], scale=1.0 / WS).then_inc(v_out[s % 2], 1)
                    for b in range(2):
                        act.wait_ge(kT_full[s % 2], 4 * g + 2 * (s // 2) + b + 1)
                        nc.scalar.activation(
                            key_parts[0:96, 8 * b:8 * b + 8, bass.ds(g * 512 + s * P, P)],
                            bank16(6 + b, BF16)[0:96, :].rearrange("p (h k) -> p h k", h=8),
                            ACT.Copy).then_inc(kT_out[b], 1)
            for j in range(1, 8, 2):
                act.wait_ge(vT_full, j + 1)
                nc.scalar.activation(v_int[:, 2 * j:2 * j + 2, :], bank16(j, BF16).rearrange("p (t d) -> p t d", t=2),
                                     ACT.Copy).then_inc(v_ready, 1)
            act.wait_ge(wq_in, 32)
            nc.scalar.activation(wq_hl[:, 0], wq_raw, ACT.Copy, scale=WS).then_inc(wq_hi, 1)
            with act.Fori(0, QT // 2) as i:
                for s in range(2):
                    act.wait_ge(x_norm_ready, 2 * i + s + 1)
                    act.wait_ge(xT_full, 2 * i + s)
                    nc.scalar.activation(x_hl[s][:, 0, :], x_norm, ACT.Copy).then_inc(x_hi, 1)
                    act.wait_ge(xT_full, 2 * i + s + 1)
                    nc.scalar.activation(tok_T[:, :, :, bass.ds(i * 2 * P + s * P, P)],
                                         bank16(s, F16).rearrange("p (l c t) -> p l c t", l=2, c=DK),
                                         ACT.Copy).then_inc(tokT_ready, 1)
            act.wait_ge(wp_scaled, 1)
            nc.scalar.activation(wp_hl[:, 0], wp_raw, ACT.Copy).then_inc(wp_hi, 1)
            with act.Fori(0, QT) as i:
                for b in range(2):
                    act.wait_ge(qT_full, 2 * i + b + 1)
                    nc.scalar.activation(q_int[0:96, 8 * b:8 * b + 8, bass.ds(i * P, P)],
                                         bank16(4 + b, BF16)[0:96, :].rearrange("p (h q) -> p h q", h=8),
                                         ACT.Copy).then_inc(qT_out, 1)

            def misc_copy(j, n, dst, src):
                act.wait_ge(misc_full, 4 * j + n + 1)
                nc.scalar.activation(dst, src, ACT.Copy).then_inc(misc_out, 1)

            def after_attention(j, h):
                if h == 4:
                    act.wait_ge(att_ready, j + 1)
                    nc.scalar.activation(att_hl[:, 0, :], att, ACT.Copy).then_inc(att_hi, 1)
                if h == 11:
                    act.wait_ge(x1_normed, j + 1)
                    nc.scalar.activation(x1_hl[:, 0, :], x1_norm, ACT.Copy).then_inc(x1_hi, 1)
                if h == 6:
                    misc_copy(j, 0, att_T, bank16(7, F16).rearrange("p (l c t) -> p l c t", l=2, c=DK))
                if h == 13:
                    misc_copy(j, 2, tok_T[:, :, :, bass.ds(j * P, P)],
                              bank16(7, F16).rearrange("p (l c t) -> p l c t", l=2, c=DK))
                if h == 15:
                    misc_copy(j, 3, logits[:, bass.ds(j, 1), :].rearrange("p a e -> p (a e)"), bank(7)[:, 0:E])

            def attention_tile(i, first):
                for h in range(H):
                    u = H * i + h
                    act.wait_ge(bias_ready, u + 1)
                    if not first or h >= 2:
                        act.wait_ge(probs_ready, u - 1)
                    for half in range(2):
                        slot = (2 * h + half) % 3
                        nc.scalar.activation(
                            p_int[h % 2][:, half * 1024:half * 1024 + 1024].rearrange("p (b k) -> p b k", b=2),
                            psum[:, 2 * slot:2 * slot + 2, :], ACT.Exp, bias=exp_bias[:, h % 2:h % 2 + 1],
                            scale=q_step_now[:, h:h + 1], accum_out=p_sum[:, h, half:half + 1]).then_inc(exp_done, 1)
                    if not first:
                        after_attention(i - 1, h)

            attention_tile(0, True)
            with act.Fori(1, QT) as i:
                attention_tile(i, False)
            for h in range(H):
                after_attention(QT - 1, h)

            flat = "p t e -> p (t e)"
            act.wait_ge(dist_ready, 1)
            nc.scalar.activation(g_inh[:, :, :], g_tmp[:, :, :], ACT.Exp, scale=-1.0).then_inc(neg_exp, 1)
            act.wait_ge(dist_ready, 2)
            nc.scalar.activation(g_w[:, :, :], g_dist[:, :, :], ACT.Exp, scale=-1.0 / 0.1).then_inc(dist_exp, 1)
            nc.scalar.activation(g_fb[:, :, :], g_dist[:, :, :], ACT.Exp, scale=-1.0 / 0.3).then_inc(dist_exp, 1)

            def cut_weights(e, par):
                for m in range(3):
                    act.wait_ge(w_in[m], 16 * e + 16)
                    nc.scalar.activation(w_hl[par][m][:, 0], w_raw[m], ACT.Copy, scale=WS).then_inc(w_hi[m], 1)

            def expert(e, par, following):
                def hidden_hi(k):
                    c, f = k // 4, k % 4
                    act.wait_ge(hidden_ready[k % 2], 4 * e + k // 2 + 1)
                    if f == 0:
                        act.wait_ge(down_out[c][1], 2 * e)
                    nc.scalar.activation(hid_T[c][:, 0, f, :], hidden[k % 2], ACT.Copy).then_inc(hid_hi, 1)

                for k in range(8):
                    act.wait_ge(gate_full, 8 * e + k + 1)
                    act.wait_ge(hidden_ready[k % 2], 4 * e + k // 2)
                    nc.scalar.activation(tanh_g[k % 2], bank(k % 2), ACT.Tanh, scale=0.5 / WS).then_inc(tanh_ready, 1)
                    if k:
                        hidden_hi(k - 1)
                hidden_hi(7)
                if following:
                    cut_weights(e + 1, 1 - par)

            cut_weights(0, 0)
            with act.Fori(0, E // 2 - 1) as i:
                expert(2 * i, 0, True)
                expert(2 * i + 1, 1, True)
            expert(E - 2, 0, True)
            expert(E - 1, 1, False)

        @block.vector
        def _(dve):
            own = Steps(dve, dve_step)
            for n in range(2):
                part = slice(n * D, (n + 1) * D)
                dve.wait_ge(wkv_hi, n + 1)
                nc.vector.scalar_tensor_tensor(wkv_hl[:, 1, :, part], wkv_raw[:, :, part], WS, wkv_hl[:, 0, :, part],
                                               ALU.mult, ALU.subtract).then_inc(wkv_ready, 1)
            dve.wait_ge(small_in, 80)
            own.link(nc.vector.tensor_scalar(wr_hl[:, 0], wr_raw[:, :, :], WS, None, ALU.mult))
            own.mark(nc.vector.scalar_tensor_tensor(wr_hl[:, 1], wr_raw[:, :, :], WS, wr_hl[:, 0], ALU.mult, ALU.subtract))
            own.mark(nc.vector.reciprocal(r_temp[:, :], temp[:, :]))

            def heads(v):
                return v.rearrange("p (h d) -> p h d", h=H)

            def each(v):
                return v.unsqueeze(2).to_broadcast([P, H, HD])

            key_steps = 9
            head = own.n
            with dve.Fori(0, SG) as g:
                dve.wait_ge(ctx_hi, g + 1)
                nc.vector.tensor_tensor(ctx_hl[:, 1], ctx_raw, ctx_hl[:, 0], ALU.subtract).then_inc(ctx_cut, 1)
                for c in (0, 2):
                    dve.wait_ge(ctxT_full, 4 * g + c + 1)
                    nc.vector.tensor_copy(ctx_T[:, :, c, :], bank16(0, F16).rearrange("p (l k) -> p l k", l=2)
                                          ).then_inc(ctxT_out[0], 1)
                own = Steps(dve, dve_step, head + key_steps * DK * g)
                for s in range(DK):
                    dve.wait_ge(k_out[s % 2], 2 * g + s // 2 + 1)
                    add = nc.vector.tensor_tensor(k_work, k_raw[s % 2], bk_all, ALU.add)
                    own.link(add)
                    own.link(nc.vector.tensor_reduce(k_amax[:, :], heads(k_work), AX.X, ALU.max,
                                                     apply_absolute_value=True))
                    own.link(nc.vector.tensor_scalar(k_step[:, :], k_amax[:, :], 1.0 / 127.0, 1e-8, ALU.mult, ALU.max))
                    own.link(nc.vector.reciprocal(k_rstep[:, :], k_step[:, :]))
                    own.link(nc.vector.tensor_tensor(heads(k_work), heads(k_work), each(k_rstep[:, :]), ALU.mult))
                    own.link(nc.vector.tensor_scalar(k_work, k_work, ROUND, ROUND, ALU.add, ALU.subtract))
                    own.link(nc.vector.tensor_tensor(heads(k_work), heads(k_work), each(k_step[:, :]), ALU.mult))
                    dve.wait_ge(kT_full[s % 2], 4 * g + 2 * (s // 2))
                    cut = k_cut[s % 2]
                    own.link(nc.vector.tensor_copy(cut[:, :, 0, :], heads(k_work)))
                    sub = nc.vector.tensor_tensor(heads(k_rest), heads(k_work), cut[:, :, 0, :], ALU.subtract)
                    sub.then_inc(k_used[s % 2], 1)
                    dve.wait_ge(k_used[s % 2], 2 * g + s // 2 + 1)
                    own.link(nc.vector.tensor_copy(cut[:, :, 1, :], heads(k_rest)))
                    nc.vector.tensor_tensor(cut[:, :, 2, :], heads(k_rest), cut[:, :, 1, :], ALU.subtract
                                            ).then_inc(k_cut_ready, 1)
                assert own.n == key_steps * DK
            own = Steps(dve, dve_step, head + key_steps * DK * SG)

            for b in range(2):
                dve.wait_ge(v_out[b], 2 * SG)
            own.link(nc.vector.tensor_reduce(v_amax[:, :], v_T, AX.X, ALU.max, apply_absolute_value=True))
            own.link(nc.vector.tensor_scalar(v_step[:, :], v_amax[:, :], 1.0 / 127.0, 1e-8, ALU.mult, ALU.max))
            own.mark(nc.vector.tensor_scalar(v_fold[:, :], v_step[:, :], PS, None, ALU.mult))
            own.link(nc.vector.reciprocal(v_rstep[:, :], v_step[:, :]))
            for m in range(DK):
                own.mark(nc.vector.tensor_scalar(v_T[:, m, :], v_T[:, m, :], v_rstep[:, m:m + 1], ROUND, ALU.mult, ALU.add))
            dve.wait_ge(dve_step, own.base + own.n)
            nc.vector.tensor_scalar(v_T_int, v_T, ROUND, None, ALU.subtract).then_inc(v_rounded, 1)
            dve.wait_ge(x_in, 16)
            for t in range(QT):
                own.mark(nc.vector.bn_stats(ln_stats[:, t, :], resid[:, t, :]))
            dve.wait_ge(dve_step, own.base + own.n)
            for t in range(QT):
                own.mark(nc.vector.bn_aggr(ln_mv[:, t, :], ln_stats[:, t, :]))
            dve.wait_ge(dve_step, own.base + own.n)

            def rsqrt_steps(own, n):
                var, half_y = ln_a[:, 0:n], ln_b[:, 0:n]
                y = ln_rstd[:, 0:n]
                own.mark(nc.vector.tensor_copy(ln_mean[:, 0:n], ln_mv[:, 0:n, 0]))
                own.link(nc.vector.tensor_scalar(var, ln_mv[:, 0:n, 1], LN_EPS, None, ALU.add))
                own.link(nc.vector.tensor_scalar(y.bitcast(I32), var.bitcast(I32), 1, None, ALU.logical_shift_right))
                own.link(nc.vector.tensor_scalar(y.bitcast(I32), y.bitcast(I32), -1.0, float(RSQRT_GUESS),
                                                 ALU.mult, ALU.add))
                for _ in range(3):
                    own.link(nc.vector.tensor_tensor(half_y, y, y, ALU.mult))
                    own.link(nc.vector.tensor_tensor(half_y, half_y, var, ALU.mult))
                    own.link(nc.vector.tensor_scalar(half_y, half_y, -0.5, 1.5, ALU.mult, ALU.add))
                    own.link(nc.vector.tensor_tensor(y, y, half_y, ALU.mult))

            rsqrt_steps(own, QT)
            for j in range(0, 8, 2):
                dve.wait_ge(vT_full, j + 1)
                nc.vector.tensor_copy(v_int[:, 2 * j:2 * j + 2, :], bank16(j, BF16).rearrange("p (t d) -> p t d", t=2)
                                      ).then_inc(v_ready, 1)

            dve.wait_ge(wq_hi, 1)
            nc.vector.scalar_tensor_tensor(wq_hl[:, 1], wq_raw, WS, wq_hl[:, 0], ALU.mult, ALU.subtract).then_inc(wq_ready, 1)
            q_scale = float(1.0 / np.sqrt(np.float32(HD)))
            own.link(nc.vector.tensor_scalar(bq_all, bq_all, q_scale, None, ALU.mult))
            dve.wait_ge(v_ready, 4 + 4)
            head = own.base + own.n
            with dve.Fori(0, QT // 2) as i:
                for s in range(2):
                    row = resid[:, bass.ds(2 * i + s, 1), :].rearrange("p a d -> p (a d)")
                    dve.wait_ge(x_cut, 2 * i + s)
                    nc.vector.tensor_scalar(x_norm, row, ln_mean[:, bass.ds(2 * i + s, 1)],
                                            ln_rstd[:, bass.ds(2 * i + s, 1)], ALU.subtract, ALU.mult).then_inc(x_norm_ready, 1)
                    dve.wait_ge(x_hi, 2 * i + s + 1)
                    nc.vector.tensor_tensor(x_hl[s][:, 1, :], x_norm, x_hl[s][:, 0, :], ALU.subtract).then_inc(x_cut, 1)
            dve.wait_ge(wp_in, 16)
            for c in range(DK):
                own.mark(nc.vector.tensor_scalar(wp_raw[:, c, :], wp_raw[:, c, :], v_fold[:, c:c + 1], None, ALU.mult))
            dve.wait_ge(dve_step, own.base + own.n)
            dve.sem_inc(wp_scaled, 1)
            dve.wait_ge(wp_hi, 1)
            nc.vector.tensor_tensor(wp_hl[:, 1], wp_raw, wp_hl[:, 0], ALU.subtract).then_inc(wp_ready, 1)
            head = own.base + own.n
            query_steps = 6
            with dve.Fori(0, QT // 2) as i:
                own = Steps(dve, dve_step, head + 2 * query_steps * i)
                for s in range(2):
                    step = q_step[:, bass.ds(2 * i + s, 1), :].rearrange("p a h -> p (a h)")
                    dve.wait_ge(q_full, 2 * i + s + 1)
                    link = nc.vector.scalar_tensor_tensor(q_raw, bank(2 + s), q_scale / WS, bq_all, ALU.mult, ALU.add)
                    own.link(link)
                    dve.sem_inc(q_out, 1)
                    own.link(nc.vector.tensor_reduce(q_amax[:, :], heads(q_raw), AX.X, ALU.max, apply_absolute_value=True))
                    own.link(nc.vector.tensor_scalar(q_amax[:, :], q_amax[:, :], 1.0 / 127.0, 1e-8, ALU.mult, ALU.max))
                    own.mark(nc.vector.tensor_copy(step, q_amax[:, :]))
                    own.link(nc.vector.reciprocal(q_rstep[:, :], q_amax[:, :]))
                    own.link(nc.vector.tensor_tensor(heads(q_raw), heads(q_raw), each(q_rstep[:, :]), ALU.mult))
                    dve.wait_ge(qT_full, 4 * i)
                    nc.vector.tensor_scalar(q_cut[s], heads(q_raw).unsqueeze(2).to_broadcast([P, H, 3, HD]), ROUND, ROUND,
                                            ALU.add, ALU.subtract).then_inc(q_cut_ready, 1)
                    dve.wait_ge(q_cut_ready, 2 * i + s + 1)
                assert own.n == 2 * query_steps
            base = head + query_steps * QT


            def convert(i, h, first):
                dve.wait_ge(exp_done, 2 * (H * i + h) + 2)
                if h >= 2:
                    dve.wait_ge(probsT_in[(h - 2) % 4], 64 * i + 16 * ((h - 2) // 4 + 1))
                elif not first:
                    dve.wait_ge(probsT_in[(h - 2) % 4], 64 * i)
                nc.vector.tensor_copy(p_bf[h % 2], p_int[h % 2]).then_inc(probs_ready, 1)

            def after_attention(j, h, own):
                if h == 3:
                    dve.wait_ge(pv_done, H * j + H)
                    nc.vector.tensor_tensor(heads(att), heads(bank(6)), each(p_rsum[:, :]), ALU.mult).then_inc(att_ready, 1)
                if h == 5:
                    own.mark(nc.vector.tensor_tensor(x_bias, resid[:, bass.ds(j, 1), :].rearrange("p a d -> p (a d)"),
                                                     bp_all[:, :], ALU.add))
                if h == 9:
                    dve.wait_ge(dve_step, own.base + own.n)
                    dve.wait_ge(misc_full, 4 * j + 2)
                    own.link(nc.vector.scalar_tensor_tensor(x1, bank(7), 1.0 / PS, x_bias, ALU.mult, ALU.add))
                    own.link(nc.vector.bn_stats(ln_stats[:, 0, :], x1))
                    dve.sem_inc(misc_out, 1)
                    nc.vector.tensor_copy(resid[:, bass.ds(j, 1), :].rearrange("p a d -> p (a d)"), x1)
                    own.link(nc.vector.bn_aggr(ln_mv[:, 0, :], ln_stats[:, 0, :]))
                    rsqrt_steps(own, 1)
                    nc.vector.tensor_scalar(x1_norm, x1, ln_mean[:, 0:1], ln_rstd[:, 0:1], ALU.subtract, ALU.mult
                                            ).then_inc(x1_normed, 1)

            def attention_tile(i, base, first):
                own = Steps(dve, dve_step, base)
                for h in range(H):
                    u = H * i + h
                    banks = [2 * ((2 * h + half) % 3) for half in range(2)]
                    dve.wait_ge(scores_full, 4 * u + 2)
                    nc.vector.tensor_reduce(s_max[:, 0:1], psum[:, banks[0]:banks[0] + 2, :], AX.XY, ALU.max)
                    for b in range(2):
                        dve.wait_ge(scores_full, 4 * u + 3 + b)
                        red = nc.vector.tensor_reduce(s_max[:, 1 + b:2 + b], bank(banks[1] + b), AX.X, ALU.max)
                    if h:
                        red.then_inc(dve_step, 1)
                        own.n += 1
                        convert(i, h - 1, first)
                    else:
                        own.link(red)
                        if not first:
                            dve.wait_ge(exp_done, 2 * u)
                            own.link(nc.vector.tensor_tensor(p_rsum[:, :], p_sum[:, :, 0], p_sum[:, :, 1], ALU.add))
                            own.mark(nc.vector.reciprocal(p_rsum[:, :], p_rsum[:, :]))
                        own.link(nc.vector.tensor_copy(q_step_now[:, :], q_step[:, bass.ds(i, 1), :].rearrange("p a h -> p (a h)")))
                    dve.wait_ge(dve_step, own.base + own.n)
                    if not first or h:
                        dve.wait_ge(bias_ready, u)
                    own.link(nc.vector.tensor_reduce(s_nmax[:, :], s_max[:, 0:3], AX.X, ALU.max, negate=True))
                    nc.vector.tensor_scalar(exp_bias[:, h % 2:h % 2 + 1], s_nmax[:, :], q_step_now[:, h:h + 1], LN255,
                                            ALU.mult, ALU.add).then_inc(bias_ready, 1)
                    if h == 0 and not first:
                        convert(i - 1, H - 1, False)
                    if not first:
                        after_attention(i - 1, h, own)
                return own.n

            base += attention_tile(0, base, True)
            per_tile = 2 * H + 3 + 20
            with dve.Fori(1, QT) as i:
                assert attention_tile(i, base + per_tile * (i - 1), False) == per_tile
            base += per_tile * (QT - 1)
            own = Steps(dve, dve_step, base)
            dve.wait_ge(exp_done, 2 * H * QT)
            own.link(nc.vector.tensor_tensor(p_rsum[:, :], p_sum[:, :, 0], p_sum[:, :, 1], ALU.add))
            own.link(nc.vector.reciprocal(p_rsum[:, :], p_rsum[:, :]))
            convert(QT - 1, H - 1, False)
            for h in range(H):
                after_attention(QT - 1, h, own)

            def tokens(v):
                return v.unsqueeze(2).to_broadcast([P, QT, E])

            dve.wait_ge(misc_out, 4 * QT)
            zs = nc.vector.tensor_scalar(g_tmp[:, :, :], logits[:, :, :], 1.0 / WS, r_temp[:, 0:1], ALU.mult, ALU.mult)
            zs.then_inc(dist_ready, 1)
            dve.wait_ge(neg_exp, 1)
            own.link(nc.vector.tensor_scalar(g_inh[:, :, :], g_inh[:, :, :], 1.0, None, ALU.add))
            own.link(nc.vector.reciprocal(g_inh[:, :, :], g_inh[:, :, :]))
            own.link(nc.vector.tensor_scalar(g_tmp[:, :, :], g_inh[:, :, :], GOLDEN_CENTER, None, ALU.subtract))
            own.link(nc.vector.tensor_scalar(g_dist[:, :, :], g_tmp[:, :, :], -1.0, None, ALU.mult))
            nc.vector.tensor_tensor(g_dist[:, :, :], g_dist[:, :, :], g_tmp[:, :, :], ALU.max).then_inc(dist_ready, 1)
            own.link(nc.vector.tensor_scalar(g_zone[:, :, :], g_inh[:, :, :], GOLDEN_UPPER, None, ALU.is_le))
            own.link(nc.vector.scalar_tensor_tensor(g_zone[:, :, :], g_inh[:, :, :], GOLDEN_LOWER, g_zone[:, :, :],
                                                    ALU.is_ge, ALU.mult))
            dve.wait_ge(dist_exp, 2)
            own.link(nc.vector.tensor_tensor(g_w[:, :, :], g_w[:, :, :], g_zone[:, :, :], ALU.mult))
            own.link(nc.vector.tensor_reduce(g_sum[:, :], g_w[:, :, :], AX.X, ALU.add))
            own.mark(nc.vector.tensor_scalar(g_none[:, :], g_sum[:, :], 1e-8, None, ALU.is_lt))
            own.mark(nc.vector.tensor_scalar(g_has[:, :], g_sum[:, :], 1e-8, None, ALU.is_ge))
            mine = g_fb[:, :, :].unsqueeze(3).to_broadcast([P, QT, E, E])
            others = g_fb[:, :, :].unsqueeze(2).to_broadcast([P, QT, E, E])
            own.mark(nc.vector.tensor_tensor(g_gt, others, mine, ALU.is_gt))
            own.mark(nc.vector.tensor_tensor(g_eq, others, mine, ALU.is_equal))
            dve.wait_ge(dve_step, own.base + own.n)
            dve.wait_ge(tri_ready, 1)
            own.link(nc.vector.tensor_tensor(g_eq, g_eq,
                                             lower_tri[:, :, :].unsqueeze(1).to_broadcast([P, QT, E, E]), ALU.mult))
            own.link(nc.vector.tensor_tensor(g_gt, g_gt, g_eq, ALU.add))
            own.link(nc.vector.tensor_reduce(g_rank[:, :, :], g_gt, AX.X, ALU.add))
            own.link(nc.vector.scalar_tensor_tensor(g_fb[:, :, :], g_rank[:, :, :], 2.0, g_fb[:, :, :], ALU.is_lt, ALU.mult))
            own.link(nc.vector.tensor_reduce(g_sum[:, :], g_fb[:, :, :], AX.X, ALU.add))
            own.link(nc.vector.tensor_scalar(g_sum[:, :], g_sum[:, :], 1e-8, None, ALU.max))
            own.link(nc.vector.reciprocal(g_sum[:, :], g_sum[:, :]))
            own.link(nc.vector.tensor_tensor(g_sum[:, :], g_sum[:, :], g_none[:, :], ALU.mult))
            own.mark(nc.vector.tensor_tensor(g_fb[:, :, :], g_fb[:, :, :], tokens(g_sum[:, :]), ALU.mult))
            own.mark(nc.vector.tensor_tensor(g_w[:, :, :], g_w[:, :, :], tokens(g_has[:, :]), ALU.mult))
            dve.wait_ge(dve_step, own.base + own.n)
            own.link(nc.vector.tensor_tensor(g_w[:, :, :], g_w[:, :, :], g_fb[:, :, :], ALU.add))
            own.link(nc.vector.tensor_reduce(g_sum[:, :], g_w[:, :, :], AX.X, ALU.add))
            own.link(nc.vector.tensor_scalar(g_sum[:, :], g_sum[:, :], 1e-8, None, ALU.max))
            own.link(nc.vector.reciprocal(g_sum[:, :], g_sum[:, :]))
            own.link(nc.vector.tensor_scalar(g_sum[:, :], g_sum[:, :], 1.0 / WS, None, ALU.mult))
            own.link(nc.vector.tensor_tensor(g_w[:, :, :], g_w[:, :, :], tokens(g_sum[:, :]), ALU.mult))

            def cut_weights(e, par, m):
                dve.wait_ge(w_hi[m], e + 1)
                nc.vector.scalar_tensor_tensor(w_hl[par][m][:, 1], w_raw[m], WS, w_hl[par][m][:, 0],
                                               ALU.mult, ALU.subtract).then_inc(w_ready[m], 1)

            def expert(e, par, base, following):
                own = Steps(dve, dve_step, base)

                def hidden_lo(k):
                    c, f = k // 4, k % 4
                    dve.wait_ge(hid_hi, 8 * e + k + 1)
                    nc.vector.tensor_tensor(hid_T[c][:, 1, f, :], hidden[k % 2], hid_T[c][:, 0, f, :], ALU.subtract
                                            ).then_inc(hid_cut, 1)

                for k in range(8):
                    if k == 0:
                        dve.wait_ge(down_out[1][1], 2 * e)
                    dve.wait_ge(tanh_ready, 8 * e + k + 1)
                    own.link(nc.vector.scalar_tensor_tensor(gate_1[k % 2], tanh_g[k % 2], 1.0, bank(k % 2), ALU.add, ALU.mult))
                    dve.wait_ge(up_full, 8 * e + k + 1)
                    dve.wait_ge(hid_cut, 8 * e + max(k - 1, 0))
                    nc.vector.scalar_tensor_tensor(hidden[k % 2], gate_1[k % 2], 0.5 / (WS * WS), bank(2 + k % 2), ALU.mult, ALU.mult
                                                   ).then_inc(hidden_ready[k % 2], 1)
                    if k == 0 and par == 0:
                        own.link(nc.vector.tensor_copy(w_now[:, :, :], g_w[:, :, bass.ds(e, 2)]))
                    if k:
                        hidden_lo(k - 1)
                hidden_lo(7)
                for t in range(QT):
                    if following and t in (0, 2, 4):
                        cut_weights(e + 1, 1 - par, t // 2)
                    c, b = t // 4, t % 2
                    dve.wait_ge(down_full, 8 * e + t + 1)
                    dve.wait_ge(down_out[c][b], 2 * e + (t % 4) // 2)
                    nc.vector.scalar_tensor_tensor(resid[:, t, :], bank(4 + 2 * c + b), w_now[:, t, par:par + 1],
                                                   resid[:, t, :], ALU.mult, ALU.add).then_inc(down_out[c][b], 1)
                return own.n

            for m in range(3):
                cut_weights(0, 0, m)
            base = own.base + own.n
            per_pair = 9 + 8
            with dve.Fori(0, E // 2 - 1) as i:
                n = expert(2 * i, 0, base + per_pair * i, True)
                n += expert(2 * i + 1, 1, base + per_pair * i + 9, True)
                assert n == per_pair
            base += per_pair * (E // 2 - 1)
            expert(E - 2, 0, base, True)
            expert(E - 1, 1, base + 9, False)

        @block.tensor
        def _(pe):
            def product(out, lhs, rhs, pieces=DK, passes=PASSES):
                n, last = 0, len(passes) * pieces - 1
                for c in range(pieces):
                    for a, b in passes:
                        ins = nc.tensor.matmul(out, lhs(a, c), rhs(b, c), start=n == 0, stop=n == last)
                        n += 1
                return ins

            pe.wait_ge(ident_ready, 2)
            with pe.Fori(0, SG) as g:
                pe.wait_ge(ctx_cut, g + 1)
                for c in range(DK):
                    pe.wait_ge(ctxT_out[c % 2], 2 * g + c // 2)
                    for part in range(2):
                        for s in range(DK):
                            ins = nc.tensor.transpose(bank16(c % 2, F16)[:, part * 512 + s * P:part * 512 + s * P + P],
                                                      ctx_hl[:, part, s, c * P:c * P + P], ident_h[:, :])
                    ins.then_inc(ctxT_full, 1)
                for b in range(2):
                    pe.wait_ge(ctxT_out[b], 2 * g + 2)
                    pe.wait_ge(wkv_ready, 2)
                for s in range(DK):
                    pe.wait_ge(k_out[s % 2], 2 * g + s // 2)
                    product(bank(2 + s % 2), lambda a, c: ctx_T[:, a, c, s * P:s * P + P],
                            lambda b, c: wkv_hl[:, b, c, 0:D]).then_inc(k_full, 1)
                for s in range(DK):
                    pe.wait_ge(v_out[s % 2], 2 * g + s // 2)
                    product(bank(4 + s % 2), lambda a, c: wkv_hl[:, a, c, D + s * P:D + s * P + P],
                            lambda b, c: ctx_T[:, b, c, :]).then_inc(v_full, 1)
                    pe.wait_ge(k_cut_ready, 4 * g + s + 1)
                    for b in range(2):
                        pe.wait_ge(kT_out[b], 4 * g + s)
                        for h in range(8):
                            ins = nc.tensor.transpose(bank16(6 + b, BF16)[0:96, h * P:h * P + P],
                                                      k_cut[s % 2][:, 8 * b + h].rearrange("p r d -> p (r d)"), ident_b[:, :])
                        ins.then_inc(kT_full[s % 2], 1)
            pe.wait_ge(v_rounded, 1)
            for b in range(2):
                pe.wait_ge(kT_out[b], 4 * SG)
            for j in range(8):
                for t in range(2):
                    for m in range(DK):
                        ins = nc.tensor.transpose(bank16(j, BF16)[:, t * 512 + m * P:t * 512 + m * P + P],
                                                  v_T_int[:, m, (2 * j + t) * P:(2 * j + t + 1) * P], ident_b[:, :])
                ins.then_inc(vT_full, 1)

            pe.wait_ge(v_ready, 8)
            with pe.Fori(0, QT // 2) as i:
                for s in range(2):
                    pe.wait_ge(x_cut, 2 * i + s + 1)
                    pe.wait_ge(tokT_ready, 2 * i)
                    for part in range(2):
                        for c in range(DK):
                            ins = nc.tensor.transpose(bank16(s, F16)[:, (part * DK + c) * P:(part * DK + c + 1) * P],
                                                      x_hl[s][:, part, c * P:c * P + P], ident_h[:, :])
                    ins.then_inc(xT_full, 1)
            pe.wait_ge(tokT_ready, QT)
            pe.wait_ge(wq_ready, 1)

            def queries(i, s):
                product(bank(2 + s), lambda a, c: tok_T[:, a, c, bass.ds(i * P, P)],
                        lambda b, c: wq_hl[:, b, c, :]).then_inc(q_full, 1)

            def transpose_queries(i, s):
                pe.wait_ge(q_cut_ready, i + 1)
                pe.wait_ge(qT_out, 2 * i)
                for b in range(2):
                    for h in range(8):
                        ins = nc.tensor.transpose(bank16(4 + b, BF16)[0:96, h * P:h * P + P],
                                                  q_cut[s][:, 8 * b + h].rearrange("p r d -> p (r d)"), ident_b[:, :])
                    ins.then_inc(qT_full, 1)

            queries(0, 0)
            queries(1, 1)
            with pe.Fori(0, QT // 2 - 1) as i:
                for s in range(2):
                    transpose_queries(2 * i + s, s)
                    pe.wait_ge(q_out, 2 * i + s + 1)
                    queries(2 * i + s + 2, s)
            for s in range(2):
                transpose_queries(QT - 2 + s, s)

            pe.wait_ge(qT_out, 2 * QT)
            pe.wait_ge(wp_ready, 1)

            def values(i, h):
                pe.wait_ge(probsT_in[h % 4], 64 * i + 16 * (h // 4 + 1))
                for t in range(KT):
                    ins = nc.tensor.matmul(bank(6)[:, h * HD:h * HD + HD], p_T[h % 4][:, t, :],
                                           v_int[:, t, h * HD:h * HD + HD], start=t == 0, stop=t == KT - 1)
                ins.then_inc(pv_done, 1)

            def transpose_rows(src):
                for part in range(2):
                    for c in range(DK):
                        ins = nc.tensor.transpose(bank16(7, F16)[:, (part * DK + c) * P:(part * DK + c + 1) * P],
                                                  src[:, part, c * P:c * P + P], ident_h[:, :])
                ins.then_inc(misc_full, 1)

            def after_attention(j, h):
                if h in (6, 8, 13, 15):
                    pe.wait_ge(misc_out, 4 * j + (6, 8, 13, 15).index(h))
                if h == 6:
                    pe.wait_ge(att_cut, j + 1)
                    transpose_rows(att_hl)
                if h == 8:
                    pe.wait_ge(misc_out, 4 * j + 1)
                    product(bank(7), lambda a, c: att_T[:, a, c, :], lambda b, c: wp_hl[:, b, c, :]).then_inc(misc_full, 1)
                if h == 13:
                    pe.wait_ge(x1_cut, j + 1)
                    transpose_rows(x1_hl)
                if h == 15:
                    pe.wait_ge(misc_out, 4 * j + 3)
                    product(bank(7)[:, 0:E], lambda a, c: tok_T[:, a, c, bass.ds(j * P, P)],
                            lambda b, c: wr_hl[:, b, c, :]).then_inc(misc_full, 1)

            last_of_slot = {0: 30, 1: 31, 2: 29}

            def attention_tile(i, first):
                for h in range(H):
                    u = H * i + h
                    for half in range(2):
                        n = 2 * h + half
                        slot = n % 3
                        if n >= 3:
                            pe.wait_ge(exp_done, 2 * H * i + n - 2)
                        elif not first:
                            pe.wait_ge(exp_done, 2 * H * (i - 1) + last_of_slot[slot] + 1)
                        for b in range(2):
                            at = (2 * half + b) * 512
                            nc.tensor.matmul(bank(2 * slot + b), q_int[0:96, h, bass.ds(i * P, P)],
                                             key_parts[0:96, h, at:at + 512], start=True, stop=True).then_inc(scores_full, 1)
                    if h >= 3:
                        if h == 3 and not first:
                            pe.wait_ge(att_ready, i)
                        values(i, h - 3)
                    elif not first:
                        values(i - 1, h - 3 + H)
                    if not first:
                        after_attention(i - 1, h)

            attention_tile(0, True)
            with pe.Fori(1, QT) as i:
                attention_tile(i, False)
            for h in range(H - 3, H):
                values(QT - 1, h)
            for h in range(H):
                after_attention(QT - 1, h)

            pe.wait_ge(misc_out, 4 * QT)

            def expert(e, par):
                gate, up, down = w_hl[par]
                for k in range(8):
                    c, f = k // 4, k % 4
                    toks = slice(c * 512, c * 512 + 512)
                    cols = slice(f * P, f * P + P)
                    pe.wait_ge(hidden_ready[k % 2], 4 * e + k // 2)
                    if k == 0:
                        pe.wait_ge(w_ready[0], e + 1)
                    product(bank(k % 2), lambda a, d: gate[:, a, d, cols], lambda b, d: tok_T[:, b, d, toks]).then_inc(gate_full, 1)
                    if k == 0:
                        pe.wait_ge(w_ready[1], e + 1)
                    product(bank(2 + k % 2), lambda a, d: up[:, a, d, cols], lambda b, d: tok_T[:, b, d, toks]).then_inc(up_full, 1)
                pe.wait_ge(w_ready[2], e + 1)
                for t in range(QT):
                    c, b2 = t // 4, t % 2
                    rows = slice((t % 4) * P, (t % 4) * P + P)
                    if t % 4 == 0:
                        pe.wait_ge(hid_cut, 8 * e + 4 * c + 4)
                    pe.wait_ge(down_out[c][b2], 2 * e + (t % 4) // 2)
                    product(bank(4 + 2 * c + b2), lambda a, d: hid_T[c][:, a, d, rows],
                            lambda b, d: down[:, b, d, :]).then_inc(down_full, 1)

            with pe.Fori(0, E // 2) as i:
                expert(2 * i, 0)
                expert(2 * i + 1, 1)


_INS = ['x', 'ctx_2048', 'L0_xattn_Wq', 'L0_xattn_bq', 'L0_xattn_Wkv', 'L0_xattn_bkv', 'L0_xattn_Wp', 'L0_xattn_bp',
        'L0_ffn_Wg', 'L0_ffn_Wu', 'L0_ffn_Wd', 'L0_ffn_Wr', 'L0_ffn_temperature']


def kernel(**inputs):
    import numpy as _np
    import concourse.bacc as _bacc
    from concourse import mybir as _mybir
    from concourse.bass_utils import run_bass_kernel_spmd as _run

    nc = _bacc.Bacc("TRN2", target_bir_lowering=False, num_devices=1)
    arrays, args = {}, []
    for name in _INS:
        a = _np.ascontiguousarray(inputs[name])
        arrays[f"in_{name}_dram"] = a
        args.append(nc.dram_tensor(f"in_{name}_dram", a.shape, _mybir.dt.from_np(a.dtype), kind="ExternalInput").ap())
    out = nc.dram_tensor("out_0_dram", (2, 512, 512), _mybir.dt.float32, kind="ExternalOutput").ap()
    xattn_moe(nc, *args, out)
    r = _run(nc, [arrays], core_ids=[0])
    return r.results[0]["out_0_dram"]
```

```python
import concourse.bass as bass
from concourse import mybir
from contextlib import ExitStack
import numpy as np

F32, F16, BF16 = mybir.dt.float32, mybir.dt.float16, mybir.dt.bfloat16
I16, I32 = mybir.dt.int16, mybir.dt.int32
ALU = mybir.AluOpType
ACT = mybir.ActivationFunctionType
AX = mybir.AxisListType

P = 128
T, S, D = 1024, 2048, 512
H, HD = 16, 32
HQ = 4
E, F = 8, 512
HALF = T // 2
DK = D // P
QT, KT = T // P, S // P
SG = S // 512
WS = 64.0
PS = 2.0 ** 14
ROUND = 1.5 * 2.0 ** 23
LN255 = float(np.log(255.0))
PASSES = ((0, 0), (0, 1), (1, 0))
LN_EPS = 1e-5
RSQRT_GUESS = 0x5F3759DF
GOLDEN_CENTER = float(1.0 / np.e)
GOLDEN_LOWER = float(0.5 - np.log(4.0 / 3.0))
GOLDEN_UPPER = 0.5


class Steps:

    def __init__(self, engine, sem, base=0, passed=None):
        self.engine, self.sem, self.base, self.n, self.passed = engine, sem, base, 0, passed

    def mark(self, instruction):
        self.n += 1
        instruction.then_inc(self.sem, 1)

    def link(self, instruction):
        self.mark(instruction)
        self.engine.wait_ge(self.sem, self.base + self.n)
        if self.passed:
            self.passed()


def before(k, n):
    return max(k - n, 0) if isinstance(k, int) else k - n


def xattn_moe(nc, A_x, A_ctx, A_wq, A_bq, A_wkv, A_bkv, A_wp, A_bp, A_wg, A_wu, A_wd, A_wr, A_temp, out):
    x_t = A_x.rearrange("b (t p) d -> p (b t) d", p=P)
    ctx_g = A_ctx.rearrange("b (g s p) d -> (b g) p s d", p=P, s=DK)
    out_rows = out.rearrange("b t d -> (b t) d")
    x1_rows = nc.dram_tensor("x1_rows", (T, 2 * D), F16, kind="Internal").ap()
    w_rows = [w.rearrange("e (c p) n -> e p c n", p=P) for w in (A_wg, A_wu, A_wd)]

    ctx = ExitStack()
    with ctx:
        def sb(name, shape, dt=F32):
            return ctx.enter_context(nc.sbuf_tensor(name, shape, dt))

        def sem(name):
            return ctx.enter_context(nc.semaphore(name))

        keys_region = sb("keys_region", [P, H * S // 2])
        query_region = sb("query_region", [P, DK * S])
        token_region = sb("token_region", [P, DK * T])
        work = sb("work", [P, 13824])
        resid = sb("resid", [P, QT, D])
        v_int = sb("v_int", [P, KT, D], F16)

        def view(region, at, words, dt, pattern=None, **dims):
            v = region[:, at:at + words]
            if dt != F32:
                v = v.bitcast(dt)
            return v.rearrange(pattern, **dims) if pattern else v

        key_parts = view(keys_region, 0, H * S // 2, F16, "p (h k) -> p h k", h=H)
        v_T = view(query_region, 0, DK * S, F32, "p (m k) -> p m k", m=DK)
        q_int = view(query_region, 0, H * T // 2, F16, "p (h q) -> p h q", h=H)
        wkv_raw = view(token_region, 0, DK * 2 * D, F32, "p (c n) -> p c n", c=DK)
        v_T_int = view(token_region, 0, DK * S // 2, F16, "p (m k) -> p m k", m=DK)
        tok_T = view(token_region, 0, DK * T, F16, "p (k t) -> p k t", k=2 * DK)

        ctx_raw = view(work, 0, 2048, F32, "p (s d) -> p s d", s=DK)
        ctx_hl = view(work, 2048, 2048, F16, "p (l s d) -> p l s d", l=2, s=DK)
        ctx_T = view(work, 4096, 2048, F16, "p (l c k) -> p l c k", l=2, c=DK)
        wkv_hl = view(work, 6144, 4096, F16, "p (l c n) -> p l c n", l=2, c=DK)
        k_raw = [view(work, 10240 + 512 * s, 512, F32) for s in range(2)]
        k_work = view(work, 11264, 512, F32)
        k_cut = [view(work, 11776 + 512 * s, 512, F16, "p (h r d) -> p h r d", h=H, r=2) for s in range(2)]
        bk_all = view(work, 12800, 512, F32)
        wq_raw = view(work, 0, 2048, F32, "p (c n) -> p c n", c=DK)
        wp_raw = view(work, 2048, 2048, F32, "p (c n) -> p c n", c=DK)
        wq_hl = view(work, 4096, 2048, F16, "p (l c n) -> p l c n", l=2, c=DK)
        x_norm = view(work, 6144, 512, F32)
        x_hl = [view(work, 6656 + 512 * s, 512, F16, "p (l d) -> p l d", l=2) for s in range(2)]
        q_raw = view(work, 7680, 512, F32)
        q_cut = [view(work, 8192 + 512 * s, 512, F16, "p (h r d) -> p h r d", h=H, r=2) for s in range(2)]
        x_T = [view(work, 9728 + 512 * s, 512, F16, "p (l c t) -> p l c t", l=2, c=DK) for s in range(2)]
        bq_all = view(work, 11264, 512, F32)
        p_int = [view(work, 1024 * s, 1024, I16) for s in range(2)]
        p_half = [view(work, 2048 + 1024 * s, 1024, F16) for s in range(2)]
        p_T = [view(work, 4096 + 1024 * s, 1024, F16, "p (t q) -> p t q", t=KT) for s in range(4)]
        att = view(work, 8192, 512, F32)
        att_hl = view(work, 8704, 512, F16, "p (l d) -> p l d", l=2)
        att_T = view(work, 9216, 512, F16, "p (k t) -> p k t", k=2 * DK)
        x_bias = view(work, 9728, 512, F32)
        x1 = view(work, 10240, 512, F32)
        x1_norm = view(work, 10752, 512, F32)
        x1_hl = view(work, 11264, 512, F16, "p (l d) -> p l d", l=2)
        wp_hl = view(work, 11776, 2048, F16, "p (l c n) -> p l c n", l=2, c=DK)
        g_gt, g_eq = (view(work, 12288 + 512 * n, 512, F32, "p (t a b) -> p t a b", t=QT, a=E) for n in range(2))
        tok_w = view(work, 13312, QT * E * 5 // 2, BF16, "p (t e c) -> p t e c", t=QT, e=E)
        slot = view(work, 13472, QT * E, F32, "p (t e) -> p t e", t=QT)
        mask = view(work, 13536, QT * E // 2, BF16, "p (t e) -> p t e", t=QT)
        w_raw = [view(keys_region, 2048 * m, 2048, F32, "p (c n) -> p c n", c=DK) for m in range(3)]
        w_hl = [[view(keys_region, 6144 + 2048 * (3 * e + m), 2048, F16, "p (l c n) -> p l c n", l=2, c=DK)
                 if 3 * e + m < 5 else
                 view(query_region, 0, 2048, F16, "p (l c n) -> p l c n", l=2, c=DK)
                 for m in range(3)] for e in range(2)]
        hid_T = [view(query_region, 2048 + 2048 * c, 2048, F16, "p (l f t) -> p l f t", l=2, f=DK) for c in range(2)]
        y_out = view(query_region, 6144, 2048, F32, "p (s d) -> p s d", s=DK)
        x_sel_T = [view(work, 2048 * c, 2048, F16, "p (s k t) -> p s k t", s=DK, k=2 * DK) for c in range(2)]
        x_sel = [view(work, 4096 + 2048 * c, 2048, F16, "p (s n) -> p s n", s=DK) for c in range(2)]
        select = view(work, 8192, 2048, BF16, "p (t s) -> p t s", t=QT)
        e_work = resid[:, :, :].rearrange("p t d -> p (t d)")
        tanh_g = [view(e_work, 512 * s, 512, F32) for s in range(2)]
        gate_1 = [view(e_work, 1024 + 512 * s, 512, F32) for s in range(2)]
        hidden = [view(e_work, 2048 + 512 * s, 512, F32) for s in range(2)]

        ident_f = sb("ident_f", [P, P])
        ident_h = sb("ident_h", [P, P], F16)
        bp_all = sb("bp_all", [P, D])
        bv_col = sb("bv_col", [P, DK])
        wr_raw = sb("wr_raw", [P, DK, E])
        wr_hl = sb("wr_hl", [P, 2, DK, E], F16)
        temp = sb("temp", [P, 1])
        r_temp = sb("r_temp", [P, 1])
        k_amax, k_step, k_rstep, k_step_w = (sb(n, [P, H]) for n in ("k_amax", "k_step", "k_rstep", "k_step_w"))
        v_amax, v_step, v_rstep, v_fold = (sb(n, [P, DK]) for n in ("v_amax", "v_step", "v_rstep", "v_fold"))
        ln_stats = sb("ln_stats", [P, QT, 6])
        ln_mv = sb("ln_mv", [P, QT, 2])
        ln_a, ln_b = (sb(n, [P, QT]) for n in ("ln_a", "ln_b"))
        ln_rstd = sb("ln_rstd", [P, QT])
        ln_mean = sb("ln_mean", [P, QT])
        q_amax, q_rstep = (sb(n, [P, H]) for n in ("q_amax", "q_rstep"))
        q_step = sb("q_step", [P, QT, 2, H])
        q_step_now = sb("q_step_now", [P, 2, H])
        ln255 = sb("ln255", [P, 1])
        s_part = sb("s_part", [P, 2, 3])
        s_max = sb("s_max", [P, 2])
        exp_bias = sb("exp_bias", [P, 2])
        p_part = sb("p_part", [P, H, 2])
        p_sum = sb("p_sum", [P, HQ])
        p_rsum = sb("p_rsum", [P, HQ])
        ln1_stats = sb("ln1_stats", [P, 6])
        ln1_mv = sb("ln1_mv", [P, 2])
        ln1_var, ln1_y, ln1_t = (sb(n, [P, 1]) for n in ("ln1_var", "ln1_y", "ln1_t"))
        g_inh, g_dist, g_w, g_zone, g_fb, g_tmp, g_rank = (
            sb(n, [P, QT, E]) for n in ("g_inh", "g_dist", "g_w", "g_zone", "g_fb", "g_tmp", "g_rank"))
        lower_tri = sb("lower_tri", [P, E, E])
        g_sum, g_none, g_has = (sb(n, [P, QT]) for n in ("g_sum", "g_none", "g_has"))
        g_count = sb("g_count", [P, E])
        n_max = sb("n_max", [P, 1], I32)
        ones = sb("ones", [P, P], BF16)
        earlier = sb("earlier", [P, P], BF16)
        slot_row = sb("slot_row", [P, HALF], F16)
        token = sb("token", [P, 3, QT], I32)
        slot_now = sb("slot_now", [P, QT])
        slot_tok_f = sb("slot_tok_f", [P, DK])
        slot_tok = [sb(f"slot_tok{c}", [P, DK], I32) for c in range(2)]
        slot_w = [sb(f"slot_w{c}", [P, DK]) for c in range(2)]

        psum = ctx.enter_context(nc.psum_tensor("psum", [P, 8, 512], F32))

        def bank(b):
            return psum[:, b, :]

        def bank16(b, dt):
            return psum[:, b, :].bitcast(dt)

        ctx_in, small_in, x_in, wq_in, wp_in = (sem(n) for n in ("ctx_in", "small_in", "x_in", "wq_in", "wp_in"))
        wkv_in = [sem(f"wkv_in{n}") for n in range(2)]
        dve_step, act_step, pool_step = sem("dve_step"), sem("act_step"), sem("pool_step")
        ident_ready = sem("ident_ready")
        wkv_hi, wkv_ready, ctx_hi, ctx_cut = (sem(n) for n in ("wkv_hi", "wkv_ready", "ctx_hi", "ctx_cut"))
        ctxT_full = sem("ctxT_full")
        ctxT_out = [sem(f"ctxT_out{b}") for b in range(2)]
        k_full = sem("k_full")
        k_out = [sem(f"k_out{b}") for b in range(2)]
        k_used = [sem(f"k_used{b}") for b in range(2)]
        k_cut_ready = sem("k_cut_ready")
        kT_full = [sem(f"kT_full{b}") for b in range(2)]
        kT_out = [sem(f"kT_out{b}") for b in range(2)]
        v_full = sem("v_full")
        v_out = [sem(f"v_out{b}") for b in range(2)]
        v_rounded, vT_full, v_ready = sem("v_rounded"), sem("vT_full"), sem("v_ready")
        wq_hi, wq_ready, wp_scaled, wp_hi, wp_ready = (
            sem(n) for n in ("wq_hi", "wq_ready", "wp_scaled", "wp_hi", "wp_ready"))
        x_norm_ready, x_hi, x_cut, xT_full, tokT_ready = (
            sem(n) for n in ("x_norm_ready", "x_hi", "x_cut", "xT_full", "tokT_ready"))
        q_full, q_out, q_rounded, q_cut_ready = (sem(n) for n in ("q_full", "q_out", "q_rounded", "q_cut_ready"))
        qT_full, qT_out = sem("qT_full"), sem("qT_out")
        scores_full, max_ready, exp_done = sem("scores_full"), sem("max_ready"), sem("exp_done")
        probs_ready, pv_done = sem("probs_ready"), sem("pv_done")
        probsT_in = [sem(f"probsT_in{b}") for b in range(4)]
        att_ready, att_cut, attT_in = (sem(n) for n in ("att_ready", "att_cut", "attT_in"))
        proj_full, proj_out, x1T_in = (sem(n) for n in ("proj_full", "proj_out", "x1T_in"))
        att_hi, x1_normed, x1_hi, x1_cut = sem("att_hi"), sem("x1_normed"), sem("x1_hi"), sem("x1_cut")
        x_bias_ready, x1_stats, pool_passed = sem("x_bias_ready"), sem("x1_stats"), sem("pool_passed")
        pe_passed, x1_summed = sem("pe_passed"), sem("x1_summed")
        logits_full = sem("logits_full")
        neg_exp, dist_ready, dist_exp = sem("neg_exp"), sem("dist_ready"), sem("dist_exp")
        tri_ready = sem("tri_ready")
        mask_ready, count_full, n_ready = sem("mask_ready"), sem("count_full"), sem("n_ready")
        w_in = [sem(f"w_in{m}") for m in range(3)]
        w_hi = [sem(f"w_hi{m}") for m in range(3)]
        w_ready = [sem(f"w_ready{m}") for m in range(3)]
        select_ready, list_full, slots_ready = sem("select_ready"), sem("list_full"), sem("slots_ready")
        gathered = [[sem(f"gathered{c}{t}") for t in range(DK)] for c in range(2)]
        selT_in = [sem(f"selT_in{c}") for c in range(2)]
        gate_full, up_full, tanh_ready = sem("gate_full"), sem("up_full"), sem("tanh_ready")
        hidden_ready = [sem(f"hidden_ready{b}") for b in range(2)]
        hid_hi, hid_cut, down_full = sem("hid_hi"), sem("hid_cut"), sem("down_full")
        y_ready = [sem(f"y_ready{b}") for b in range(2)]
        y_added = [sem(f"y_added{t}") for t in range(DK)]
        rows_stored = sem("rows_stored")
        stored, sp_passed = sem("stored"), sem("sp_passed")

        block = ctx.enter_context(nc.Block())

        @block.sync
        def _(sp):
            def passed():
                sp.sem_inc(sp_passed, 1)

            sp.dma_start(ctx_raw, ctx_g[0]).then_inc(ctx_in, 16)
            wkv_v = A_wkv.rearrange("(c p) n -> p c n", p=P)
            for n in range(2):
                sp.dma_start(wkv_raw[:, :, n * D:(n + 1) * D], wkv_v[:, :, n * D:(n + 1) * D]).then_inc(wkv_in[n], 16)
            with nc.allow_non_contiguous_dma("small constants"):
                sp.dma_start(bk_all, A_bkv[0:D].partition_broadcast(P)).then_inc(small_in, 16)
                sp.dma_start(bv_col[:, :], A_bkv[D:2 * D].rearrange("(m p) -> p m", p=P)).then_inc(small_in, 16)
                sp.dma_start(bp_all[:, :], A_bp.partition_broadcast(P)).then_inc(small_in, 16)
                sp.dma_start(temp[:, :], A_temp.partition_broadcast(P)).then_inc(small_in, 16)
                sp.dma_start(wr_raw[:, :, :], A_wr.rearrange("(c p) e -> p c e", p=P)).then_inc(small_in, 16)
            sp.dma_start(resid[:, :, :], x_t).then_inc(x_in, 16)
            with sp.Fori(1, SG) as g:
                sp.wait_ge(ctx_cut, g)
                passed()
                sp.dma_start(ctx_raw, ctx_g[bass.ds(g, 1)].rearrange("a p s d -> (a p) s d")).then_inc(ctx_in, 16)
            sp.wait_ge(kT_full[1], 2 * 2 * SG)
            sp.wait_ge(k_cut_ready, SG * DK)
            sp.dma_start(wq_raw, A_wq.rearrange("(c p) n -> p c n", p=P)).then_inc(wq_in, 16)
            sp.dma_start(bq_all, A_bq.partition_broadcast(P)).then_inc(wq_in, 16)
            sp.dma_start(wp_raw, A_wp.rearrange("(c p) n -> p c n", p=P)).then_inc(wp_in, 16)

            def transpose_attention(j):
                sp.wait_ge(att_cut, j + 1)
                passed()
                sp.dma_start_transpose(att_T, att_hl.rearrange("p l d -> p (l d)")).then_inc(attT_in, 16)

            def store_rows(j):
                sp.wait_ge(x1_cut, j + 1)
                passed()
                rows = x1_hl.rearrange("p l d -> p (l d)")
                sp.dma_start_transpose(tok_T[:, :, bass.ds(j * P, P)], rows).then_inc(x1T_in, 16)
                sp.dma_start(x1_rows[bass.ds(j * P, P), :], rows).then_inc(rows_stored, 16)
                sp.dma_start(out_rows[bass.ds(j * P, P), :], x1).then_inc(stored, 16)

            def transpose_tile(i, first, after_rows):
                for h in range(H):
                    u = H * i + h
                    sp.wait_ge(probs_ready, u + 1)
                    passed()
                    if not first or h >= 4:
                        sp.wait_ge(pv_done, u - 3)
                        passed()
                    sp.dma_start_transpose(p_T[h % 4], p_half[h % 2]).then_inc(probsT_in[h % 4], 16)
                    if h == 2 and after_rows:
                        store_rows(i - 2)
                    if h == 3 and not first:
                        transpose_attention(i - 1)

            transpose_tile(0, True, False)
            transpose_tile(1, False, False)
            with sp.Fori(2, QT) as i:
                transpose_tile(i, False, True)
            store_rows(QT - 2)
            transpose_attention(QT - 1)
            store_rows(QT - 1)

            def load_weights(k, e):
                for m in range(3):
                    sp.wait_ge(w_ready[m], k)
                    passed()
                    src = w_rows[m][bass.ds(e, 1)].rearrange("a p c n -> (a p) c n")
                    sp.dma_start(w_raw[m], src).then_inc(w_in[m], 16)

            def transpose_selected(i, par):
                for t in range(DK):
                    sp.wait_ge(gathered[par][t], 16 * i + 16)
                    if t == 0:
                        sp.wait_ge(up_full, DK * before(2 * i + par, 1))
                    passed()
                    sp.dma_start_transpose(x_sel_T[par][:, t], x_sel[par][:, t, :]).then_inc(selT_in[par], 16)

            def experts(k0):
                i0 = k0 // 2
                load_weights(k0, 0)
                transpose_selected(i0, 0)
                load_weights(k0 + 1, 1)
                with sp.Fori(0, E // 2 - 1) as i:
                    transpose_selected(i + i0, 1)
                    load_weights(2 * i + 2 + k0, 2 * i + 2)
                    transpose_selected(i + 1 + i0, 0)
                    load_weights(2 * i + 3 + k0, 2 * i + 3)
                transpose_selected(E // 2 - 1 + i0, 1)

            sp.wait_ge(scores_full, 3 * H * QT)
            experts(0)
            sp.wait_ge(n_ready, 1)
            with sp.If(sp.value_load(n_max[0:1, 0:1], min_val=0, max_val=T) > HALF):
                experts(E)
            sp.wait_ge(rows_stored, 16 * QT)
            sp.wait_ge(stored, 16 * QT)

        @block.gpsimd
        def _(pool):
            def passed():
                pool.sem_inc(pool_passed, 1)

            own = Steps(pool, pool_step)
            norm_steps = 14
            nc.gpsimd.memset(ln255[:, :], LN255).then_inc(ident_ready, 1)
            own.link(nc.gpsimd.memset(ident_f[:, :], 0.0))
            own.link(nc.gpsimd.affine_select(out=ident_f[:, :], in_=ident_f[:, :], compare_op=ALU.not_equal, fill=1.0,
                                             base=0, pattern=[[-1, P]], channel_multiplier=1))
            own.link(nc.gpsimd.tensor_copy(ident_h[:, :], ident_f[:, :]))
            pool.sem_inc(ident_ready, 1)
            for n in range(HALF // P):
                own.link(nc.gpsimd.iota(ident_f[:, :].bitcast(I32), pattern=[[1, P]], base=n * P, channel_multiplier=0))
                own.link(nc.gpsimd.tensor_copy(slot_row[:, n * P:n * P + P], ident_f[:, :].bitcast(I32)))
            nc.gpsimd.iota(token[:, 0, :], pattern=[[P, QT]], base=0, channel_multiplier=1).then_inc(tri_ready, 1)
            nc.gpsimd.iota(token[:, 1, :], pattern=[[P, QT]], base=0, channel_multiplier=0).then_inc(tri_ready, 1)
            nc.gpsimd.iota(token[:, 2, :], pattern=[[0, QT]], base=0, channel_multiplier=1).then_inc(tri_ready, 1)
            own.link(nc.gpsimd.memset(ident_f[:, :], 1.0))
            own.link(nc.gpsimd.tensor_copy(ones[:, :], ident_f[:, :]))
            own.link(nc.gpsimd.affine_select(out=ident_f[:, :], in_=ident_f[:, :], compare_op=ALU.is_gt, fill=0.0,
                                             base=0, pattern=[[1, P]], channel_multiplier=-1))
            nc.gpsimd.tensor_copy(earlier[:, :], ident_f[:, :]).then_inc(tri_ready, 1)
            own.link(nc.gpsimd.memset(lower_tri[:, :, :], 1.0))
            nc.gpsimd.affine_select(out=lower_tri[:, :, :], in_=lower_tri[:, :, :], compare_op=ALU.is_gt, fill=0.0,
                                    base=0, pattern=[[1, E], [-1, E]], channel_multiplier=0).then_inc(tri_ready, 1)

            head = own.n
            pool.wait_ge(small_in, 80)
            pool.wait_ge(x_norm_ready, QT)

            def add_bias(j):
                nc.gpsimd.tensor_tensor(x_bias, row(j), bp_all[:, :], ALU.add).then_inc(x_bias_ready, 1)

            def row(j):
                return resid[:, bass.ds(j, 1), :].rearrange("p a d -> p (a d)")

            def attention_lo(j):
                pool.wait_ge(att_hi, j + 1)
                nc.gpsimd.tensor_tensor(att_hl[:, 1, :], att, att_hl[:, 0, :], ALU.subtract).then_inc(att_cut, 1)

            def normalise(j):
                pool.wait_ge(x1_stats, j + 1)
                passed()
                own = Steps(pool, pool_step, head + norm_steps * j, passed)
                var, y, t = ln1_var[:, :], ln1_y[:, :], ln1_t[:, :]
                own.link(nc.gpsimd.tensor_scalar(var, ln1_mv[:, 1:2], LN_EPS, None, ALU.add))
                own.link(nc.gpsimd.tensor_scalar(y.bitcast(I32), var.bitcast(I32), -0.5, float(RSQRT_GUESS), ALU.mult, ALU.add))
                for _ in range(3):
                    own.link(nc.gpsimd.tensor_tensor(t, y, y, ALU.mult))
                    own.link(nc.gpsimd.tensor_tensor(t, t, var, ALU.mult))
                    own.link(nc.gpsimd.tensor_scalar(t, t, -0.5, 1.5, ALU.mult, ALU.add))
                    own.link(nc.gpsimd.tensor_tensor(y, y, t, ALU.mult))
                nc.gpsimd.tensor_scalar(x1_norm, x1, ln1_mv[:, 0:1], y, ALU.subtract, ALU.mult).then_inc(x1_normed, 1)
                assert own.n == norm_steps
                pool.wait_ge(x1_hi, j + 1)
                nc.gpsimd.tensor_tensor(x1_hl[:, 1, :], x1_norm, x1_hl[:, 0, :], ALU.subtract).then_inc(x1_cut, 1)

            with pool.Fori(0, QT) as j:
                add_bias(j)
                attention_lo(j)
                normalise(j)

            def gather(i, par):
                k = 2 * i + par
                pool.wait_ge(slots_ready, k + 1)
                pool.wait_ge(selT_in[par], 64 * i)
                passed()
                for t in range(DK):
                    nc.gpsimd.indirect_dma_start(
                        x_sel[par][:, t, :], None, x1_rows, bass.IndirectOffsetOnAxis(ap=slot_tok[par][:, t:t + 1], axis=0)
                    ).then_inc(gathered[par][t], 16)

            def scatter(i, par):
                k = 2 * i + par
                for t in range(DK):
                    pool.wait_ge(y_ready[t % 2], 2 * k + t // 2 + 1)
                    pool.wait_ge(y_added[(t - 1) % DK], 16 * k if t == 0 else 16 * k + 16)
                    passed()
                    nc.gpsimd.indirect_dma_start(
                        out_rows, bass.IndirectOffsetOnAxis(ap=slot_tok[par][:, t:t + 1], axis=0), y_out[:, t, :], None,
                        compute_op=ALU.add).then_inc(y_added[t], 16)

            def experts(k0):
                i0 = k0 // 2
                gather(i0, 0)
                with pool.Fori(0, E // 2 - 1) as i:
                    gather(i + i0, 1)
                    scatter(i + i0, 0)
                    gather(i + 1 + i0, 0)
                    scatter(i + i0, 1)
                last = E // 2 - 1 + i0
                gather(last, 1)
                scatter(last, 0)
                scatter(last, 1)
                for t in range(DK):
                    pool.wait_ge(y_added[t], 16 * (k0 + E))

            pool.wait_ge(rows_stored, 16 * QT)
            pool.wait_ge(stored, 16 * QT)
            experts(0)
            pool.wait_ge(n_ready, 1)
            with pool.If(pool.value_load(n_max[0:1, 0:1], min_val=0, max_val=T) > HALF):
                experts(E)

        @block.scalar
        def _(act):
            for n in range(2):
                act.wait_ge(wkv_in[n], 16)
                part = slice(n * D, (n + 1) * D)
                nc.scalar.activation(wkv_hl[:, 0, :, part], wkv_raw[:, :, part], ACT.Copy, scale=WS).then_inc(wkv_hi, 1)
            act.wait_ge(small_in, 80)
            act.wait_ge(ident_ready, 2)
            with act.Fori(0, SG) as g:
                act.wait_ge(ctx_in, 16 * g + 16)
                nc.scalar.activation(ctx_hl[:, 0], ctx_raw, ACT.Copy).then_inc(ctx_hi, 1)
                for c in (1, 3):
                    act.wait_ge(ctxT_full, 4 * g + c + 1)
                    nc.scalar.activation(ctx_T[:, :, c, :], bank16(1, F16).rearrange("p (l k) -> p l k", l=2),
                                         ACT.Copy).then_inc(ctxT_out[1], 1)
                for s in range(DK):
                    act.wait_ge(k_full, 4 * g + s + 1)
                    act.wait_ge(k_used[s % 2], 2 * g + s // 2)
                    nc.scalar.activation(k_raw[s % 2], bank(2 + s % 2), ACT.Copy, scale=1.0 / WS).then_inc(k_out[s % 2], 1)
                for s in range(DK):
                    act.wait_ge(v_full, 4 * g + s + 1)
                    nc.scalar.activation(v_T[:, s, bass.ds(g * 512, 512)], bank(4 + s % 2), ACT.Identity,
                                         bias=bv_col[:, s:s + 1], scale=1.0 / WS).then_inc(v_out[s % 2], 1)
                    for b in range(2):
                        act.wait_ge(kT_full[s % 2], 4 * g + 2 * (s // 2) + b + 1)
                        nc.scalar.activation(
                            key_parts[0:64, 8 * b:8 * b + 8, bass.ds(g * 512 + s * P, P)],
                            bank16(6 + b, F16)[0:64, :].rearrange("p (h k) -> p h k", h=8),
                            ACT.Copy).then_inc(kT_out[b], 1)
            for j in range(1, 8, 2):
                act.wait_ge(vT_full, j + 1)
                nc.scalar.activation(v_int[:, 2 * j:2 * j + 2, :], bank16(j, F16).rearrange("p (t d) -> p t d", t=2),
                                     ACT.Copy).then_inc(v_ready, 1)
            act.wait_ge(wq_in, 32)
            nc.scalar.activation(wq_hl[:, 0], wq_raw, ACT.Copy, scale=WS).then_inc(wq_hi, 1)
            with act.Fori(0, QT // 2) as i:
                for s in range(2):
                    act.wait_ge(x_norm_ready, 2 * i + s + 1)
                    act.wait_ge(xT_full, 2 * i + s)
                    nc.scalar.activation(x_hl[s][:, 0, :], x_norm, ACT.Copy).then_inc(x_hi, 1)
                    act.wait_ge(xT_full, 2 * i + s + 1)
                    nc.scalar.activation(tok_T[:, :, bass.ds(i * 2 * P + s * P, P)],
                                         bank16(s, F16).rearrange("p (k t) -> p k t", k=2 * DK),
                                         ACT.Copy).then_inc(tokT_ready, 1)
            act.wait_ge(wp_scaled, 1)
            nc.scalar.activation(wp_hl[:, 0], wp_raw, ACT.Copy).then_inc(wp_hi, 1)
            with act.Fori(0, QT) as i:
                for b in range(2):
                    act.wait_ge(qT_full, 2 * i + b + 1)
                    nc.scalar.activation(q_int[0:64, 8 * b:8 * b + 8, bass.ds(i * P, P)],
                                         bank16(4 + b, F16)[0:64, :].rearrange("p (h q) -> p h q", h=8),
                                         ACT.Copy).then_inc(qT_out, 1)

            def cut_attention(j):
                act.wait_ge(att_ready, HQ * j + HQ)
                nc.scalar.activation(att_hl[:, 0, :], att, ACT.Copy).then_inc(att_hi, 1)

            def cut_rows(j):
                act.wait_ge(x1_normed, j + 1)
                act.wait_ge(x1T_in, 16 * j)
                act.wait_ge(rows_stored, 16 * j)
                nc.scalar.activation(x1_hl[:, 0, :], x1_norm, ACT.Copy).then_inc(x1_hi, 1)

            def attention_tile(i, first, after_rows):
                for h in range(H):
                    u = H * i + h
                    act.wait_ge(max_ready, u + 1)
                    nc.scalar.activation(exp_bias[:, h % 2:h % 2 + 1], s_max[:, h % 2:h % 2 + 1], ACT.Identity,
                                         bias=ln255[:, :], scale=q_step_now[:, 1, h:h + 1]).then_inc(act_step, 1)
                    act.wait_ge(act_step, u + 1)
                    if not first or h >= 2:
                        act.wait_ge(probs_ready, u - 1)
                    for part, (b, n, at) in enumerate(((6, 1, 1536), (3 * (h % 2), 3, 0))):
                        nc.scalar.activation(
                            p_int[h % 2][:, at:at + n * 512].rearrange("p (b k) -> p b k", b=n),
                            psum[:, b:b + n, :], ACT.Exp, bias=exp_bias[:, h % 2:h % 2 + 1],
                            scale=q_step_now[:, 0, h:h + 1], accum_out=p_part[:, h, part:part + 1]).then_inc(exp_done, 1)
                    if h == 1 and after_rows:
                        cut_rows(i - 2)
                    if h == 3 and not first:
                        cut_attention(i - 1)

            attention_tile(0, True, False)
            attention_tile(1, False, False)
            with act.Fori(2, QT) as i:
                attention_tile(i, False, True)
            cut_rows(QT - 2)
            cut_attention(QT - 1)
            cut_rows(QT - 1)

            act.wait_ge(dist_ready, 1)
            nc.scalar.activation(g_inh[:, :, :], g_tmp[:, :, :], ACT.Exp, scale=-1.0).then_inc(neg_exp, 1)
            act.wait_ge(dist_ready, 2)
            nc.scalar.activation(g_w[:, :, :], g_dist[:, :, :], ACT.Exp, scale=-1.0 / 0.1).then_inc(dist_exp, 1)
            nc.scalar.activation(g_fb[:, :, :], g_dist[:, :, :], ACT.Exp, scale=-1.0 / 0.3).then_inc(dist_exp, 1)

            def cut_weights(k, par, m):
                act.wait_ge(w_in[m], 16 * k + 16)
                nc.scalar.activation(w_hl[par][m][:, 0], w_raw[m], ACT.Copy, scale=WS).then_inc(w_hi[m], 1)

            def expert(i, par, following):
                k = 2 * i + par

                def hidden_hi(f):
                    act.wait_ge(hidden_ready[f % 2], 2 * k + f // 2 + 1)
                    nc.scalar.activation(hid_T[par][:, 0, f, :], hidden[f % 2], ACT.Copy).then_inc(hid_hi, 1)

                for f in range(DK):
                    act.wait_ge(gate_full, DK * k + f + 1)
                    act.wait_ge(hidden_ready[f % 2], 2 * k + f // 2)
                    nc.scalar.activation(tanh_g[f % 2], bank(f % 2), ACT.Tanh, scale=0.5 / WS).then_inc(tanh_ready, 1)
                    if f:
                        hidden_hi(f - 1)
                        if following:
                            cut_weights(k + 1, 1 - par, f - 1)
                hidden_hi(DK - 1)
                act.wait_ge(slots_ready, k + 1)
                for t in range(DK):
                    act.wait_ge(down_full, DK * k + t + 1)
                    act.wait_ge(y_added[t], 16 * k)
                    nc.scalar.activation(y_out[:, t, :], bank(4 + t % 2), ACT.Copy, scale=slot_w[par][:, t:t + 1]
                                         ).then_inc(y_ready[t % 2], 1)

            def experts(k0):
                i0 = k0 // 2
                for m in range(3):
                    cut_weights(k0, 0, m)
                with act.Fori(0, E // 2 - 1) as i:
                    expert(i + i0, 0, True)
                    expert(i + i0, 1, True)
                expert(E // 2 - 1 + i0, 0, True)
                expert(E // 2 - 1 + i0, 1, False)

            experts(0)
            act.wait_ge(n_ready, 1)
            with act.If(act.value_load(n_max[0:1, 0:1], min_val=0, max_val=T) > HALF):
                experts(E)

        @block.vector
        def _(dve):
            own = Steps(dve, dve_step)
            for n in range(2):
                part = slice(n * D, (n + 1) * D)
                dve.wait_ge(wkv_hi, n + 1)
                nc.vector.scalar_tensor_tensor(wkv_hl[:, 1, :, part], wkv_raw[:, :, part], WS, wkv_hl[:, 0, :, part],
                                               ALU.mult, ALU.subtract).then_inc(wkv_ready, 1)
            dve.wait_ge(small_in, 80)
            own.link(nc.vector.tensor_scalar(wr_hl[:, 0], wr_raw[:, :, :], WS, None, ALU.mult))
            own.mark(nc.vector.scalar_tensor_tensor(wr_hl[:, 1], wr_raw[:, :, :], WS, wr_hl[:, 0], ALU.mult, ALU.subtract))
            own.mark(nc.vector.reciprocal(r_temp[:, :], temp[:, :]))

            def heads(v):
                return v.rearrange("p (h d) -> p h d", h=H)

            def each(v):
                return v.unsqueeze(2).to_broadcast([P, H, HD])

            key_steps = 9
            head = own.n
            with dve.Fori(0, SG) as g:
                dve.wait_ge(ctx_hi, g + 1)
                nc.vector.tensor_tensor(ctx_hl[:, 1], ctx_raw, ctx_hl[:, 0], ALU.subtract).then_inc(ctx_cut, 1)
                for c in (0, 2):
                    dve.wait_ge(ctxT_full, 4 * g + c + 1)
                    nc.vector.tensor_copy(ctx_T[:, :, c, :], bank16(0, F16).rearrange("p (l k) -> p l k", l=2)
                                          ).then_inc(ctxT_out[0], 1)
                own = Steps(dve, dve_step, head + key_steps * DK * g)
                for s in range(DK):
                    dve.wait_ge(k_out[s % 2], 2 * g + s // 2 + 1)
                    own.link(nc.vector.tensor_tensor(k_work, k_raw[s % 2], bk_all, ALU.add))
                    dve.sem_inc(k_used[s % 2], 1)
                    own.link(nc.vector.tensor_reduce(k_amax[:, :], heads(k_work), AX.X, ALU.max,
                                                     apply_absolute_value=True))
                    own.link(nc.vector.tensor_scalar(k_step[:, :], k_amax[:, :], 1.0 / 127.0, 1e-8, ALU.mult, ALU.max))
                    own.link(nc.vector.reciprocal(k_rstep[:, :], k_step[:, :]))
                    own.link(nc.vector.tensor_tensor(heads(k_work), heads(k_work), each(k_rstep[:, :]), ALU.mult))
                    own.mark(nc.vector.tensor_scalar(k_step_w[:, :], k_step[:, :], WS, None, ALU.mult))
                    own.link(nc.vector.tensor_scalar(k_work, k_work, ROUND, ROUND, ALU.add, ALU.subtract))
                    own.link(nc.vector.tensor_tensor(heads(k_work), heads(k_work), each(k_step_w[:, :]), ALU.mult))
                    dve.wait_ge(kT_full[s % 2], 4 * g + 2 * (s // 2))
                    cut = k_cut[s % 2]
                    own.link(nc.vector.tensor_copy(cut[:, :, 0, :], heads(k_work)))
                    nc.vector.tensor_tensor(cut[:, :, 1, :], heads(k_work), cut[:, :, 0, :], ALU.subtract
                                            ).then_inc(k_cut_ready, 1)
                    dve.wait_ge(k_cut_ready, 4 * g + s + 1)
                assert own.n == key_steps * DK
            own = Steps(dve, dve_step, head + key_steps * DK * SG)

            for b in range(2):
                dve.wait_ge(v_out[b], 2 * SG)
            own.link(nc.vector.tensor_reduce(v_amax[:, :], v_T, AX.X, ALU.max, apply_absolute_value=True))
            own.link(nc.vector.tensor_scalar(v_step[:, :], v_amax[:, :], 1.0 / 127.0, 1e-8, ALU.mult, ALU.max))
            own.mark(nc.vector.tensor_scalar(v_fold[:, :], v_step[:, :], PS, None, ALU.mult))
            own.link(nc.vector.reciprocal(v_rstep[:, :], v_step[:, :]))
            for m in range(DK):
                own.mark(nc.vector.tensor_scalar(v_T[:, m, :], v_T[:, m, :], v_rstep[:, m:m + 1], ROUND, ALU.mult, ALU.add))
            dve.wait_ge(dve_step, own.base + own.n)
            nc.vector.tensor_scalar(v_T_int, v_T, ROUND, None, ALU.subtract).then_inc(v_rounded, 1)
            dve.wait_ge(x_in, 16)
            for t in range(QT):
                own.mark(nc.vector.bn_stats(ln_stats[:, t, :], resid[:, t, :]))
            dve.wait_ge(dve_step, own.base + own.n)
            for t in range(QT):
                own.mark(nc.vector.bn_aggr(ln_mv[:, t, :], ln_stats[:, t, :]))
            dve.wait_ge(dve_step, own.base + own.n)

            def rsqrt_steps(own, n):
                var, half_y = ln_a[:, 0:n], ln_b[:, 0:n]
                y = ln_rstd[:, 0:n]
                own.mark(nc.vector.tensor_copy(ln_mean[:, 0:n], ln_mv[:, 0:n, 0]))
                own.link(nc.vector.tensor_scalar(var, ln_mv[:, 0:n, 1], LN_EPS, None, ALU.add))
                own.link(nc.vector.tensor_scalar(y.bitcast(I32), var.bitcast(I32), 1, None, ALU.logical_shift_right))
                own.link(nc.vector.tensor_scalar(y.bitcast(I32), y.bitcast(I32), -1.0, float(RSQRT_GUESS),
                                                 ALU.mult, ALU.add))
                for _ in range(3):
                    own.link(nc.vector.tensor_tensor(half_y, y, y, ALU.mult))
                    own.link(nc.vector.tensor_tensor(half_y, half_y, var, ALU.mult))
                    own.link(nc.vector.tensor_scalar(half_y, half_y, -0.5, 1.5, ALU.mult, ALU.add))
                    own.link(nc.vector.tensor_tensor(y, y, half_y, ALU.mult))

            rsqrt_steps(own, QT)
            for j in range(0, 8, 2):
                dve.wait_ge(vT_full, j + 1)
                nc.vector.tensor_copy(v_int[:, 2 * j:2 * j + 2, :], bank16(j, F16).rearrange("p (t d) -> p t d", t=2)
                                      ).then_inc(v_ready, 1)

            dve.wait_ge(wq_hi, 1)
            nc.vector.scalar_tensor_tensor(wq_hl[:, 1], wq_raw, WS, wq_hl[:, 0], ALU.mult, ALU.subtract).then_inc(wq_ready, 1)
            q_scale = float(1.0 / np.sqrt(np.float32(HD)))
            own.link(nc.vector.tensor_scalar(bq_all, bq_all, q_scale, None, ALU.mult))
            dve.wait_ge(v_ready, 4 + 4)
            head = own.base + own.n
            with dve.Fori(0, QT // 2) as i:
                for s in range(2):
                    row = resid[:, bass.ds(2 * i + s, 1), :].rearrange("p a d -> p (a d)")
                    dve.wait_ge(x_cut, 2 * i + s)
                    nc.vector.tensor_scalar(x_norm, row, ln_mean[:, bass.ds(2 * i + s, 1)],
                                            ln_rstd[:, bass.ds(2 * i + s, 1)], ALU.subtract, ALU.mult).then_inc(x_norm_ready, 1)
                    dve.wait_ge(x_hi, 2 * i + s + 1)
                    nc.vector.tensor_tensor(x_hl[s][:, 1, :], x_norm, x_hl[s][:, 0, :], ALU.subtract).then_inc(x_cut, 1)
            dve.wait_ge(wp_in, 16)
            for c in range(DK):
                own.mark(nc.vector.tensor_scalar(wp_raw[:, c, :], wp_raw[:, c, :], v_fold[:, c:c + 1], None, ALU.mult))
            dve.wait_ge(dve_step, own.base + own.n)
            dve.sem_inc(wp_scaled, 1)
            dve.wait_ge(wp_hi, 1)
            nc.vector.tensor_tensor(wp_hl[:, 1], wp_raw, wp_hl[:, 0], ALU.subtract).then_inc(wp_ready, 1)
            head = own.base + own.n
            query_steps = 7
            with dve.Fori(0, QT // 2) as i:
                own = Steps(dve, dve_step, head + 2 * query_steps * i)
                for s in range(2):
                    step, minus_step = (q_step[:, bass.ds(2 * i + s, 1), n, :].rearrange("p a h -> p (a h)") for n in range(2))
                    dve.wait_ge(q_full, 2 * i + s + 1)
                    link = nc.vector.scalar_tensor_tensor(q_raw, bank(2 + s), q_scale / WS, bq_all, ALU.mult, ALU.add)
                    own.link(link)
                    dve.sem_inc(q_out, 1)
                    own.link(nc.vector.tensor_reduce(q_amax[:, :], heads(q_raw), AX.X, ALU.max, apply_absolute_value=True))
                    own.link(nc.vector.tensor_scalar(q_amax[:, :], q_amax[:, :], 1.0 / 127.0, 1e-8, ALU.mult, ALU.max))
                    own.mark(nc.vector.tensor_scalar(step, q_amax[:, :], 1.0 / WS, None, ALU.mult))
                    own.mark(nc.vector.tensor_scalar(minus_step, q_amax[:, :], -1.0 / WS, None, ALU.mult))
                    own.link(nc.vector.reciprocal(q_rstep[:, :], q_amax[:, :]))
                    own.link(nc.vector.tensor_tensor(heads(q_raw), heads(q_raw), each(q_rstep[:, :]), ALU.mult))
                    dve.wait_ge(qT_full, 4 * i)
                    nc.vector.tensor_scalar(q_cut[s], heads(q_raw).unsqueeze(2).to_broadcast([P, H, 2, HD]), ROUND, ROUND,
                                            ALU.add, ALU.subtract).then_inc(q_cut_ready, 1)
                    dve.wait_ge(q_cut_ready, 2 * i + s + 1)
                assert own.n == 2 * query_steps
            base = head + query_steps * QT

            def convert(i, h):
                dve.wait_ge(exp_done, 2 * (H * i + h) + 2)
                if h >= 2:
                    dve.wait_ge(probsT_in[(h - 2) % 4], 64 * i + 16 * ((h - 2) // 4 + 1))
                else:
                    dve.wait_ge(probsT_in[(h - 2) % 4], 64 * i)
                nc.vector.tensor_copy(p_half[h % 2], p_int[h % 2]).then_inc(probs_ready, 1)

            def divide(i, n, own):
                these = slice(HQ * n, HQ * n + HQ)
                own.link(nc.vector.tensor_tensor(p_sum[:, :], p_part[:, these, 0], p_part[:, these, 1], ALU.add))
                own.link(nc.vector.reciprocal(p_rsum[:, :], p_sum[:, :]))
                dve.wait_ge(pv_done, H * i + HQ * n + HQ)
                if n == 0:
                    dve.wait_ge(att_cut, i)
                at = (n % 2) * HQ * HD
                nc.vector.tensor_tensor(heads(att)[:, these, :], bank(7)[:, at:at + HQ * HD].rearrange("p (h d) -> p h d", h=HQ),
                                        p_rsum[:, :].unsqueeze(2).to_broadcast([P, HQ, HD]), ALU.mult).then_inc(att_ready, 1)

            def after_attention(j, h, own):
                if h == 3:
                    divide(j, 3, own)
                if h in (11, 15):
                    half = slice(256 * (h == 15), 256 * (h == 15) + 256)
                    if h == 11:
                        dve.wait_ge(x_bias_ready, j + 1)
                        dve.wait_ge(stored, 16 * j)
                    dve.wait_ge(proj_full, 2 * j + (h == 15) + 1)
                    link = nc.vector.scalar_tensor_tensor(x1[:, half], bank(7)[:, 256:512], 1.0 / PS, x_bias[:, half], ALU.mult, ALU.add)
                    link.then_inc(proj_out, 1)
                if h == 15:
                    dve.wait_ge(proj_out, 2 * j + 2)
                    own.link(nc.vector.bn_stats(ln1_stats[:, :], x1))
                    dve.sem_inc(x1_summed, 1)
                    nc.vector.bn_aggr(ln1_mv[:, :], ln1_stats[:, :]).then_inc(x1_stats, 1)

            def attention_tile(i, base, first):
                own = Steps(dve, dve_step, base)
                for h in range(H):
                    u = H * i + h
                    if h >= 2:
                        convert(i, h - 2)
                    elif not first:
                        convert(i - 1, H + h - 2)
                    if not first:
                        after_attention(i - 1, h, own)
                    if h in (7, 11, 15):
                        divide(i, h // 4 - 1, own)
                    if h in (0, H // 2):
                        half = slice(h, h + H // 2)
                        own.mark(nc.vector.tensor_copy(
                            q_step_now[:, :, half], q_step[:, bass.ds(i, 1), :, half].rearrange("p a n h -> p (a n) h")))
                    first_bank = 3 * (h % 2)
                    dve.wait_ge(scores_full, 3 * u + 1)
                    nc.vector.tensor_reduce(s_part[:, h % 2, 0:1], psum[:, first_bank:first_bank + 2, :], AX.XY, ALU.max)
                    dve.wait_ge(scores_full, 3 * u + 2)
                    nc.vector.tensor_reduce(s_part[:, h % 2, 1:2], bank(first_bank + 2), AX.X, ALU.max)
                    dve.wait_ge(scores_full, 3 * u + 3)
                    own.link(nc.vector.tensor_reduce(s_part[:, h % 2, 2:3], bank(6), AX.X, ALU.max))
                    nc.vector.tensor_reduce(s_max[:, h % 2:h % 2 + 1], s_part[:, h % 2, :], AX.X, ALU.max).then_inc(max_ready, 1)
                return own.n

            base += attention_tile(0, base, True)
            per_tile = H + 2 + 2 * HQ + 1
            with dve.Fori(1, QT) as i:
                assert attention_tile(i, base + per_tile * (i - 1), False) == per_tile
            base += per_tile * (QT - 1)
            own = Steps(dve, dve_step, base)
            for h in (H - 2, H - 1):
                convert(QT - 1, h)
            for h in range(H):
                after_attention(QT - 1, h, own)

            def tokens(v):
                return v.unsqueeze(2).to_broadcast([P, QT, E])

            dve.wait_ge(logits_full, 1)
            zs = nc.vector.tensor_scalar(g_tmp[:, :, :], bank(0)[:, 0:QT * E].rearrange("p (t e) -> p t e", t=QT), 1.0 / WS, r_temp[:, 0:1], ALU.mult, ALU.mult)
            zs.then_inc(dist_ready, 1)
            dve.wait_ge(neg_exp, 1)
            own.link(nc.vector.tensor_scalar(g_inh[:, :, :], g_inh[:, :, :], 1.0, None, ALU.add))
            own.link(nc.vector.reciprocal(g_inh[:, :, :], g_inh[:, :, :]))
            own.link(nc.vector.tensor_scalar(g_tmp[:, :, :], g_inh[:, :, :], GOLDEN_CENTER, None, ALU.subtract))
            own.link(nc.vector.tensor_scalar(g_dist[:, :, :], g_tmp[:, :, :], -1.0, None, ALU.mult))
            nc.vector.tensor_tensor(g_dist[:, :, :], g_dist[:, :, :], g_tmp[:, :, :], ALU.max).then_inc(dist_ready, 1)
            own.link(nc.vector.tensor_scalar(g_zone[:, :, :], g_inh[:, :, :], GOLDEN_UPPER, None, ALU.is_le))
            own.link(nc.vector.scalar_tensor_tensor(g_zone[:, :, :], g_inh[:, :, :], GOLDEN_LOWER, g_zone[:, :, :],
                                                    ALU.is_ge, ALU.mult))
            dve.wait_ge(dist_exp, 2)
            own.link(nc.vector.tensor_tensor(g_w[:, :, :], g_w[:, :, :], g_zone[:, :, :], ALU.mult))
            own.link(nc.vector.tensor_reduce(g_sum[:, :], g_w[:, :, :], AX.X, ALU.add))
            own.mark(nc.vector.tensor_scalar(g_none[:, :], g_sum[:, :], 1e-8, None, ALU.is_lt))
            own.mark(nc.vector.tensor_scalar(g_has[:, :], g_sum[:, :], 1e-8, None, ALU.is_ge))
            mine = g_fb[:, :, :].unsqueeze(3).to_broadcast([P, QT, E, E])
            others = g_fb[:, :, :].unsqueeze(2).to_broadcast([P, QT, E, E])
            own.mark(nc.vector.tensor_tensor(g_gt, others, mine, ALU.is_gt))
            own.mark(nc.vector.tensor_tensor(g_eq, others, mine, ALU.is_equal))
            dve.wait_ge(dve_step, own.base + own.n)
            dve.wait_ge(tri_ready, 1)
            own.link(nc.vector.tensor_tensor(g_eq, g_eq,
                                             lower_tri[:, :, :].unsqueeze(1).to_broadcast([P, QT, E, E]), ALU.mult))
            own.link(nc.vector.tensor_tensor(g_gt, g_gt, g_eq, ALU.add))
            own.link(nc.vector.tensor_reduce(g_rank[:, :, :], g_gt, AX.X, ALU.add))
            own.link(nc.vector.scalar_tensor_tensor(g_fb[:, :, :], g_rank[:, :, :], 2.0, g_fb[:, :, :], ALU.is_lt, ALU.mult))
            own.link(nc.vector.tensor_reduce(g_sum[:, :], g_fb[:, :, :], AX.X, ALU.add))
            own.link(nc.vector.tensor_scalar(g_sum[:, :], g_sum[:, :], 1e-8, None, ALU.max))
            own.link(nc.vector.reciprocal(g_sum[:, :], g_sum[:, :]))
            own.link(nc.vector.tensor_tensor(g_sum[:, :], g_sum[:, :], g_none[:, :], ALU.mult))
            own.mark(nc.vector.tensor_tensor(g_fb[:, :, :], g_fb[:, :, :], tokens(g_sum[:, :]), ALU.mult))
            own.mark(nc.vector.tensor_tensor(g_w[:, :, :], g_w[:, :, :], tokens(g_has[:, :]), ALU.mult))
            dve.wait_ge(dve_step, own.base + own.n)
            own.link(nc.vector.tensor_tensor(g_w[:, :, :], g_w[:, :, :], g_fb[:, :, :], ALU.add))
            own.link(nc.vector.tensor_reduce(g_sum[:, :], g_w[:, :, :], AX.X, ALU.add))
            own.link(nc.vector.tensor_scalar(g_sum[:, :], g_sum[:, :], 1e-8, None, ALU.max))
            own.link(nc.vector.reciprocal(g_sum[:, :], g_sum[:, :]))
            own.link(nc.vector.tensor_scalar(g_sum[:, :], g_sum[:, :], 1.0 / WS, None, ALU.mult))
            own.link(nc.vector.tensor_tensor(g_w[:, :, :], g_w[:, :, :], tokens(g_sum[:, :]), ALU.mult))

            nc.vector.tensor_scalar(mask, g_w[:, :, :], 0.0, None, ALU.not_equal).then_inc(mask_ready, 1)
            dve.wait_ge(tri_ready, 5)
            own.mark(nc.vector.tensor_copy(tok_w[:, :, :, 0], tokens(token[:, 1, :])))
            own.mark(nc.vector.tensor_copy(tok_w[:, :, :, 1], tokens(token[:, 2, :])))
            own.link(nc.vector.tensor_copy(tok_w[:, :, :, 2], g_w[:, :, :]))
            own.link(nc.vector.tensor_tensor(g_tmp[:, :, :], g_w[:, :, :], tok_w[:, :, :, 2], ALU.subtract))
            own.link(nc.vector.tensor_copy(tok_w[:, :, :, 3], g_tmp[:, :, :]))
            own.mark(nc.vector.tensor_tensor(tok_w[:, :, :, 4], g_tmp[:, :, :], tok_w[:, :, :, 3], ALU.subtract))
            dve.wait_ge(count_full, 1)
            place = bank(1)[:, 0:QT * E].rearrange("p (t e) -> p t e", t=QT)
            own.mark(nc.vector.tensor_copy(g_count[:, :], bank(1)[:, QT * E:QT * E + E]))
            nc.vector.tensor_reduce(n_max[:, :], bank(1)[:, QT * E:QT * E + E], AX.X, ALU.max).then_inc(n_ready, 1)
            own.link(nc.vector.tensor_tensor(g_rank[:, :, :], place, tokens(token[:, 0, :]), ALU.subtract))
            own.link(nc.vector.tensor_tensor(slot, g_count[:, :].unsqueeze(1).to_broadcast([P, QT, E]), g_rank[:, :, :],
                                             ALU.subtract))
            own.link(nc.vector.tensor_tensor(g_fb[:, :, :], place, slot, ALU.subtract))
            own.link(nc.vector.tensor_tensor(g_fb[:, :, :], g_fb[:, :, :], mask, ALU.mult))
            own.link(nc.vector.tensor_tensor(slot, slot, g_fb[:, :, :], ALU.add))

            def cut_weights(k, par, m):
                dve.wait_ge(w_hi[m], k + 1)
                nc.vector.scalar_tensor_tensor(w_hl[par][m][:, 1], w_raw[m], WS, w_hl[par][m][:, 0],
                                               ALU.mult, ALU.subtract).then_inc(w_ready[m], 1)

            def select_tokens(own, e, first_slot):
                own.link(nc.vector.tensor_scalar(slot_now[:, :], slot[:, :, bass.ds(e, 1)].rearrange("p t a -> p (t a)"),
                                                 float(-first_slot), None, ALU.add))
                for t in range(QT):
                    ins = nc.vector.tensor_scalar(select[:, t, :], slot_row[:, :], slot_now[:, t:t + 1], None, ALU.is_equal)
                ins.then_inc(select_ready, 1)

            def slots(own, i, par):
                k = 2 * i + par
                dve.wait_ge(list_full, k + 1)
                dve.wait_ge(y_added[DK - 1], 16 * before(k, 1))
                parts = bank(7)[:, 0:5 * DK].rearrange("p (s c) -> p s c", c=5)
                own.link(nc.vector.tensor_reduce(slot_tok_f[:, :], parts[:, :, 0:2], AX.X, ALU.add))
                own.mark(nc.vector.tensor_copy(slot_tok[par][:, :], slot_tok_f[:, :]))
                nc.vector.tensor_reduce(slot_w[par][:, :], parts[:, :, 2:5], AX.X, ALU.add).then_inc(slots_ready, 1)

            def expert(i, par, base, e, first_slot, following):
                own = Steps(dve, dve_step, base)
                k = 2 * i + par
                after = (i, 1) if par == 0 else (i + 1, 0)

                def hidden_lo(f):
                    dve.wait_ge(hid_hi, DK * k + f + 1)
                    nc.vector.tensor_tensor(hid_T[par][:, 1, f, :], hidden[f % 2], hid_T[par][:, 0, f, :], ALU.subtract
                                            ).then_inc(hid_cut, 1)

                for f in range(DK):
                    dve.wait_ge(tanh_ready, DK * k + f + 1)
                    own.link(nc.vector.scalar_tensor_tensor(gate_1[f % 2], tanh_g[f % 2], 1.0, bank(f % 2), ALU.add, ALU.mult))
                    dve.wait_ge(up_full, DK * k + f + 1)
                    dve.wait_ge(hid_cut, DK * k + max(f - 1, 0))
                    nc.vector.scalar_tensor_tensor(hidden[f % 2], gate_1[f % 2], 0.5 / (WS * WS), bank(2 + f % 2), ALU.mult, ALU.mult
                                                   ).then_inc(hidden_ready[f % 2], 1)
                    if f:
                        hidden_lo(f - 1)
                    if following and f == 0:
                        select_tokens(own, e + 1, first_slot)
                    if following and f >= 1:
                        cut_weights(k + 1, 1 - par, f - 1)
                    if following and f == 2:
                        slots(own, *after)
                hidden_lo(DK - 1)
                return own.n

            def experts(k0, first_slot, base):
                i0 = k0 // 2
                own = Steps(dve, dve_step, base)
                select_tokens(own, 0, first_slot)
                slots(own, i0, 0)
                for m in range(3):
                    cut_weights(k0, 0, m)
                base = base + own.n
                n = DK + 3
                with dve.Fori(0, E // 2 - 1) as i:
                    assert expert(i + i0, 0, base + 2 * n * i, 2 * i, first_slot, True) == n
                    assert expert(i + i0, 1, base + 2 * n * i + n, 2 * i + 1, first_slot, True) == n
                base += 2 * n * (E // 2 - 1)
                base += expert(E // 2 - 1 + i0, 0, base, E - 2, first_slot, True)
                base += expert(E // 2 - 1 + i0, 1, base, E - 1, first_slot, False)
                return base

            base = experts(0, 0, own.base + own.n)
            with dve.If(dve.value_load(n_max[0:1, 0:1], min_val=0, max_val=T) > HALF):
                experts(E, HALF, base)

        @block.tensor
        def _(pe):
            def passed():
                pe.sem_inc(pe_passed, 1)

            def product(out, lhs, rhs, pieces=DK, passes=PASSES):
                n, last = 0, len(passes) * pieces - 1
                for c in range(pieces):
                    for a, b in passes:
                        ins = nc.tensor.matmul(out, lhs(a, c), rhs(b, c), start=n == 0, stop=n == last)
                        n += 1
                return ins

            pe.wait_ge(ident_ready, 2)
            with pe.Fori(0, SG) as g:
                pe.wait_ge(ctx_cut, g + 1)
                for c in range(DK):
                    pe.wait_ge(ctxT_out[c % 2], 2 * g + c // 2)
                    for part in range(2):
                        for s in range(DK):
                            ins = nc.tensor.transpose(bank16(c % 2, F16)[:, part * 512 + s * P:part * 512 + s * P + P],
                                                      ctx_hl[:, part, s, c * P:c * P + P], ident_h[:, :])
                    ins.then_inc(ctxT_full, 1)
                for b in range(2):
                    pe.wait_ge(ctxT_out[b], 2 * g + 2)
                    pe.wait_ge(wkv_ready, 2)
                for s in range(DK):
                    pe.wait_ge(k_out[s % 2], 2 * g + s // 2)
                    product(bank(2 + s % 2), lambda a, c: ctx_T[:, a, c, s * P:s * P + P],
                            lambda b, c: wkv_hl[:, b, c, 0:D]).then_inc(k_full, 1)
                for s in range(DK):
                    pe.wait_ge(v_out[s % 2], 2 * g + s // 2)
                    product(bank(4 + s % 2), lambda a, c: wkv_hl[:, a, c, D + s * P:D + s * P + P],
                            lambda b, c: ctx_T[:, b, c, :]).then_inc(v_full, 1)
                    pe.wait_ge(k_cut_ready, 4 * g + s + 1)
                    for b in range(2):
                        pe.wait_ge(kT_out[b], 4 * g + s)
                        passed()
                        for h in range(8):
                            ins = nc.tensor.transpose(bank16(6 + b, F16)[0:64, h * P:h * P + P],
                                                      k_cut[s % 2][:, 8 * b + h].rearrange("p r d -> p (r d)"), ident_h[:, :])
                        ins.then_inc(kT_full[s % 2], 1)
            pe.wait_ge(v_rounded, 1)
            for b in range(2):
                pe.wait_ge(kT_out[b], 4 * SG)
            for j in range(8):
                for t in range(2):
                    for m in range(DK):
                        ins = nc.tensor.transpose(bank16(j, F16)[:, t * 512 + m * P:t * 512 + m * P + P],
                                                  v_T_int[:, m, (2 * j + t) * P:(2 * j + t + 1) * P], ident_h[:, :])
                ins.then_inc(vT_full, 1)

            pe.wait_ge(v_ready, 8)
            with pe.Fori(0, QT // 2) as i:
                for s in range(2):
                    pe.wait_ge(x_cut, 2 * i + s + 1)
                    pe.wait_ge(tokT_ready, 2 * i)
                    for part in range(2):
                        for c in range(DK):
                            ins = nc.tensor.transpose(bank16(s, F16)[:, (part * DK + c) * P:(part * DK + c + 1) * P],
                                                      x_hl[s][:, part, c * P:c * P + P], ident_h[:, :])
                    ins.then_inc(xT_full, 1)
            pe.wait_ge(tokT_ready, QT)
            pe.wait_ge(wq_ready, 1)

            def queries(i, s):
                product(bank(2 + s), lambda a, c: tok_T[:, a * DK + c, bass.ds(i * P, P)],
                        lambda b, c: wq_hl[:, b, c, :]).then_inc(q_full, 1)

            def transpose_queries(i, s):
                pe.wait_ge(q_cut_ready, i + 1)
                pe.wait_ge(qT_out, 2 * i)
                passed()
                for b in range(2):
                    for h in range(8):
                        ins = nc.tensor.transpose(bank16(4 + b, F16)[0:64, h * P:h * P + P],
                                                  q_cut[s][:, 8 * b + h].rearrange("p r d -> p (r d)"), ident_h[:, :])
                    ins.then_inc(qT_full, 1)

            queries(0, 0)
            queries(1, 1)
            with pe.Fori(0, QT // 2 - 1) as i:
                for s in range(2):
                    transpose_queries(2 * i + s, s)
                    pe.wait_ge(q_out, 2 * i + s + 1)
                    queries(2 * i + s + 2, s)
            for s in range(2):
                transpose_queries(QT - 2 + s, s)

            pe.wait_ge(qT_out, 2 * QT)
            pe.wait_ge(wp_ready, 1)

            def values(i, h, after=False):
                n, at = h // HQ, (h // HQ) % 2 * HQ * HD + h % HQ * HD
                if h % HQ == 0:
                    pe.wait_ge(att_ready, HQ * i + n)
                if h in (8, 12) and after:
                    pe.wait_ge(proj_out, 2 * (i - 1) + h // 4 - 1)
                pe.wait_ge(probsT_in[h % 4], 64 * i + 16 * (h // 4 + 1))
                for t in range(KT):
                    ins = nc.tensor.matmul(bank(7)[:, at:at + HD], p_T[h % 4][:, t, :],
                                           v_int[:, t, h * HD:h * HD + HD], start=t == 0, stop=t == KT - 1)
                ins.then_inc(pv_done, 1)

            def after_attention(j, h):
                if 7 <= h <= 14:
                    n = h - 7
                    if n == 0:
                        pe.wait_ge(attT_in, 16 * j + 16)
                    if n % 4 == 0:
                        pe.wait_ge(proj_out, 2 * j + n // 4)
                    ins = product(bank(7)[:, 256 + n % 4 * 64:320 + n % 4 * 64], lambda a, c: att_T[:, a * DK + c, :],
                                  lambda b, c: wp_hl[:, b, c, n * 64:n * 64 + 64])
                    if n % 4 == 3:
                        ins.then_inc(proj_full, 1)

            def scores(i, h, first):
                u = H * i + h
                if not first or h >= 2:
                    pe.wait_ge(exp_done, 2 * u - 2)
                    passed()
                for piece in range(4):
                    if piece == 3 and (not first or h >= 1):
                        pe.wait_ge(exp_done, 2 * u - 1)
                        passed()
                    ins = nc.tensor.matmul(bank(6 if piece == 3 else 3 * (h % 2) + piece), q_int[0:64, h, bass.ds(i * P, P)],
                                           key_parts[0:64, h, piece * 512:piece * 512 + 512], start=True, stop=True)
                    if piece >= 1:
                        ins.then_inc(scores_full, 1)

            def attention_tile(i, first):
                for h in range(H):
                    scores(i, h, first)
                    if h >= 3:
                        values(i, h - 3, not first)
                    elif not first:
                        values(i - 1, h - 3 + H)
                    if not first:
                        after_attention(i - 1, h)

            attention_tile(0, True)
            with pe.Fori(1, QT) as i:
                attention_tile(i, False)
            for h in range(H - 3, H):
                values(QT - 1, h)
            for h in range(H):
                after_attention(QT - 1, h)

            pe.wait_ge(x1T_in, 16 * QT)
            pe.wait_ge(proj_out, 2 * QT)
            for t in range(QT):
                ins = product(bank(0)[:, t * E:t * E + E], lambda a, c: tok_T[:, a * DK + c, t * P:t * P + P],
                              lambda b, c: wr_hl[:, b, c, :])
            ins.then_inc(logits_full, 1)

            pe.wait_ge(mask_ready, 1)
            for t in range(QT + 1):
                for r in range(min(t + 1, QT)):
                    ins = nc.tensor.matmul(bank(1)[:, t * E:t * E + E], (earlier if r == t else ones)[:, :], mask[:, r, :],
                                           start=r == 0, stop=r == min(t, QT - 1))
            ins.then_inc(count_full, 1)

            def list_slots(i, par, e):
                k = 2 * i + par
                pe.wait_ge(select_ready, k + 1)
                pe.wait_ge(slots_ready, k)
                for s in range(DK):
                    for t in range(QT):
                        ins = nc.tensor.matmul(bank(7)[:, 5 * s:5 * s + 5], select[:, t, s * P:s * P + P],
                                               tok_w[:, t, bass.ds(e, 1), :].rearrange("p a c -> p (a c)"),
                                               start=t == 0, stop=t == QT - 1)
                ins.then_inc(list_full, 1)

            def expert(i, par, e, following):
                k = 2 * i + par
                gate, up, down = w_hl[par]
                pe.wait_ge(selT_in[par], 64 * i + 64)
                for f in range(DK):
                    cols = slice(f * P, f * P + P)
                    if following and f == DK - 1:
                        list_slots(*((i, 1) if par == 0 else (i + 1, 0)), e + 1)
                    pe.wait_ge(hidden_ready[f % 2], 2 * k + f // 2)
                    if f == 0:
                        pe.wait_ge(w_ready[0], k + 1)
                    product(bank(f % 2), lambda a, d: gate[:, a, d, cols], lambda b, d: x_sel_T[par][:, :, b * DK + d, :]
                            ).then_inc(gate_full, 1)
                    if f == 0:
                        pe.wait_ge(w_ready[1], k + 1)
                    product(bank(2 + f % 2), lambda a, d: up[:, a, d, cols], lambda b, d: x_sel_T[par][:, :, b * DK + d, :]
                            ).then_inc(up_full, 1)
                pe.wait_ge(w_ready[2], k + 1)
                pe.wait_ge(hid_cut, DK * k + DK)
                for t in range(DK):
                    pe.wait_ge(y_ready[t % 2], 2 * k + t // 2)
                    product(bank(4 + t % 2), lambda a, d: hid_T[par][:, a, d, t * P:t * P + P],
                            lambda b, d: down[:, b, d, :]).then_inc(down_full, 1)

            def experts(k0):
                i0 = k0 // 2
                list_slots(i0, 0, 0)
                with pe.Fori(0, E // 2 - 1) as i:
                    expert(i + i0, 0, 2 * i, True)
                    expert(i + i0, 1, 2 * i + 1, True)
                expert(E // 2 - 1 + i0, 0, E - 2, True)
                expert(E // 2 - 1 + i0, 1, E - 1, False)

            experts(0)
            pe.wait_ge(n_ready, 1)
            with pe.If(pe.value_load(n_max[0:1, 0:1], min_val=0, max_val=T) > HALF):
                experts(E)


_INS = ['x', 'ctx_2048', 'L0_xattn_Wq', 'L0_xattn_bq', 'L0_xattn_Wkv', 'L0_xattn_bkv', 'L0_xattn_Wp', 'L0_xattn_bp',
        'L0_ffn_Wg', 'L0_ffn_Wu', 'L0_ffn_Wd', 'L0_ffn_Wr', 'L0_ffn_temperature']


def kernel(**inputs):
    import numpy as _np
    import concourse.bacc as _bacc
    from concourse import mybir as _mybir
    from concourse.bass_utils import run_bass_kernel_spmd as _run

    nc = _bacc.Bacc("TRN2", target_bir_lowering=False, num_devices=1)
    arrays, args = {}, []
    for name in _INS:
        a = _np.ascontiguousarray(inputs[name])
        arrays[f"in_{name}_dram"] = a
        args.append(nc.dram_tensor(f"in_{name}_dram", a.shape, _mybir.dt.from_np(a.dtype), kind="ExternalInput").ap())
    out = nc.dram_tensor("out_0_dram", (2, 512, 512), _mybir.dt.float32, kind="ExternalOutput").ap()
    xattn_moe(nc, *args, out)
    r = _run(nc, [arrays], core_ids=[0])
    return r.results[0]["out_0_dram"]
```

```python
import concourse.bass as bass
from concourse import mybir
from contextlib import ExitStack
import numpy as np

F32, F16, BF16 = mybir.dt.float32, mybir.dt.float16, mybir.dt.bfloat16
I16, I32 = mybir.dt.int16, mybir.dt.int32
ALU = mybir.AluOpType
ACT = mybir.ActivationFunctionType
AX = mybir.AxisListType

P = 128
T, S, D = 1024, 2048, 512
H, HD = 16, 32
HQ = 8
E, F = 8, 512
HALF = T // 2
DK = D // P
QT, KT = T // P, S // P
SG = S // 512
WS = 64.0
PS = 2.0 ** 14
Q_BANKS = (4, 5, 7, 3)
LN255 = float(np.log(255.0))
HALVES = (slice(0, 2), slice(2, 4))
PASSES = ((0, 0), (0, 1), (1, 0))
LN_EPS = 1e-5
RSQRT_GUESS = 0x5F3759DF
GOLDEN_CENTER = float(1.0 / np.e)
GOLDEN_LOWER = float(0.5 - np.log(4.0 / 3.0))
GOLDEN_UPPER = 0.5


class Steps:

    def __init__(self, engine, sem, base=0, passed=None):
        self.engine, self.sem, self.base, self.n, self.passed = engine, sem, base, 0, passed

    def mark(self, instruction):
        self.n += 1
        instruction.then_inc(self.sem, 1)
        return self.n

    def after(self, n):
        self.engine.wait_ge(self.sem, self.base + n)

    def link(self, instruction):
        self.mark(instruction)
        self.engine.wait_ge(self.sem, self.base + self.n)
        if self.passed:
            self.passed()


def before(k, n):
    return max(k - n, 0) if isinstance(k, int) else k - n


def xattn_moe(nc, A_x, A_ctx, A_wq, A_bq, A_wkv, A_bkv, A_wp, A_bp, A_wg, A_wu, A_wd, A_wr, A_temp, out):
    x_t = A_x.rearrange("b (t p) d -> p (b t) d", p=P)
    ctx_g = A_ctx.rearrange("b (g s p) d -> (b g) p s d", p=P, s=DK)
    wkv_v = A_wkv.rearrange("(c p) n -> p c n", p=P)
    out_rows = out.rearrange("b t d -> (b t) d")
    x1_rows = nc.dram_tensor("x1_rows", (T, 2 * D), F16, kind="Internal").ap()
    w_rows = [w.rearrange("e (c p) n -> e p c n", p=P) for w in (A_wg, A_wu, A_wd)]

    ctx = ExitStack()
    with ctx:
        def sb(name, shape, dt=F32):
            return ctx.enter_context(nc.sbuf_tensor(name, shape, dt))

        def sem(name):
            return ctx.enter_context(nc.semaphore(name))

        keys_region = sb("keys_region", [P, H * S // 4])
        query_region = sb("query_region", [P, H * T // 4])
        token_region = sb("token_region", [P, DK * T])
        spare = sb("spare", [P, 12288])
        work = sb("work", [P, 13824])
        resid = sb("resid", [P, QT, D])
        values_region = sb("values_region", [P, KT * D // 2])

        def view(region, at, words, dt, pattern=None, **dims):
            v = region[:, at:at + words]
            if dt != F32:
                v = v.bitcast(dt)
            return v.rearrange(pattern, **dims) if pattern else v

        key_parts = view(keys_region, 0, H * S // 4, F16, "p (h k) -> p h k", h=H // 2)
        q_int = view(query_region, 0, H * T // 4, F16, "p (h q) -> p h q", h=H // 2)
        v_int = view(values_region, 0, KT * D // 2, F16, "p (t d) -> p t d", t=KT)
        tok_T = view(token_region, 0, DK * T, F16, "p (k t) -> p k t", k=2 * DK)

        wkv_raw = view(token_region, 0, DK * 2 * D, F32, "p (c n) -> p c n", c=DK)
        wkv_hl = view(query_region, 0, DK * 2 * D, F16, "p (l c n) -> p l c n", l=2, c=DK)
        v_T = view(spare, 0, DK * S, F32, "p (m k) -> p m k", m=DK)
        wq_hl = view(spare, 8192, 2048, F16, "p (l c n) -> p l c n", l=2, c=DK)
        wp_raw = view(spare, 10240, 2048, F32, "p (c n) -> p c n", c=DK)
        ctx_T = view(work, 0, 8192, F16, "p (g s k t) -> p g s k t", g=SG, s=DK, k=2 * DK)
        ctx_raw = view(work, 8192, 2048, F32, "p (s d) -> p s d", s=DK)
        wq_raw = view(work, 8192, 2048, F32, "p (c n) -> p c n", c=DK)
        ctx_hl = view(work, 10240, 2048, F16, "p (s l d) -> p s l d", s=DK, l=2)
        bias_raw = view(work, 12288, 1024, F32, "p (n d) -> p n d", n=2)
        bias_hi = view(work, 13312, 512, F16, "p (n d) -> p n d", n=2)
        k_cut = [view(values_region, 512 * n, 512, F16, "p (h r d) -> p h r d", h=H, r=2) for n in range(2)]
        k_deq = [view(values_region, 1024 + 512 * n, 512, F32, "p (h d) -> p h d", h=H) for n in range(2)]
        k_int = [view(values_region, 2048 + 256 * n, 256, I16, "p (h d) -> p h d", h=H) for n in range(2)]
        x_norm = view(values_region, 2560, 512, F32)
        x_hl = view(values_region, 3072, 512, F16, "p (l d) -> p l d", l=2)
        bp_all = view(values_region, 3584, 512, F32)
        q_cut = [view(work, 12288 + 512 * n, 512, F16, "p (h r d) -> p h r d", h=H, r=2) for n in range(2)]
        q_i16 = [view(work, 13312 + 256 * n, 256, I16, "p (h d) -> p h d", h=H) for n in range(2)]
        v_i16 = view(work, 0, DK * S // 2, I16, "p (m k) -> p m k", m=DK)
        v_T_int = view(work, 4096, DK * S // 2, F16, "p (m k) -> p m k", m=DK)
        p_int = [view(work, 1024 * n, 1024, I16) for n in range(2)]
        p_half = [view(region, at, 1024, F16) for region, at in ((work, 2048), (work, 3072), (spare, 10240), (spare, 11264))]
        p_T = [view(work, 4096 + 1024 * n, 1024, F16, "p (t q) -> p t q", t=KT) for n in range(4)]
        att = view(work, 8192, 512, F32)
        att_hl = view(work, 8704, 512, F16, "p (l d) -> p l d", l=2)
        att_T = view(work, 9216, 512, F16, "p (k t) -> p k t", k=2 * DK)
        q_now = view(work, 9728, 512, F16, "p (h q) -> p h q", h=H // 2)
        wp_hl = view(work, 10240, 2048, F16, "p (l c n) -> p l c n", l=2, c=DK)
        x1 = view(work, 12288, 512, F32)
        x1_norm = view(work, 12800, 512, F32)
        x1_hl = view(work, 13312, 512, F16, "p (l d) -> p l d", l=2)
        g_gt, g_eq = (view(work, 10240 + 512 * n, 512, F32, "p (t a b) -> p t a b", t=QT, a=E) for n in range(2))
        tok_w = view(work, 11264, QT * E * 5 // 2, BF16, "p (t e c) -> p t e c", t=QT, e=E)
        slot = view(work, 11424, QT * E, F32, "p (t e) -> p t e", t=QT)
        masks = view(work, 11488, (QT + 1) * E // 2, BF16)
        mask = masks[:, 0:QT * E].rearrange("p (t e) -> p t e", t=QT)
        w_raw = [view(spare, 2048 * m, 2048, F32, "p (c n) -> p c n", c=DK) for m in range(3)]
        w_hl = [[view(region, at + 2048 * m, 2048, F16, "p (l c n) -> p l c n", l=2, c=DK) for m in range(3)]
                for region, at in ((spare, 6144), (keys_region, 0))]
        y_out = view(keys_region, 6144, 2048, F32, "p (s d) -> p s d", s=DK)
        hid_T = [view(query_region, 2048 * c, 2048, F16, "p (l f t) -> p l f t", l=2, f=DK) for c in range(2)]
        x_sel_T = [view(work, 2048 * c, 2048, F16, "p (s k t) -> p s k t", s=DK, k=2 * DK) for c in range(2)]
        x_sel = [view(work, 4096 + 2048 * c, 2048, F16, "p (s n) -> p s n", s=DK) for c in range(2)]
        select = view(work, 8192, 2048, BF16, "p (t s) -> p t s", t=QT)
        e_work = resid[:, :, :].rearrange("p t d -> p (t d)")
        tanh_g = [view(e_work, 512 * n, 512, F32) for n in range(2)]
        gate_1 = [view(e_work, 1024 + 512 * n, 512, F32) for n in range(2)]
        hidden = [view(e_work, 2048 + 512 * n, 512, F32) for n in range(2)]

        scratch = sb("scratch", [P, P])
        bias_hl = sb("bias_hl", [P, 2, D], F16)
        bias_one = sb("bias_one", [P, P], F16)
        bv_col = sb("bv_col", [P, DK])
        wr_raw = sb("wr_raw", [P, DK, E])
        wr_hl = sb("wr_hl", [P, 2, DK, E], F16)
        temp = sb("temp", [P, 1])
        r_temp = sb("r_temp", [P, 1])
        k_amax, k_step, k_rstep = (sb(n, [P, H]) for n in ("k_amax", "k_step", "k_rstep"))
        v_part = sb("v_part", [P, DK, SG])
        v_amax, v_step, v_rstep, v_fold = (sb(n, [P, DK]) for n in ("v_amax", "v_step", "v_rstep", "v_fold"))
        ln_stats = sb("ln_stats", [P, QT, 6])
        ln_mv = sb("ln_mv", [P, QT, 2])
        ln_a, ln_b = (sb(n, [P, QT]) for n in ("ln_a", "ln_b"))
        ln_rstd = sb("ln_rstd", [P, QT])
        ln_mean = sb("ln_mean", [P, QT])
        q_amax, q_rstep = (sb(n, [P, H]) for n in ("q_amax", "q_rstep"))
        q_quantum = scratch[:, :].rearrange("p (t h) -> p t h", t=QT)
        q_step = sb("q_step", [P, QT, 2, H])
        q_step_now = sb("q_step_now", [P, 2, H])
        ln255 = sb("ln255", [P, 1])
        s_part = sb("s_part", [P, 2, 3])
        s_max = sb("s_max", [P, 2])
        exp_bias = sb("exp_bias", [P, 2])
        p_part = sb("p_part", [P, H, 2])
        p_sum = sb("p_sum", [P, HQ])
        p_rsum = sb("p_rsum", [P, HQ])
        ln1_stats = sb("ln1_stats", [P, 2, 6])
        ln1_mv = sb("ln1_mv", [P, 2])
        ln1_var, ln1_y, ln1_t = (sb(n, [P, 1]) for n in ("ln1_var", "ln1_y", "ln1_t"))
        g_inh, g_dist, g_w, g_zone, g_fb, g_tmp, g_rank = (
            sb(n, [P, QT, E]) for n in ("g_inh", "g_dist", "g_w", "g_zone", "g_fb", "g_tmp", "g_rank"))
        lower_tri = sb("lower_tri", [P, E, E])
        g_sum, g_none, g_has = (sb(n, [P, QT]) for n in ("g_sum", "g_none", "g_has"))
        g_count = sb("g_count", [P, E])
        n_max = sb("n_max", [P, 1], I32)
        ones = sb("ones", [P, P], BF16)
        earlier = sb("earlier", [P, P], BF16)
        slot_row = sb("slot_row", [P, HALF], F16)
        token = sb("token", [P, 3, QT], I32)
        slot_now = sb("slot_now", [P, QT])
        slot_tok_f = sb("slot_tok_f", [P, DK])
        slot_tok = [sb(f"slot_tok{c}", [P, DK], I32) for c in range(2)]
        slot_w = [sb(f"slot_w{c}", [P, DK]) for c in range(2)]

        psum = ctx.enter_context(nc.psum_tensor("psum", [P, 8, 512], F32))

        def bank(b):
            return psum[:, b, :]

        ctx_in, small_in, wq_in, wp_in = (sem(n) for n in ("ctx_in", "small_in", "wq_in", "wp_in"))
        x_in = [sem(f"x_in{n}") for n in range(2)]
        wkv_in = [sem(f"wkv_in{n}") for n in range(2)]
        dve_step, act_step, pool_step = sem("dve_step"), sem("act_step"), sem("pool_step")
        dve_passed, pe_passed, act_passed = sem("dve_passed"), sem("pe_passed"), sem("act_passed")
        const_ready = sem("const_ready")
        wkv_hi, wkv_ready, ctx_hi, ctx_cut = (sem(n) for n in ("wkv_hi", "wkv_ready", "ctx_hi", "ctx_cut"))
        ctxT_in = [sem(f"ctxT_in{t}") for t in range(DK)]
        bias_in, bias_cut, bias_ready = sem("bias_in"), sem("bias_cut"), sem("bias_ready")
        k_full, k_deq_ready, k_hi = sem("k_full"), sem("k_deq_ready"), sem("k_hi")
        k_out, k_cut_ready, kT_in = ([sem(f"{n}{b}") for b in range(2)] for n in ("k_out", "k_cut_ready", "kT_in"))
        v_full, v_max_done, v_scaled, v_rounded, v_halved, vT_in = (
            sem(n) for n in ("v_full", "v_max_done", "v_scaled", "v_rounded", "v_halved", "vT_in"))
        v_out = [sem(f"v_out{b}") for b in range(2)]
        ln_summed, ln_ready, x_norm_ready, x_hi, x_cut, xT_in, x_biased = (
            sem(n) for n in ("ln_summed", "ln_ready", "x_norm_ready", "x_hi", "x_cut", "xT_in", "x_biased"))
        wq_hi, wq_ready, wp_hi, wp_ready = (
            sem(n) for n in ("wq_hi", "wq_ready", "wp_hi", "wp_ready"))
        q_full = sem("q_full")
        q_out, q_cut_ready, qT_in = ([sem(f"{n}{b}") for b in range(2)] for n in ("q_out", "q_cut_ready", "qT_in"))
        scores_full, max_ready, exp_done = sem("scores_full"), sem("max_ready"), sem("exp_done")
        probs_ready, pv_done = sem("probs_ready"), sem("pv_done")
        probsT_in = [sem(f"probsT_in{b}") for b in range(4)]
        att_ready, att_cut, attT_in = (sem(n) for n in ("att_ready", "att_cut", "attT_in"))
        proj_full, proj_out, x1_added, x1T_in = (sem(n) for n in ("proj_full", "proj_out", "x1_added", "x1T_in"))
        att_hi, x1_normed, x1_hi, x1_cut = sem("att_hi"), sem("x1_normed"), sem("x1_hi"), sem("x1_cut")
        q_now_ready, x1_stats, pool_passed = (sem(n) for n in ("q_now_ready", "x1_stats", "pool_passed"))
        deviation_ready = sem("deviation_ready")
        logits_full = sem("logits_full")
        neg_exp, dist_ready, dist_exp = sem("neg_exp"), sem("dist_ready"), sem("dist_exp")
        tri_ready = sem("tri_ready")
        mask_ready, count_full, n_ready = sem("mask_ready"), sem("count_full"), sem("n_ready")
        w_in = [sem(f"w_in{m}") for m in range(3)]
        w_hi = [sem(f"w_hi{m}") for m in range(3)]
        w_ready = [sem(f"w_ready{m}") for m in range(3)]
        select_ready, list_full, slots_ready = sem("select_ready"), sem("list_full"), sem("slots_ready")
        gathered = [[sem(f"gathered{c}{t}") for t in range(DK)] for c in range(2)]
        selT_in = [sem(f"selT_in{c}") for c in range(2)]
        gate_full, up_full, tanh_ready = sem("gate_full"), sem("up_full"), sem("tanh_ready")
        hidden_ready = [sem(f"hidden_ready{b}") for b in range(2)]
        hid_hi, hid_cut, down_full = sem("hid_hi"), sem("hid_cut"), sem("down_full")
        y_ready = [sem(f"y_ready{b}") for b in range(2)]
        y_added = [sem(f"y_added{t}") for t in range(DK)]
        rows_stored = sem("rows_stored")
        stored, sp_passed = sem("stored"), sem("sp_passed")

        block = ctx.enter_context(nc.Block())

        @block.sync
        def _(sp):
            def passed():
                sp.sem_inc(sp_passed, 1)

            def load_ctx(g):
                sp.dma_start(ctx_raw, ctx_g[bass.ds(g, 1)].rearrange("a p s d -> (a p) s d")).then_inc(ctx_in, 16)

            load_ctx(0)
            with nc.allow_non_contiguous_dma("small constants"):
                for row in (0, 32):
                    sp.dma_start(bias_raw[row:row + 1, 0, :], A_bkv[0:D].unsqueeze(0)).then_inc(bias_in, 16)
                    sp.dma_start(bias_raw[row:row + 1, 1, :], A_bq.unsqueeze(0)).then_inc(bias_in, 16)
                sp.dma_start(wkv_raw[:, :, 0:D], wkv_v[:, :, 0:D]).then_inc(wkv_in[0], 16)
                sp.dma_start(bv_col[:, :], A_bkv[D:2 * D].rearrange("(m p) -> p m", p=P)).then_inc(small_in, 16)
                sp.dma_start(wkv_raw[:, :, D:2 * D], wkv_v[:, :, D:2 * D]).then_inc(wkv_in[1], 16)

            def transpose_ctx(g):
                for t in range(DK):
                    if t in (0, DK // 2):
                        sp.wait_ge(ctx_cut, 2 * g + t // 2 + 1)
                        passed()
                    sp.dma_start_transpose(ctx_T[:, bass.ds(g, 1), t].rearrange("p a k t -> p (a k) t"),
                                           ctx_hl[:, t].rearrange("p l d -> p (l d)")).then_inc(ctxT_in[t], 16)

            def transpose_keys(i, b):
                sp.wait_ge(k_cut_ready[b], i + 1)
                passed()
                sp.dma_start_transpose(key_parts[:, :, bass.ds(i * 2 * P + b * P, P)], k_cut[b].rearrange("p h r d -> p (h r d)")
                                       ).then_inc(kT_in[b], 16)

            def transpose_x(j):
                sp.wait_ge(x_cut, j + 1)
                passed()
                sp.dma_start_transpose(tok_T[:, :, bass.ds(j * P, P)], x_hl.rearrange("p l d -> p (l d)")).then_inc(xT_in, 16)

            def key_pair(i):
                transpose_keys(i, 0)
                transpose_keys(i, 1)
                transpose_x(i)

            transpose_ctx(0)
            with nc.allow_non_contiguous_dma("small constants"):
                sp.dma_start(bp_all, A_bp.partition_broadcast(P)).then_inc(small_in, 16)
                sp.dma_start(temp[:, :], A_temp.partition_broadcast(P)).then_inc(small_in, 16)
                sp.dma_start(wr_raw[:, :, :], A_wr.rearrange("(c p) e -> p c e", p=P)).then_inc(small_in, 16)
            for n in range(2):
                half = slice(n * QT // 2, (n + 1) * QT // 2)
                sp.dma_start(resid[:, half, :], x_t[:, half, :]).then_inc(x_in[n], 16)
                if n == 0:
                    load_ctx(1)
            sp.dma_start(wp_raw, A_wp.rearrange("(c p) n -> p c n", p=P)).then_inc(wp_in, 16)
            with sp.Fori(0, SG - 2) as g:
                transpose_ctx(g + 1)
                key_pair(2 * g)
                load_ctx(g + 2)
                key_pair(2 * g + 1)
            transpose_ctx(SG - 1)
            for n in range(DK):
                key_pair(2 * SG - DK + n)
                if n == 0:
                    sp.dma_start(wq_raw, A_wq.rearrange("(c p) n -> p c n", p=P)).then_inc(wq_in, 16)
            for b in range(2):
                sp.wait_ge(kT_in[b], 16 * KT // 2)
            sp.wait_ge(xT_in, 16 * QT)
            sp.wait_ge(x_biased, QT)
            with sp.Fori(0, QT // 2) as i:
                for b in range(2):
                    sp.wait_ge(q_cut_ready[b], i + 1)
                    passed()
                    sp.dma_start_transpose(q_int[:, :, bass.ds(i * 2 * P + b * P, P)], q_cut[b].rearrange("p h r d -> p (h r d)")
                                           ).then_inc(qT_in[b], 16)
                sp.wait_ge(v_halved, i + 1)
                passed()
                sp.dma_start_transpose(v_int[:, :, bass.ds(i * P, P)], v_T_int[:, bass.ds(i, 1), :].rearrange("p a k -> p (a k)")
                                       ).then_inc(vT_in, 16)
            sp.wait_ge(vT_in, 16 * DK)

            def load_weights(k, e, matrices=range(3)):
                for m in matrices:
                    sp.wait_ge(w_ready[m], k)
                    passed()
                    src = w_rows[m][bass.ds(e, 1)].rearrange("a p c n -> (a p) c n")
                    sp.dma_start(w_raw[m], src).then_inc(w_in[m], 16)

            def transpose_attention(j):
                sp.wait_ge(att_cut, j + 1)
                passed()
                sp.dma_start_transpose(att_T, att_hl.rearrange("p l d -> p (l d)")).then_inc(attT_in, 16)

            def store_rows(j):
                sp.wait_ge(x1_cut, j + 1)
                passed()
                rows = x1_hl.rearrange("p l d -> p (l d)")
                sp.dma_start_transpose(tok_T[:, :, bass.ds(j * P, P)], rows).then_inc(x1T_in, 16)
                sp.dma_start(x1_rows[bass.ds(j * P, P), :], rows).then_inc(rows_stored, 16)
                sp.dma_start(out_rows[bass.ds(j * P, P), :], x1).then_inc(stored, 16)

            def transpose_tile(i, first, after_rows):
                for h in range(H):
                    u = H * i + h
                    sp.wait_ge(probs_ready, u + 1)
                    passed()
                    if not first or h >= 4:
                        sp.wait_ge(pv_done, u - 3)
                        passed()
                    sp.dma_start_transpose(p_T[h % 4], p_half[h % 4]).then_inc(probsT_in[h % 4], 16)
                    if first and h in (9, 11, 13):
                        sp.wait_ge(v_rounded, DK)
                        load_weights(0, 0, [(h - 9) // 2])
                    if h == 2 and after_rows:
                        store_rows(i - 2)
                    if h == 3 and not first:
                        transpose_attention(i - 1)

            transpose_tile(0, True, False)
            transpose_tile(1, False, False)
            with sp.Fori(2, QT) as i:
                transpose_tile(i, False, True)
            store_rows(QT - 2)
            transpose_attention(QT - 1)
            store_rows(QT - 1)

            def transpose_selected(i, par):
                for t in range(DK):
                    sp.wait_ge(gathered[par][t], 16 * i + 16)
                    if t == 0:
                        sp.wait_ge(up_full, DK * before(2 * i + par, 1))
                    passed()
                    sp.dma_start_transpose(x_sel_T[par][:, t], x_sel[par][:, t, :]).then_inc(selT_in[par], 16)

            def experts(k0):
                i0 = k0 // 2
                if k0:
                    load_weights(k0, 0)
                load_weights(k0 + 1, 1)
                transpose_selected(i0, 0)
                with sp.Fori(0, E // 2 - 1) as i:
                    transpose_selected(i + i0, 1)
                    load_weights(2 * i + 2 + k0, 2 * i + 2)
                    transpose_selected(i + 1 + i0, 0)
                    load_weights(2 * i + 3 + k0, 2 * i + 3)
                transpose_selected(E // 2 - 1 + i0, 1)

            experts(0)
            sp.wait_ge(n_ready, 1)
            with sp.If(sp.value_load(n_max[0:1, 0:1], min_val=0, max_val=T) > HALF):
                experts(E)
            sp.wait_ge(rows_stored, 16 * QT)
            sp.wait_ge(stored, 16 * QT)

        @block.gpsimd
        def _(pool):
            def passed():
                pool.sem_inc(pool_passed, 1)

            own = Steps(pool, pool_step)
            nc.gpsimd.memset(ln255[:, :], LN255).then_inc(const_ready, 1)
            own.mark(nc.gpsimd.memset(bias_one[:, :], 0.0))
            own.link(nc.gpsimd.memset(bias_hl[:, :, :], 0.0))
            for row in (0, 32):
                own.link(nc.gpsimd.memset(bias_one[row:row + 1, :], 1.0))
            pool.sem_inc(const_ready, 2)
            for n in range(HALF // P):
                own.link(nc.gpsimd.iota(scratch[:, :].bitcast(I32), pattern=[[1, P]], base=n * P, channel_multiplier=0))
                own.link(nc.gpsimd.tensor_copy(slot_row[:, n * P:n * P + P], scratch[:, :].bitcast(I32)))
            nc.gpsimd.iota(token[:, 0, :], pattern=[[P, QT]], base=0, channel_multiplier=1).then_inc(tri_ready, 1)
            nc.gpsimd.iota(token[:, 1, :], pattern=[[P, QT]], base=0, channel_multiplier=0).then_inc(tri_ready, 1)
            nc.gpsimd.iota(token[:, 2, :], pattern=[[0, QT]], base=0, channel_multiplier=1).then_inc(tri_ready, 1)
            own.link(nc.gpsimd.memset(scratch[:, :], 1.0))
            own.link(nc.gpsimd.tensor_copy(ones[:, :], scratch[:, :]))
            own.link(nc.gpsimd.affine_select(out=scratch[:, :], in_=scratch[:, :], compare_op=ALU.is_gt, fill=0.0,
                                             base=0, pattern=[[1, P]], channel_multiplier=-1))
            nc.gpsimd.tensor_copy(earlier[:, :], scratch[:, :]).then_inc(tri_ready, 1)
            own.link(nc.gpsimd.memset(lower_tri[:, :, :], 1.0))
            nc.gpsimd.affine_select(out=lower_tri[:, :, :], in_=lower_tri[:, :, :], compare_op=ALU.is_gt, fill=0.0,
                                    base=0, pattern=[[1, E], [-1, E]], channel_multiplier=0).then_inc(tri_ready, 1)

            def rsqrt_steps(own, var, y, t):
                own.link(nc.gpsimd.tensor_scalar(var, var, LN_EPS, None, ALU.add))
                own.link(nc.gpsimd.tensor_scalar(y.bitcast(I32), var.bitcast(I32), -0.5, float(RSQRT_GUESS), ALU.mult, ALU.add))
                for _ in range(3):
                    own.link(nc.gpsimd.tensor_tensor(t, y, y, ALU.mult))
                    own.link(nc.gpsimd.tensor_tensor(t, t, var, ALU.mult))
                    own.link(nc.gpsimd.tensor_scalar(t, t, -0.5, 1.5, ALU.mult, ALU.add))
                    own.link(nc.gpsimd.tensor_tensor(y, y, t, ALU.mult))

            def row(j):
                return resid[:, bass.ds(j, 1), :].rearrange("p a d -> p (a d)")

            def keys_low(j):
                for b in range(2):
                    pool.wait_ge(k_hi, 2 * j + b + 1)
                    nc.gpsimd.tensor_tensor(k_cut[b][:, :, 1, :], k_deq[b], k_cut[b][:, :, 0, :], ALU.subtract
                                            ).then_inc(k_cut_ready[b], 1)

            def x_low(j):
                pool.wait_ge(x_hi, j + 1)
                nc.gpsimd.tensor_tensor(x_hl[:, 1, :], x_norm, x_hl[:, 0, :], ALU.subtract).then_inc(x_cut, 1)
                nc.gpsimd.tensor_tensor(row(j), row(j), bp_all, ALU.add).then_inc(x_biased, 1)

            keys_low(0)
            pool.wait_ge(ln_summed, 1)
            own.mark(nc.gpsimd.tensor_copy(ln_mean[:, :], ln_mv[:, :, 0]))
            own.link(nc.gpsimd.tensor_copy(ln_a[:, :], ln_mv[:, :, 1]))
            rsqrt_steps(own, ln_a[:, :], ln_rstd[:, :], ln_b[:, :])
            pool.sem_inc(ln_ready, 1)

            pool.wait_ge(small_in, 64)
            x_low(0)
            with pool.Fori(1, QT) as j:
                keys_low(j)
                x_low(j)

            def queries_now(i, second):
                pairs = slice(DK * second, DK * second + DK)
                nc.gpsimd.tensor_copy(q_now[:, pairs, :], q_int[:, pairs, bass.ds(i * P, P)]).then_inc(q_now_ready, 1)

            norm_steps = 15

            def attention_lo(j):
                pool.wait_ge(att_hi, j + 1)
                nc.gpsimd.tensor_tensor(att_hl[:, 1, :], att, att_hl[:, 0, :], ALU.subtract).then_inc(att_cut, 1)

            def add_rows(j):
                for half in range(2):
                    columns = slice(256 * half, 256 * half + 256)
                    pool.wait_ge(proj_out, 2 * j + half + 1)
                    passed()
                    nc.gpsimd.tensor_tensor(x1[:, columns], x1[:, columns], row(j)[:, columns], ALU.add).then_inc(x1_added, 1)

            def deviation(j):
                add_rows(j)
                pool.wait_ge(x1_stats, j + 1)
                passed()
                own = Steps(pool, pool_step, norm_base + norm_steps * j, passed)
                own.link(nc.gpsimd.tensor_copy(ln1_var[:, :], ln1_mv[:, 1:2]))
                rsqrt_steps(own, ln1_var[:, :], ln1_y[:, :], ln1_t[:, :])
                assert own.n == norm_steps

            def normalise(j):
                deviation(j)
                nc.gpsimd.tensor_scalar(x1_norm, x1, ln1_mv[:, 0:1], ln1_y[:, :], ALU.subtract, ALU.mult).then_inc(x1_normed, 1)
                pool.wait_ge(x1_hi, j + 1)
                nc.gpsimd.tensor_tensor(x1_hl[:, 1, :], x1_norm, x1_hl[:, 0, :], ALU.subtract).then_inc(x1_cut, 1)

            def next_queries(i, second):
                pool.wait_ge(scores_full, 3 * H * (i - 1) + 3 * (H // 2) * (1 + second))
                passed()
                queries_now(i, second)

            pool.wait_ge(wq_ready, 1)
            pool.wait_ge(qT_in[0], 16)
            queries_now(0, 0)
            queries_now(0, 1)
            own.base, own.n = own.base + own.n, 0
            pool.wait_ge(wp_hi, DK)
            for c in range(DK):
                own.link(nc.gpsimd.tensor_scalar(wp_raw[:, c, :], wp_raw[:, c, :], v_fold[:, c:c + 1], None, ALU.mult))
                nc.gpsimd.tensor_tensor(wp_hl[:, 1, c, :], wp_raw[:, c, :], wp_hl[:, 0, c, :], ALU.subtract).then_inc(wp_ready, 1)
            for b in range(2):
                pool.wait_ge(qT_in[b], 16 * QT // 2)
            next_queries(1, 0)
            norm_base = own.base + own.n
            with pool.Fori(0, QT - 2) as j:
                next_queries(j + 1, 1)
                attention_lo(j)
                next_queries(j + 2, 0)
                normalise(j)
            next_queries(QT - 1, 1)
            attention_lo(QT - 2)
            deviation(QT - 2)
            pool.sem_inc(deviation_ready, 1)

            def gather(i, par):
                k = 2 * i + par
                pool.wait_ge(slots_ready, k + 1)
                pool.wait_ge(selT_in[par], 64 * i)
                passed()
                for t in range(DK):
                    nc.gpsimd.indirect_dma_start(
                        x_sel[par][:, t, :], None, x1_rows, bass.IndirectOffsetOnAxis(ap=slot_tok[par][:, t:t + 1], axis=0)
                    ).then_inc(gathered[par][t], 16)

            def scatter(i, par):
                k = 2 * i + par
                for t in range(DK):
                    pool.wait_ge(y_ready[t % 2], 2 * k + t // 2 + 1)
                    if t == 0:
                        for other in y_added:
                            pool.wait_ge(other, 16 * k)
                    passed()
                    nc.gpsimd.indirect_dma_start(
                        out_rows, bass.IndirectOffsetOnAxis(ap=slot_tok[par][:, t:t + 1], axis=0), y_out[:, t, :], None,
                        compute_op=ALU.add).then_inc(y_added[t], 16)

            def experts(k0):
                i0 = k0 // 2
                gather(i0, 0)
                with pool.Fori(0, E // 2 - 1) as i:
                    gather(i + i0, 1)
                    scatter(i + i0, 0)
                    gather(i + 1 + i0, 0)
                    scatter(i + i0, 1)
                last = E // 2 - 1 + i0
                gather(last, 1)
                scatter(last, 0)
                scatter(last, 1)
                for t in range(DK):
                    pool.wait_ge(y_added[t], 16 * (k0 + E))

            pool.wait_ge(rows_stored, 16 * QT)
            pool.wait_ge(stored, 16 * QT)
            experts(0)
            pool.wait_ge(n_ready, 1)
            with pool.If(pool.value_load(n_max[0:1, 0:1], min_val=0, max_val=T) > HALF):
                experts(E)

        @block.scalar
        def _(act):
            def ctx_high(g):
                act.wait_ge(ctx_in, 16 * g + 16)
                for t in range(DK):
                    act.wait_ge(ctxT_in[t], 16 * g)
                act.sem_inc(act_passed, 1)
                for half in HALVES:
                    nc.scalar.activation(ctx_hl[:, half, 0, :], ctx_raw[:, half, :], ACT.Copy).then_inc(ctx_hi, 1)

            def wkv_high(n):
                act.wait_ge(wkv_in[n], 16)
                part = slice(n * D, (n + 1) * D)
                for half in HALVES:
                    nc.scalar.activation(wkv_hl[:, 0, half, part], wkv_raw[:, half, part], ACT.Copy, scale=WS).then_inc(wkv_hi, 1)

            ctx_high(0)
            act.wait_ge(const_ready, 3)
            act.wait_ge(bias_in, 64)
            nc.scalar.activation(bias_hl[0:1, :, :], bias_raw[0:1, :, :], ACT.Copy, scale=WS).then_inc(bias_cut, 1)
            wkv_high(0)
            nc.scalar.activation(bias_hi[32:33, :, :], bias_raw[32:33, :, :], ACT.Copy, scale=WS).then_inc(bias_cut, 1)
            wkv_high(1)
            act.wait_ge(small_in, 64)

            def key_group(g, following):
                for t in range(DK):
                    b = t % 2
                    act.wait_ge(k_deq_ready, 4 * g + t + 1)
                    act.wait_ge(kT_in[b], 32 * g + 16 * (t // 2))
                    nc.scalar.activation(k_cut[b][:, :, 0, :], k_deq[b], ACT.Copy).then_inc(k_hi, 1)
                    act.wait_ge(v_full, 4 * g + t + 1)
                    nc.scalar.activation(v_T[:, t, bass.ds(g * 512, 512)], bank(2 + b), ACT.Identity,
                                         bias=bv_col[:, t:t + 1], scale=1.0 / WS).then_inc(v_out[b], 1)
                    if b:
                        j = 2 * g + t // 2
                        act.wait_ge(x_norm_ready, j + 1)
                        act.wait_ge(xT_in, 16 * j)
                        nc.scalar.activation(x_hl[:, 0, :], x_norm, ACT.Copy).then_inc(x_hi, 1)
                    if t == 0 and following:
                        ctx_high(g + 1)

            with act.Fori(0, SG - 1) as g:
                key_group(g, True)
            act.wait_ge(wq_in, 16)
            nc.scalar.activation(wq_hl[:, 0], wq_raw, ACT.Copy, scale=WS).then_inc(wq_hi, 1)
            key_group(SG - 1, False)

            act.wait_ge(v_scaled, 2)
            act.wait_ge(wp_in, 16)
            with act.Fori(0, QT // 2) as i:
                nc.scalar.activation(v_i16[:, bass.ds(i, 1), :].rearrange("p a k -> p (a k)"),
                                     v_T[:, bass.ds(i, 1), :].rearrange("p a k -> p (a k)"), ACT.Copy,
                                     scale=v_rstep[:, bass.ds(i, 1)]).then_inc(v_rounded, 1)
                nc.scalar.activation(wp_hl[:, 0, bass.ds(i, 1), :].rearrange("p a n -> p (a n)"),
                                     wp_raw[:, bass.ds(i, 1), :].rearrange("p a n -> p (a n)"), ACT.Copy,
                                     scale=v_fold[:, bass.ds(i, 1)]).then_inc(wp_hi, 1)
                for b in range(2):
                    act.wait_ge(q_out[b], i + 1)
                    act.wait_ge(qT_in[b], 16 * i)
                    nc.scalar.activation(q_cut[b], q_i16[b].unsqueeze(2).to_broadcast([P, H, 2, HD]), ACT.Copy
                                         ).then_inc(q_cut_ready[b], 1)

            def cut_weights(k, par, m):
                act.wait_ge(w_in[m], 16 * k + 16)
                nc.scalar.activation(w_hl[par][m][:, 0], w_raw[m], ACT.Copy, scale=WS).then_inc(w_hi[m], 1)

            def cut_attention(j):
                act.wait_ge(att_ready, 2 * j + 2)
                nc.scalar.activation(att_hl[:, 0, :], att, ACT.Copy).then_inc(att_hi, 1)

            def cut_rows(j):
                act.wait_ge(x1_normed, j + 1)
                act.wait_ge(x1T_in, 16 * j)
                act.wait_ge(rows_stored, 16 * j)
                nc.scalar.activation(x1_hl[:, 0, :], x1_norm, ACT.Copy).then_inc(x1_hi, 1)

            def take_projection(j, half):
                if half == 0:
                    act.wait_ge(stored, 16 * j)
                act.wait_ge(proj_full, 2 * j + half + 1)
                nc.scalar.activation(x1[:, 256 * half:256 * half + 256], bank(7)[:, 256:512], ACT.Copy, scale=1.0 / PS).then_inc(proj_out, 1)

            def attention_tile(i, first, after_rows):
                for h in range(H):
                    u = H * i + h
                    act.wait_ge(max_ready, u + 1)
                    nc.scalar.activation(exp_bias[:, h % 2:h % 2 + 1], s_max[:, h % 2:h % 2 + 1], ACT.Identity,
                                         bias=ln255[:, :], scale=q_step_now[:, 1, h:h + 1]).then_inc(act_step, 1)
                    act.wait_ge(act_step, u + 1)
                    if not first or h >= 2:
                        act.wait_ge(probs_ready, u - 1)
                    for part, (b, n, at) in enumerate(((6, 1, 1536), (3 * (h % 2), 3, 0))):
                        nc.scalar.activation(
                            p_int[h % 2][:, at:at + n * 512].rearrange("p (b k) -> p b k", b=n),
                            psum[:, b:b + n, :], ACT.Exp, bias=exp_bias[:, h % 2:h % 2 + 1],
                            scale=q_step_now[:, 0, h:h + 1], accum_out=p_part[:, h, part:part + 1]).then_inc(exp_done, 1)
                    if h == 1 and after_rows:
                        cut_rows(i - 2)
                    if h == 3 and not first:
                        cut_attention(i - 1)
                    if h in (8, 12) and not first:
                        take_projection(i - 1, h // 12)

            attention_tile(0, True, False)
            attention_tile(1, False, False)
            with act.Fori(2, QT) as i:
                attention_tile(i, False, True)
            cut_weights(0, 0, 0)
            cut_rows(QT - 2)
            cut_attention(QT - 1)
            cut_weights(0, 0, 1)
            for b in range(4):
                act.wait_ge(probsT_in[b], 16 * H // 4 * QT)
            cut_weights(0, 0, 2)
            cut_rows(QT - 1)

            act.wait_ge(logits_full, 1)
            nc.scalar.activation(g_inh[:, :, :], bank(2)[:, 0:QT * E].rearrange("p (t e) -> p t e", t=QT), ACT.Exp,
                                 scale=r_temp[:, 0:1]).then_inc(neg_exp, 1)
            act.wait_ge(dist_ready, 1)
            nc.scalar.activation(g_fb[:, :, :], g_dist[:, :, :], ACT.Exp, scale=-1.0 / 0.3).then_inc(dist_exp, 1)
            nc.scalar.activation(g_w[:, :, :], g_dist[:, :, :], ACT.Exp, scale=-1.0 / 0.1).then_inc(dist_exp, 1)

            def expert(i, par, following):
                k = 2 * i + par

                def hidden_hi(f):
                    act.wait_ge(hidden_ready[f % 2], 2 * k + f // 2 + 1)
                    nc.scalar.activation(hid_T[par][:, 0, f, :], hidden[f % 2], ACT.Copy).then_inc(hid_hi, 1)

                for f in range(DK):
                    if f:
                        hidden_hi(f - 1)
                    act.wait_ge(gate_full, DK * k + f + 1)
                    act.wait_ge(hidden_ready[f % 2], 2 * k + f // 2)
                    nc.scalar.activation(tanh_g[f % 2], bank(f % 2), ACT.Tanh, scale=0.5 / WS).then_inc(tanh_ready, 1)
                    if following and f in (1, 2):
                        cut_weights(k + 1, 1 - par, f - 1)
                hidden_hi(DK - 1)
                if following:
                    cut_weights(k + 1, 1 - par, 2)
                act.wait_ge(slots_ready, k + 1)
                for t in range(DK):
                    act.wait_ge(down_full, DK * k + t + 1)
                    act.wait_ge(y_added[t], 16 * k)
                    nc.scalar.activation(y_out[:, t, :], bank(4 + t % 3), ACT.Copy, scale=slot_w[par][:, t:t + 1]
                                         ).then_inc(y_ready[t % 2], 1)

            def experts(k0):
                i0 = k0 // 2
                if k0:
                    for m in range(3):
                        cut_weights(k0, 0, m)
                with act.Fori(0, E // 2 - 1) as i:
                    expert(i + i0, 0, True)
                    expert(i + i0, 1, True)
                expert(E // 2 - 1 + i0, 0, True)
                expert(E // 2 - 1 + i0, 1, False)

            experts(0)
            act.wait_ge(n_ready, 1)
            with act.If(act.value_load(n_max[0:1, 0:1], min_val=0, max_val=T) > HALF):
                experts(E)

        @block.vector
        def _(dve):
            own = Steps(dve, dve_step)
            def heads(v):
                return v.rearrange("p (h d) -> p h d", h=H)

            def each(v):
                return v.unsqueeze(2).to_broadcast([P, H, HD])

            def ctx_low(g):
                for n, half in enumerate(HALVES):
                    dve.wait_ge(ctx_hi, 2 * g + n + 1)
                    dve.sem_inc(dve_passed, 1)
                    nc.vector.tensor_tensor(ctx_hl[:, half, 1, :], ctx_raw[:, half, :], ctx_hl[:, half, 0, :], ALU.subtract
                                            ).then_inc(ctx_cut, 1)

            def wkv_low(n):
                part = slice(n * D, (n + 1) * D)
                for m, half in enumerate(HALVES):
                    dve.wait_ge(wkv_hi, 2 * n + m + 1)
                    nc.vector.scalar_tensor_tensor(wkv_hl[:, 1, half, part], wkv_raw[:, half, part], WS, wkv_hl[:, 0, half, part],
                                                   ALU.mult, ALU.subtract).then_inc(wkv_ready, 1)

            ctx_low(0)
            wkv_low(0)
            dve.wait_ge(bias_cut, 2)
            nc.vector.scalar_tensor_tensor(bias_hl[32:33, :, :], bias_raw[32:33, :, :], WS, bias_hi[32:33, :, :],
                                           ALU.mult, ALU.subtract).then_inc(bias_ready, 1)
            wkv_low(1)
            key_steps = 3

            def keys(g, t, own):
                b = t % 2
                dve.wait_ge(k_full, 4 * g + t + 1)
                own.link(nc.vector.tensor_reduce(k_amax[:, :], heads(bank(b)), AX.X, ALU.max, apply_absolute_value=True))
                own.link(nc.vector.tensor_scalar(k_step[:, :], k_amax[:, :], 1.0 / 127.0, WS * 1e-8, ALU.mult, ALU.max))
                own.link(nc.vector.reciprocal(k_rstep[:, :], k_step[:, :]))
                nc.vector.tensor_tensor(k_int[b], heads(bank(b)), each(k_rstep[:, :]), ALU.mult).then_inc(k_out[b], 1)
                dve.wait_ge(k_out[b], 2 * g + t // 2 + 1)
                dve.wait_ge(k_cut_ready[b], 2 * g + t // 2)
                nc.vector.tensor_tensor(k_deq[b], k_int[b], each(k_step[:, :]), ALU.mult).then_inc(k_deq_ready, 1)
                dve.wait_ge(k_deq_ready, 4 * g + t + 1)

            def normalise_x(j):
                row = resid[:, bass.ds(j, 1), :].rearrange("p a d -> p (a d)")
                dve.wait_ge(ln_ready, 1)
                dve.wait_ge(x_cut, j)
                dve.sem_inc(dve_passed, 1)
                nc.vector.tensor_scalar(x_norm, row, ln_mean[:, bass.ds(j, 1)], ln_rstd[:, bass.ds(j, 1)],
                                        ALU.subtract, ALU.mult).then_inc(x_norm_ready, 1)

            def x_statistics(n, own):
                dve.wait_ge(x_in[n], 16)
                for t in range(n * QT // 2, (n + 1) * QT // 2):
                    own.mark(nc.vector.bn_stats(ln_stats[:, t, :], resid[:, t, :]))
                if n == 1:
                    dve.wait_ge(dve_step, own.base + own.n)
                    for t in range(QT):
                        ins = nc.vector.bn_aggr(ln_mv[:, t, :], ln_stats[:, t, :])
                    ins.then_inc(ln_summed, 1)

            def key_group(g, base, following, first=False):
                own = Steps(dve, dve_step, base)
                for t in range(DK):
                    keys(g, t, own)
                    if following and t == 1:
                        ctx_low(g + 1)
                    if first and t < 2:
                        x_statistics(t, own)
                    if t == (2 if first else 1):
                        normalise_x(2 * g)
                    if t == 3:
                        normalise_x(2 * g + 1)
                for b in range(2):
                    dve.wait_ge(v_out[b], 2 * g + 2)
                dve.sem_inc(v_max_done, 1)
                nc.vector.tensor_reduce(v_part[:, :, bass.ds(g, 1)].rearrange("p m a -> p (m a)"),
                                        v_T[:, :, bass.ds(g * 512, 512)], AX.X, ALU.max, apply_absolute_value=True
                                        ).then_inc(v_max_done, 1)
                return own.n

            head = key_group(0, own.n, True, True) - key_steps * DK
            with dve.Fori(1, SG - 1) as g:
                assert key_group(g, head + key_steps * DK * g, True) == key_steps * DK
            dve.wait_ge(wq_hi, 1)
            nc.vector.scalar_tensor_tensor(wq_hl[:, 1], wq_raw, WS, wq_hl[:, 0], ALU.mult, ALU.subtract).then_inc(wq_ready, 1)
            key_group(SG - 1, head + key_steps * DK * (SG - 1), False)
            own = Steps(dve, dve_step, head + key_steps * DK * SG)
            dve.wait_ge(v_max_done, 2 * SG)
            own.link(nc.vector.tensor_reduce(v_amax[:, :], v_part[:, :, :], AX.X, ALU.max))
            own.link(nc.vector.tensor_scalar(v_step[:, :], v_amax[:, :], 1.0 / 127.0, 1e-8, ALU.mult, ALU.max))
            nc.vector.reciprocal(v_rstep[:, :], v_step[:, :]).then_inc(v_scaled, 1)
            nc.vector.tensor_scalar(v_fold[:, :], v_step[:, :], PS, None, ALU.mult).then_inc(v_scaled, 1)
            dve.wait_ge(small_in, 64)
            own.link(nc.vector.tensor_scalar(wr_hl[:, 0], wr_raw[:, :, :], WS, None, ALU.mult))
            own.mark(nc.vector.scalar_tensor_tensor(wr_hl[:, 1], wr_raw[:, :, :], WS, wr_hl[:, 0], ALU.mult, ALU.subtract))
            own.link(nc.vector.reciprocal(r_temp[:, :], temp[:, :]))
            own.mark(nc.vector.tensor_scalar(r_temp[:, :], r_temp[:, :], -1.0 / WS, None, ALU.mult))

            q_scale = float(1.0 / np.sqrt(np.float32(HD)))
            query_steps = 3
            head = own.base + own.n
            dve.wait_ge(tri_ready, 5)
            def query_pair(i, i2):
                own = Steps(dve, dve_step, head + 2 * query_steps * i)
                for b in range(2):
                    q_bank = bank(Q_BANKS[2 * i2 + b])
                    quantum = q_quantum[:, bass.ds(2 * i + b, 1), :].rearrange("p a h -> p (a h)")
                    dve.wait_ge(q_full, 2 * i + b + 1)
                    own.link(nc.vector.tensor_reduce(q_amax[:, :], heads(q_bank), AX.X, ALU.max, apply_absolute_value=True))
                    own.link(nc.vector.tensor_scalar(quantum, q_amax[:, :], q_scale / WS / 127.0, 1e-8, ALU.mult, ALU.max))
                    dve.sem_inc(dve_passed, 1)
                    own.link(nc.vector.reciprocal(q_rstep[:, :], quantum))
                    dve.wait_ge(q_cut_ready[b], i)
                    nc.vector.scalar_tensor_tensor(q_i16[b], heads(q_bank), q_scale / WS, each(q_rstep[:, :]),
                                                   ALU.mult, ALU.mult).then_inc(q_out[b], 1)
                    dve.wait_ge(q_out[b], i + 1)
                assert own.n == 2 * query_steps
                dve.wait_ge(v_rounded, i + 1)
                dve.sem_inc(dve_passed, 1)
                nc.vector.tensor_copy(v_T_int[:, bass.ds(i, 1), :].rearrange("p a k -> p (a k)"),
                                      v_i16[:, bass.ds(i, 1), :].rearrange("p a k -> p (a k)")).then_inc(v_halved, 1)

            with dve.Fori(0, QT // 4) as i:
                query_pair(2 * i, 0)
                query_pair(2 * i + 1, 1)
            own = Steps(dve, dve_step, head + query_steps * QT)
            for n, sign in enumerate((1.0, -1.0)):
                own.mark(nc.vector.tensor_scalar(q_step[:, :, n, :], q_quantum[:, :, :], sign / WS, None, ALU.mult))
            dve.wait_ge(dve_step, own.base + own.n)
            base = own.base + own.n

            def convert(i, h):
                dve.wait_ge(exp_done, 2 * H * i + 2 * h + 2)
                nc.vector.tensor_copy(p_half[h % 4], p_int[h % 2]).then_inc(probs_ready, 1)

            def add_sums(n, own):
                these = slice(HQ * n, HQ * n + HQ)
                own.mark(nc.vector.tensor_tensor(p_sum[:, :], p_part[:, these, 0], p_part[:, these, 1], ALU.add))

            def invert_sums(own):
                dve.wait_ge(dve_step, own.base + own.n - 1)
                own.mark(nc.vector.reciprocal(p_rsum[:, :], p_sum[:, :]))

            def divide(i, n, own):
                dve.wait_ge(dve_step, own.base + own.n)
                dve.wait_ge(pv_done, H * i + HQ * n + HQ)
                if n == 0:
                    dve.wait_ge(att_cut, i)
                these = slice(HQ * n, HQ * n + HQ)
                nc.vector.tensor_tensor(heads(att)[:, these, :], bank(7)[:, 0:HQ * HD].rearrange("p (h d) -> p h d", h=HQ),
                                        p_rsum[:, :].unsqueeze(2).to_broadcast([P, HQ, HD]), ALU.mult).then_inc(att_ready, 1)

            def add_projection(j, half, source):
                columns = slice(256 * half, 256 * half + 256)
                dve.wait_ge(proj_full, 2 * j + half + 1)
                nc.vector.scalar_tensor_tensor(x1[:, columns], source, 1.0 / PS, resid[:, bass.ds(j, 1), columns].rearrange("p a d -> p (a d)"),
                                               ALU.mult, ALU.add).then_inc(x1_added, 1)

            def half_statistics(j, half, own):
                dve.wait_ge(x1_added, 2 * j + half + 1)
                own.mark(nc.vector.bn_stats(ln1_stats[:, half, :], x1[:, 256 * half:256 * half + 256]))

            def mean_and_variance():
                nc.vector.bn_aggr(ln1_mv[:, :], ln1_stats[:, :, :].rearrange("p n s -> p (n s)")).then_inc(x1_stats, 1)

            def cut_weights(k, par, m):
                dve.wait_ge(w_hi[m], k + 1)
                nc.vector.scalar_tensor_tensor(w_hl[par][m][:, 1], w_raw[m], WS, w_hl[par][m][:, 0],
                                               ALU.mult, ALU.subtract).then_inc(w_ready[m], 1)

            def attention_tile(i, base, first):
                own = Steps(dve, dve_step, base)
                for h in range(H):
                    u = H * i + h
                    if h == 4 and first:
                        dve.wait_ge(wp_ready, DK)
                    if h >= 2:
                        convert(i, h - 2)
                    elif not first:
                        convert(i - 1, H + h - 2)
                    if h == 4 and not first:
                        divide(i - 1, 1, own)
                    if h == 12:
                        divide(i, 0, own)
                    if h in (11, 15) and not first:
                        half_statistics(i - 1, h // 15, own)
                        statistics = own.n
                    first_bank = 3 * (h % 2)
                    dve.wait_ge(scores_full, 3 * H * i + 3 * h + 1)
                    nc.vector.tensor_reduce(s_part[:, h % 2, 0:1], bank(first_bank), AX.X, ALU.max)
                    dve.wait_ge(scores_full, 3 * H * i + 3 * h + 2)
                    nc.vector.tensor_reduce(s_part[:, h % 2, 1:2], psum[:, first_bank + 1:first_bank + 3, :], AX.XY, ALU.max)
                    dve.wait_ge(scores_full, 3 * H * i + 3 * h + 3)
                    own.mark(nc.vector.tensor_reduce(s_part[:, h % 2, 2:3], bank(6), AX.X, ALU.max))
                    parts = own.n
                    if h in (0, 4):
                        half = slice(2 * h, 2 * h + H // 2)
                        own.mark(nc.vector.tensor_copy(
                            q_step_now[:, :, half], q_step[:, bass.ds(i, 1), :, half].rearrange("p a n h -> p (a n) h")))
                    if h == 10 or h == 2 and not first:
                        add_sums(h // 10 ^ 1, own)
                    if h == 11 or h == 3 and not first:
                        invert_sums(own)
                    dve.wait_ge(dve_step, own.base + parts)
                    nc.vector.tensor_reduce(s_max[:, h % 2:h % 2 + 1], s_part[:, h % 2, :], AX.X, ALU.max).then_inc(max_ready, 1)
                    if h == 15 and not first:
                        own.after(statistics)
                        dve.sem_inc(dve_passed, 1)
                        mean_and_variance()
                return own.n

            base += attention_tile(0, base, True)
            per_tile = H + 2 + 4 + 2
            with dve.Fori(1, QT) as i:
                assert attention_tile(i, base + per_tile * (i - 1), False) == per_tile
            base += per_tile * (QT - 1)

            own = Steps(dve, dve_step, base)
            convert(QT - 1, H - 2)
            dve.wait_ge(probsT_in[(H - 5) % 4], 64 * (QT - 1) + 16 * ((H - 5) // 4 + 1))
            convert(QT - 1, H - 1)
            add_sums(1, own)
            own.after(own.n)
            own.mark(nc.vector.reciprocal(p_rsum[:, :], p_sum[:, :]))

            def rows_low(j):
                dve.wait_ge(x1_hi, j + 1)
                nc.vector.tensor_tensor(x1_hl[:, 1, :], x1_norm, x1_hl[:, 0, :], ALU.subtract).then_inc(x1_cut, 1)

            dve.wait_ge(deviation_ready, 1)
            nc.vector.tensor_scalar(x1_norm, x1, ln1_mv[:, 0:1], ln1_y[:, :], ALU.subtract, ALU.mult).then_inc(x1_normed, 1)
            rows_low(QT - 2)
            divide(QT - 1, 1, own)
            dve.wait_ge(att_hi, QT)
            nc.vector.tensor_tensor(att_hl[:, 1, :], att, att_hl[:, 0, :], ALU.subtract).then_inc(att_cut, 1)
            for m in range(2):
                cut_weights(0, 0, m)
            dve.wait_ge(stored, 16 * (QT - 1))
            for half in range(2):
                add_projection(QT - 1, half, bank(half)[:, 0:256])
                half_statistics(QT - 1, half, own)
            own.after(own.n)
            mean_and_variance()
            dve.wait_ge(x1_stats, QT)
            mean, var, y, t = ln1_mv[:, 0:1], ln_a[:, 0:1], ln_rstd[:, 0:1], ln_b[:, 0:1]
            own.link(nc.vector.tensor_scalar(var, ln1_mv[:, 1:2], LN_EPS, None, ALU.add))
            own.link(nc.vector.tensor_scalar(y.bitcast(I32), var.bitcast(I32), -0.5, float(RSQRT_GUESS), ALU.mult, ALU.add))
            scale = 1.0
            for _ in range(3):
                own.link(nc.vector.scalar_tensor_tensor(t, y, var, y, ALU.mult, ALU.mult))
                own.link(nc.vector.scalar_tensor_tensor(y, t, 3.0 * scale ** 2, y, ALU.subtract, ALU.mult))
                scale = -2.0 * scale ** 3
            own.link(nc.vector.tensor_scalar(y, y, 1.0 / scale, None, ALU.mult))
            nc.vector.tensor_scalar(x1_norm, x1, mean, y, ALU.subtract, ALU.mult).then_inc(x1_normed, 1)
            rows_low(QT - 1)
            cut_weights(0, 0, 2)

            def tokens(v):
                return v.unsqueeze(2).to_broadcast([P, QT, E])

            dve.wait_ge(neg_exp, 1)
            own.link(nc.vector.tensor_scalar(g_inh[:, :, :], g_inh[:, :, :], 1.0, None, ALU.add))
            own.link(nc.vector.reciprocal(g_inh[:, :, :], g_inh[:, :, :]))
            own.link(nc.vector.tensor_scalar(g_tmp[:, :, :], g_inh[:, :, :], GOLDEN_CENTER, None, ALU.subtract))
            nc.vector.scalar_tensor_tensor(g_dist[:, :, :], g_tmp[:, :, :], -1.0, g_tmp[:, :, :], ALU.mult, ALU.max).then_inc(dist_ready, 1)
            own.link(nc.vector.tensor_scalar(g_zone[:, :, :], g_inh[:, :, :], GOLDEN_UPPER, None, ALU.is_le))
            zone = own.mark(nc.vector.scalar_tensor_tensor(g_zone[:, :, :], g_inh[:, :, :], GOLDEN_LOWER, g_zone[:, :, :],
                                                           ALU.is_ge, ALU.mult))
            mine = g_fb[:, :, :].unsqueeze(3).to_broadcast([P, QT, E, E])
            others = g_fb[:, :, :].unsqueeze(2).to_broadcast([P, QT, E, E])
            dve.wait_ge(tri_ready, 5)
            dve.wait_ge(dist_exp, 1)
            own.mark(nc.vector.tensor_tensor(g_gt, others, mine, ALU.is_gt))
            equal = own.mark(nc.vector.tensor_tensor(g_eq, others, mine, ALU.is_equal))
            dve.wait_ge(dist_exp, 2)
            own.after(zone)
            in_zone = own.mark(nc.vector.tensor_tensor(g_w[:, :, :], g_w[:, :, :], g_zone[:, :, :], ALU.mult))
            own.after(equal)
            earlier_equal = own.mark(nc.vector.tensor_tensor(
                g_eq, g_eq, lower_tri[:, :, :].unsqueeze(1).to_broadcast([P, QT, E, E]), ALU.mult))
            own.after(in_zone)
            zone_sum = own.mark(nc.vector.tensor_reduce(g_sum[:, :], g_w[:, :, :], AX.X, ALU.add))
            own.after(earlier_equal)
            ahead = own.mark(nc.vector.tensor_tensor(g_gt, g_gt, g_eq, ALU.add))
            own.after(zone_sum)
            own.mark(nc.vector.tensor_scalar(g_none[:, :], g_sum[:, :], 1e-8, None, ALU.is_lt))
            has = own.mark(nc.vector.tensor_scalar(g_has[:, :], g_sum[:, :], 1e-8, None, ALU.is_ge))
            own.after(ahead)
            rank = own.mark(nc.vector.tensor_reduce(g_rank[:, :, :], g_gt, AX.X, ALU.add))
            own.after(has)
            own.mark(nc.vector.tensor_tensor(g_w[:, :, :], g_w[:, :, :], tokens(g_has[:, :]), ALU.mult))
            own.after(rank)
            own.link(nc.vector.scalar_tensor_tensor(g_fb[:, :, :], g_rank[:, :, :], 2.0, g_fb[:, :, :], ALU.is_lt, ALU.mult))
            own.link(nc.vector.tensor_tensor(g_fb[:, :, :], g_fb[:, :, :], tokens(g_none[:, :]), ALU.mult))
            own.link(nc.vector.tensor_tensor(g_w[:, :, :], g_w[:, :, :], g_fb[:, :, :], ALU.add))
            own.link(nc.vector.tensor_reduce(g_sum[:, :], g_w[:, :, :], AX.X, ALU.add))
            own.link(nc.vector.tensor_scalar(g_sum[:, :], g_sum[:, :], 1e-8, None, ALU.max))
            own.link(nc.vector.reciprocal(g_sum[:, :], g_sum[:, :]))
            own.link(nc.vector.scalar_tensor_tensor(g_w[:, :, :], g_w[:, :, :], 1.0 / WS, tokens(g_sum[:, :]), ALU.mult, ALU.mult))

            nc.vector.memset(masks[:, QT * E:QT * E + E], 0.0)
            nc.vector.tensor_scalar(mask, g_w[:, :, :], 0.0, None, ALU.not_equal).then_inc(mask_ready, 1)
            own.mark(nc.vector.tensor_copy(tok_w[:, :, :, 0], tokens(token[:, 1, :])))
            own.mark(nc.vector.tensor_copy(tok_w[:, :, :, 1], tokens(token[:, 2, :])))
            own.link(nc.vector.tensor_copy(tok_w[:, :, :, 2], g_w[:, :, :]))
            own.link(nc.vector.tensor_tensor(g_tmp[:, :, :], g_w[:, :, :], tok_w[:, :, :, 2], ALU.subtract))
            own.link(nc.vector.tensor_copy(tok_w[:, :, :, 3], g_tmp[:, :, :]))
            own.mark(nc.vector.tensor_tensor(tok_w[:, :, :, 4], g_tmp[:, :, :], tok_w[:, :, :, 3], ALU.subtract))
            dve.wait_ge(count_full, 1)
            place = bank(1)[:, 0:QT * E].rearrange("p (t e) -> p t e", t=QT)
            own.mark(nc.vector.tensor_copy(g_count[:, :], bank(1)[:, QT * E:QT * E + E]))
            nc.vector.tensor_reduce(n_max[:, :], bank(1)[:, QT * E:QT * E + E], AX.X, ALU.max).then_inc(n_ready, 1)
            own.link(nc.vector.tensor_tensor(g_rank[:, :, :], place, tokens(token[:, 0, :]), ALU.subtract))
            own.link(nc.vector.tensor_tensor(slot, g_count[:, :].unsqueeze(1).to_broadcast([P, QT, E]), g_rank[:, :, :],
                                             ALU.subtract))
            own.link(nc.vector.copy_predicated(slot, mask.bitcast(I16), place))

            def select_tokens(own, e, first_slot):
                own.link(nc.vector.tensor_scalar(slot_now[:, :], slot[:, :, bass.ds(e, 1)].rearrange("p t a -> p (t a)"),
                                                 float(-first_slot), None, ALU.add))
                for t in range(QT):
                    ins = nc.vector.tensor_scalar(select[:, t, :], slot_row[:, :], slot_now[:, t:t + 1], None, ALU.is_equal)
                ins.then_inc(select_ready, 1)

            def slots(own, i, par):
                k = 2 * i + par
                dve.wait_ge(list_full, k + 1)
                dve.wait_ge(y_added[DK - 1], 16 * before(k, 1))
                parts = bank(7)[:, 0:5 * DK].rearrange("p (s c) -> p s c", c=5)
                own.link(nc.vector.tensor_reduce(slot_tok_f[:, :], parts[:, :, 0:2], AX.X, ALU.add))
                own.mark(nc.vector.tensor_copy(slot_tok[par][:, :], slot_tok_f[:, :]))
                nc.vector.tensor_reduce(slot_w[par][:, :], parts[:, :, 2:5], AX.X, ALU.add).then_inc(slots_ready, 1)

            def expert(i, par, base, e, first_slot, following):
                own = Steps(dve, dve_step, base)
                k = 2 * i + par
                after = (i, 1) if par == 0 else (i + 1, 0)

                def hidden_lo(f):
                    dve.wait_ge(hid_hi, DK * k + f + 1)
                    nc.vector.tensor_tensor(hid_T[par][:, 1, f, :], hidden[f % 2], hid_T[par][:, 0, f, :], ALU.subtract
                                            ).then_inc(hid_cut, 1)

                for f in range(DK):
                    if f:
                        hidden_lo(f - 1)
                    dve.wait_ge(tanh_ready, DK * k + f + 1)
                    own.link(nc.vector.scalar_tensor_tensor(gate_1[f % 2], tanh_g[f % 2], 1.0, bank(f % 2), ALU.add, ALU.mult))
                    dve.wait_ge(up_full, DK * k + f + 1)
                    dve.wait_ge(hid_cut, DK * k + max(f - 1, 0))
                    nc.vector.scalar_tensor_tensor(hidden[f % 2], gate_1[f % 2], 0.5 / (WS * WS), bank(2 + f % 2), ALU.mult, ALU.mult
                                                   ).then_inc(hidden_ready[f % 2], 1)
                    if following and f == 0:
                        select_tokens(own, e + 1, first_slot)
                    if following and f in (1, 2):
                        cut_weights(k + 1, 1 - par, f - 1)
                    if following and f == 2:
                        slots(own, *after)
                hidden_lo(DK - 1)
                if following:
                    cut_weights(k + 1, 1 - par, 2)
                return own.n

            def experts(k0, first_slot, base):
                i0 = k0 // 2
                own = Steps(dve, dve_step, base)
                select_tokens(own, 0, first_slot)
                slots(own, i0, 0)
                if k0:
                    for m in range(3):
                        cut_weights(k0, 0, m)
                base = base + own.n
                n = DK + 3
                with dve.Fori(0, E // 2 - 1) as i:
                    assert expert(i + i0, 0, base + 2 * n * i, 2 * i, first_slot, True) == n
                    assert expert(i + i0, 1, base + 2 * n * i + n, 2 * i + 1, first_slot, True) == n
                base += 2 * n * (E // 2 - 1)
                base += expert(E // 2 - 1 + i0, 0, base, E - 2, first_slot, True)
                base += expert(E // 2 - 1 + i0, 1, base, E - 1, first_slot, False)
                return base

            base = experts(0, 0, own.base + own.n)
            with dve.If(dve.value_load(n_max[0:1, 0:1], min_val=0, max_val=T) > HALF):
                experts(E, HALF, base)

        @block.tensor
        def _(pe):
            def product(out, lhs, rhs, pieces=range(DK), start=True, stop=True):
                terms = [(c, a, b) for c in pieces for a, b in PASSES]
                for n, (c, a, b) in enumerate(terms):
                    ins = nc.tensor.matmul(out, lhs(a, c), rhs(b, c), start=start and n == 0, stop=stop and n == len(terms) - 1)
                return ins

            def add_bias(out, n):
                return nc.tensor.matmul(out, bias_one[0:33, :], bias_hl[0:33, n, :], start=False, stop=True)

            def keys(g, t):
                b = t % 2
                pe.wait_ge(ctxT_in[t], 16 * g + 16)
                pe.wait_ge(wkv_ready, 2)
                pe.wait_ge(k_out[b], 2 * g + t // 2)
                product(bank(b), lambda a, c: ctx_T[:, bass.ds(g, 1), t, a * DK + c, :].rearrange("p a t -> p (a t)"),
                        lambda b, c: wkv_hl[:, b, c, 0:D], stop=False)
                pe.wait_ge(const_ready, 3)
                pe.wait_ge(bias_ready, 1)
                add_bias(bank(b), 0).then_inc(k_full, 1)

            def values_T(g, t):
                b = t % 2
                for n in range(2, DK):
                    pe.wait_ge(ctxT_in[n], 16 * g + 16)
                pe.wait_ge(wkv_ready, 4)
                pe.wait_ge(v_out[b], 2 * g + t // 2)
                product(bank(2 + b), lambda a, c: wkv_hl[:, a, c, D + t * P:D + t * P + P],
                        lambda b, c: ctx_T[:, bass.ds(g, 1), :, b * DK + c, :].rearrange("p a s t -> p (a s) t")).then_inc(v_full, 1)

            with pe.Fori(0, SG) as g:
                for t in (0, 1):
                    keys(g, t)
                for t in (0, 1):
                    values_T(g, t)
                for t in (2, 3):
                    keys(g, t)
                for t in (2, 3):
                    values_T(g, t)

            pe.wait_ge(wq_ready, 1)
            with pe.Fori(0, QT // 4) as i:
                for n in range(4):
                    t = 4 * i + n
                    if n >= 2:
                        pe.wait_ge(q_out[n % 2], 2 * i)
                    if n == 3:
                        pe.wait_ge(v_out[1], 2 * SG)
                    pe.wait_ge(xT_in, 16 * t + 16)
                    pe.sem_inc(pe_passed, 1)
                    product(bank(Q_BANKS[n]), lambda a, c: tok_T[:, a * DK + c, bass.ds(t * P, P)], lambda b, c: wq_hl[:, b, c, :], stop=False)
                    add_bias(bank(Q_BANKS[n]), 1).then_inc(q_full, 1)
                for b in range(2):
                    pe.wait_ge(q_out[b], 2 * i + 1)

            for b in range(2):
                pe.wait_ge(kT_in[b], 16 * KT // 2)

            def values(i, h, after=False):
                n = h // HQ
                if h % HQ == 0:
                    pe.wait_ge(att_ready, 2 * i + n)
                if h in (6, 10) and after:
                    pe.wait_ge(proj_out, 2 * (i - 1) + (1 if h == 6 else 2))
                if not after and h == 0:
                    pe.wait_ge(vT_in, 16 * DK)
                pe.wait_ge(probsT_in[h % 4], 64 * i + 16 * (h // 4 + 1))
                at = h % HQ * HD
                for t in range(KT):
                    ins = nc.tensor.matmul(bank(7)[:, at:at + HD], p_T[h % 4][:, t, :],
                                           v_int[:, t, h * HD:h * HD + HD], start=t == 0, stop=t == KT - 1)
                ins.then_inc(pv_done, 1)

            def project(out, j, first, columns):
                if first:
                    pe.wait_ge(wp_ready, DK)
                    pe.wait_ge(attT_in, 16 * j + 16)
                return product(out, lambda a, c: att_T[:, a * DK + c, :], lambda b, c: wp_hl[:, b, c, columns])

            def after_attention(j, h):
                if h in (8, 9, 12, 13):
                    half, piece = (h - 8) // 4, h % 4
                    if piece == 0:
                        pe.wait_ge(proj_out, 2 * j + half)
                    ins = project(bank(7)[:, 256 + piece * P:256 + piece * P + P], j, h == 8,
                                  slice(256 * half + piece * P, 256 * half + piece * P + P))
                    if piece:
                        ins.then_inc(proj_full, 1)

            def scores(i, h, first):
                u = H * i + h
                rows = slice(64 * (h % 2), 64 * (h % 2) + 64)
                if h % (H // 2) == 0:
                    pe.wait_ge(q_now_ready, 2 * i + h // (H // 2) + 1)
                if first and h == 1:
                    for b in range(2):
                        pe.wait_ge(q_out[b], QT // 2)
                if not first or h >= 2:
                    pe.wait_ge(exp_done, 2 * u - 2)
                for piece in range(4):
                    if piece == 3 and (not first or h >= 1):
                        pe.wait_ge(exp_done, 2 * u - 1)
                    ins = nc.tensor.matmul(bank(6 if piece == 3 else 3 * (h % 2) + piece), q_now[rows, h // 2, :],
                                           key_parts[rows, h // 2, piece * 512:piece * 512 + 512], start=True, stop=True)
                    if piece != 1:
                        ins.then_inc(scores_full, 1)

            def attention_tile(i, first):
                for h in range(H):
                    scores(i, h, first)
                    if h >= 4:
                        values(i, h - 4, not first)
                    elif not first:
                        values(i - 1, h - 4 + H, True)
                    if not first:
                        after_attention(i - 1, h)

            attention_tile(0, True)
            with pe.Fori(1, QT) as i:
                attention_tile(i, False)
            def logits(t):
                return product(bank(2)[:, t * E:t * E + E], lambda a, c: tok_T[:, a * DK + c, t * P:t * P + P],
                               lambda b, c: wr_hl[:, b, c, :])

            for h in range(H - 4, H):
                values(QT - 1, h, True)
            pe.wait_ge(exp_done, 2 * H * QT)
            pe.wait_ge(x1T_in, 16 * (QT - 1))
            for t in range(QT - 1):
                logits(t)
            for half in range(2):
                project(bank(half)[:, 0:256], QT - 1, half == 0, slice(256 * half, 256 * half + 256)).then_inc(proj_full, 1)

            pe.wait_ge(x1T_in, 16 * QT)
            logits(QT - 1).then_inc(logits_full, 1)

            pe.wait_ge(mask_ready, 1)
            nc.tensor.matmul(bank(1)[:, 0:QT * E + E], earlier[:, :], masks, start=True, stop=False)
            for d in range(1, QT + 1):
                ins = nc.tensor.matmul(bank(1)[:, d * E:QT * E + E], ones[:, :], masks[:, 0:(QT + 1 - d) * E],
                                       start=False, stop=d == QT)
            ins.then_inc(count_full, 1)

            def list_slots(i, par, e):
                k = 2 * i + par
                pe.wait_ge(select_ready, k + 1)
                pe.wait_ge(slots_ready, k)
                for s in range(DK):
                    for t in range(QT):
                        ins = nc.tensor.matmul(bank(7)[:, 5 * s:5 * s + 5], select[:, t, s * P:s * P + P],
                                               tok_w[:, t, bass.ds(e, 1), :].rearrange("p a c -> p (a c)"),
                                               start=t == 0, stop=t == QT - 1)
                ins.then_inc(list_full, 1)

            def expert(i, par, e, following):
                k = 2 * i + par
                gate, up, down = w_hl[par]
                pe.wait_ge(selT_in[par], 64 * i + 64)
                for f in range(DK):
                    cols = slice(f * P, f * P + P)
                    if following and f == DK - 1:
                        list_slots(*((i, 1) if par == 0 else (i + 1, 0)), e + 1)
                    pe.wait_ge(hidden_ready[f % 2], 2 * k + f // 2)
                    if f == 0:
                        pe.wait_ge(w_ready[0], k + 1)
                    product(bank(f % 2), lambda a, d: gate[:, a, d, cols], lambda b, d: x_sel_T[par][:, :, b * DK + d, :]
                            ).then_inc(gate_full, 1)
                    if f == 0:
                        pe.wait_ge(w_ready[1], k + 1)
                    product(bank(2 + f % 2), lambda a, d: up[:, a, d, cols], lambda b, d: x_sel_T[par][:, :, b * DK + d, :]
                            ).then_inc(up_full, 1)
                pe.wait_ge(w_ready[2], k + 1)

                def down_product(t, pieces):
                    return product(bank(4 + t % 3), lambda a, d: hid_T[par][:, a, d, t * P:t * P + P],
                                   lambda b, d: down[:, b, d, :], pieces=pieces, start=0 in pieces, stop=DK - 1 in pieces)

                pe.wait_ge(hid_cut, DK * k + DK - 1)
                pe.wait_ge(y_ready[1], 2 * k)
                for t in range(2):
                    down_product(t, range(DK - 1))
                pe.wait_ge(hid_cut, DK * k + DK)
                for t in range(2):
                    down_product(t, [DK - 1]).then_inc(down_full, 1)
                for t in range(2, DK):
                    if t == 3:
                        pe.wait_ge(y_ready[0], 2 * k + 1)
                    down_product(t, range(DK)).then_inc(down_full, 1)

            def experts(k0):
                i0 = k0 // 2
                list_slots(i0, 0, 0)
                with pe.Fori(0, E // 2 - 1) as i:
                    expert(i + i0, 0, 2 * i, True)
                    expert(i + i0, 1, 2 * i + 1, True)
                expert(E // 2 - 1 + i0, 0, E - 2, True)
                expert(E // 2 - 1 + i0, 1, E - 1, False)

            experts(0)
            pe.wait_ge(n_ready, 1)
            with pe.If(pe.value_load(n_max[0:1, 0:1], min_val=0, max_val=T) > HALF):
                experts(E)


_INS = ['x', 'ctx_2048', 'L0_xattn_Wq', 'L0_xattn_bq', 'L0_xattn_Wkv', 'L0_xattn_bkv', 'L0_xattn_Wp', 'L0_xattn_bp',
        'L0_ffn_Wg', 'L0_ffn_Wu', 'L0_ffn_Wd', 'L0_ffn_Wr', 'L0_ffn_temperature']


def kernel(**inputs):
    import numpy as _np
    import concourse.bacc as _bacc
    from concourse import mybir as _mybir
    from concourse.bass_utils import run_bass_kernel_spmd as _run

    nc = _bacc.Bacc("TRN2", target_bir_lowering=False, num_devices=1)
    arrays, args = {}, []
    for name in _INS:
        a = _np.ascontiguousarray(inputs[name])
        arrays[f"in_{name}_dram"] = a
        args.append(nc.dram_tensor(f"in_{name}_dram", a.shape, _mybir.dt.from_np(a.dtype), kind="ExternalInput").ap())
    out = nc.dram_tensor("out_0_dram", (2, 512, 512), _mybir.dt.float32, kind="ExternalOutput").ap()
    xattn_moe(nc, *args, out)
    r = _run(nc, [arrays], core_ids=[0])
    return r.results[0]["out_0_dram"]
```
